# Optimizing a Trainium2 kernel written in Bass

```python
import numpy as np
import jax
import jax.numpy as jnp

def _softmax(x, axis=-1):
    return jax.nn.softmax(x, axis=axis)

def _gelu(x):
    return jax.nn.gelu(x, approximate=True)

def _silu(x):
    return jax.nn.silu(x)

def _sigmoid(x):
    return jax.nn.sigmoid(x)

def _layernorm(x, axis=-1, eps=1e-05):
    m = jnp.mean(x, axis=axis, keepdims=True)
    v = jnp.var(x, axis=axis, keepdims=True)
    return (x - m) / jnp.sqrt(v + eps)

def _scatter_add(tgt, idx, src, axis=0):
    return tgt.at[idx].add(src)

def _segment_sum(src, seg, n):
    return jax.ops.segment_sum(src, seg, n)
kernel_name = 'mk_gnn_resnorm_d4_gnn_r8_cafccf'

def setup_inputs(seed: int=0):
    np.random.seed(seed)
    _w = jnp.asarray

    def _rec_inputs():
        import jax
        import jax.numpy as jnp
        _gk = jax.random.key(seed)
        x = -0.0005121 + 1.001 * jax.random.normal(jax.random.fold_in(_gk, 1), (6250, 64), jnp.float32)
        src = jax.random.randint(jax.random.fold_in(_gk, 2), (200000,), 0, 6250, jnp.int32)
        dst = jnp.minimum((6250 * jax.random.uniform(jax.random.fold_in(_gk, 3), (200000,)) ** 2.0).astype(jnp.int32), 49999)
        _o = jnp.argsort(dst, stable=True)
        src = src[_o]
        dst = dst[_o]
        edge_attr_64 = 0.000135552 + 1.00015 * jax.random.normal(jax.random.fold_in(_gk, 12), (200000, 64), jnp.float32)
        edge_attr_64_n2 = 0.000135552 + 1.00015 * jax.random.normal(jax.random.fold_in(_gk, 13), (200000, 64), jnp.float32)
        edge_attr_64_n3 = 0.000135552 + 1.00015 * jax.random.normal(jax.random.fold_in(_gk, 14), (200000, 64), jnp.float32)
        return (x, src, dst, edge_attr_64, edge_attr_64_n2, edge_attr_64_n3)
    x, src, dst, edge_attr_64, edge_attr_64_n2, edge_attr_64_n3 = _rec_inputs()

    def _L0_gnn_setup():
        import jax, jax.numpy as jnp
        import numpy as np
        D_MODEL = 64
        N_HEAD = 1
        N_NODES = 6250
        N_EDGES = 100000
        EPS = 1e-06
        NEG_SLOPE = 0.01
        key = jax.random.key(seed)
        ks = jax.random.split(key, 12)
        d, H = (D_MODEL, N_HEAD)
        xav = lambda k, shp: jax.random.normal(k, shp, jnp.float32) * np.sqrt(2.0 / (shp[0] + shp[1]))
        return {'h': jax.random.normal(ks[0], (N_NODES, d), jnp.float32), 'eh': jax.random.normal(ks[1], (N_EDGES, d), jnp.float32), 'qrh': jax.random.normal(ks[2], (N_EDGES, d), jnp.float32), 'qeh': jax.random.normal(ks[3], (N_EDGES, d), jnp.float32), 'src': jax.random.randint(ks[4], (N_EDGES,), 0, N_NODES, jnp.int32), 'dst': jax.random.randint(ks[5], (N_EDGES,), 0, N_NODES, jnp.int32), 'W_msg': xav(ks[6], (2 * d, H * d)), 'W_q': xav(ks[7], (2 * d, H * d)), 'W_k': xav(ks[8], (2 * d, H * d)), 'W_out': xav(ks[9], (H * d, d)), 'gamma': jnp.ones((d,), jnp.float32), 'beta': jnp.zeros((d,), jnp.float32)}
    _L0_gnn_all = _L0_gnn_setup()
    _L0_gnn_in = {k: v for k, v in _L0_gnn_all.items() if k in ('W_msg', 'W_q', 'W_k', 'W_out', 'gamma', 'beta')}
    del _L0_gnn_all

    def _L1_gnn_setup():
        import jax, jax.numpy as jnp
        import numpy as np
        NUM_NODES = 6250
        EMBED_DIM = 64
        NUM_EDGES = 156250
        NUM_LAYERS = 3
        key = jax.random.key(seed)
        k1, k2 = jax.random.split(key)
        edge_index = jax.random.randint(k1, (2, NUM_EDGES), 0, NUM_NODES, dtype=jnp.int64) if jax.config.read('jax_enable_x64') else jax.random.randint(k1, (2, NUM_EDGES), 0, NUM_NODES, dtype=jnp.int32)
        embedding_weight = jax.random.normal(k2, (NUM_NODES, EMBED_DIM), dtype=jnp.float32)
        return {'edge_index': edge_index, 'embedding_weight': embedding_weight}
    _L1_gnn_all = _L1_gnn_setup()
    _L1_gnn_in = {k: v for k, v in _L1_gnn_all.items() if k in ()}
    del _L1_gnn_all

    def _L2_gnn_setup():
        import jax, jax.numpy as jnp
        import numpy as np
        N_NODES = 12500
        N_EDGES = 200000
        D_FEAT = 64
        key = jax.random.key(seed)
        k1, k2 = jax.random.split(key)
        x = jax.random.normal(k1, (N_NODES, D_FEAT), dtype=jnp.float32)
        edge_index = jax.random.randint(k2, (2, N_EDGES), 0, N_NODES, dtype=jnp.int64)
        return {'x': x, 'edge_index': edge_index}
    _L2_gnn_all = _L2_gnn_setup()
    _L2_gnn_in = {k: v for k, v in _L2_gnn_all.items() if k in ()}
    del _L2_gnn_all

    def _L3_gnn_setup():
        import jax, jax.numpy as jnp
        import numpy as np
        N_NODES = 12500
        N_EDGES = 200000
        D_IN = 64
        D_OUT = 64

        def _scatter_mean(msgs, index, num_segments):
            s = jax.ops.segment_sum(msgs, index, num_segments=num_segments)
            cnt = jax.ops.segment_sum(jnp.ones((index.shape[0],), msgs.dtype), index, num_segments=num_segments)
            return s / jnp.clip(cnt, 1.0)[:, None]
        key = jax.random.key(seed)
        k1, k2, k3, k4 = jax.random.split(key, 4)
        x = jax.random.normal(k1, (N_NODES, D_IN), dtype=jnp.float32)
        edge_index = jax.random.randint(k2, (2, N_EDGES), 0, N_NODES, dtype=jnp.int32)
        limit = float(np.sqrt(6.0 / (D_IN + D_OUT)))
        W1 = jax.random.uniform(k3, (D_OUT, D_IN), jnp.float32, -limit, limit)
        Wr = jax.random.uniform(k4, (D_OUT, D_IN), jnp.float32, -limit, limit)
        br = jnp.zeros((D_OUT,), jnp.float32)
        return {'x': x, 'edge_index': edge_index, 'W1': W1, 'Wr': Wr, 'br': br}
    _L3_gnn_all = _L3_gnn_setup()
    _L3_gnn_in = {k: v for k, v in _L3_gnn_all.items() if k in ('W1', 'Wr', 'br')}
    del _L3_gnn_all
    return {'x': x, 'src': src, 'dst': dst, 'edge_attr_64': edge_attr_64, 'edge_attr_64_n2': edge_attr_64_n2, 'edge_attr_64_n3': edge_attr_64_n3, 'L0_gnn_W_msg': _L0_gnn_in['W_msg'], 'L0_gnn_W_q': _L0_gnn_in['W_q'], 'L0_gnn_W_k': _L0_gnn_in['W_k'], 'L0_gnn_W_out': _L0_gnn_in['W_out'], 'L0_gnn_gamma': _L0_gnn_in['gamma'], 'L0_gnn_beta': _L0_gnn_in['beta'], 'L3_gnn_W1': _L3_gnn_in['W1'], 'L3_gnn_Wr': _L3_gnn_in['Wr'], 'L3_gnn_br': _L3_gnn_in['br']}

def reference(x, src, dst, edge_attr_64, edge_attr_64_n2, edge_attr_64_n3, L0_gnn_W_msg, L0_gnn_W_q, L0_gnn_W_k, L0_gnn_W_out, L0_gnn_gamma, L0_gnn_beta, L3_gnn_W1, L3_gnn_Wr, L3_gnn_br):
    import jax
    import jax.numpy as jnp

    def _L0_gnn_ref(h, eh, qrh, qeh, src, dst, W_msg, W_q, W_k, W_out, gamma, beta):
        import jax, jax.numpy as jnp
        import numpy as np
        D_MODEL = 64
        N_HEAD = 1
        N_NODES = 6250
        N_EDGES = 100000
        EPS = 1e-06
        NEG_SLOPE = 0.01
        N, d = h.shape
        E = eh.shape[0]
        H = W_msg.shape[1] // d
        temp = jnp.asarray(d, h.dtype) ** 0.5
        src_h = h[src]
        se = jnp.concatenate([src_h, eh], axis=-1)
        msg = jax.nn.leaky_relu(se @ W_msg, NEG_SLOPE).reshape(E, H, d)
        q = (jnp.concatenate([qrh, qeh], axis=-1) @ W_q / temp).reshape(E, H, d)
        k = (se @ W_k).reshape(E, H, d)
        att = jnp.sum(q * k, axis=-1)
        m = jax.ops.segment_max(att, dst, num_segments=N)
        e = jnp.exp(att - jax.lax.stop_gradient(m)[dst])
        denom = jax.ops.segment_sum(e, dst, num_segments=N)
        alpha = e / denom[dst]
        agg = jax.ops.segment_sum(alpha[..., None] * msg, dst, num_segments=N)
        hn = jax.nn.leaky_relu(agg.reshape(N, H * d) @ W_out, NEG_SLOPE) + h
        mu = jnp.mean(hn, axis=-1, keepdims=True)
        var = jnp.mean((hn - mu) ** 2, axis=-1, keepdims=True)
        ln = (hn - mu) / jnp.sqrt(var + EPS) * gamma + beta
        deg = jax.ops.segment_sum(jnp.ones((E,), h.dtype), dst, num_segments=N)
        return jnp.where(deg[:, None] > 0, ln, h)

    def _L1_gnn_ref(edge_index, embedding_weight):
        import jax, jax.numpy as jnp
        import numpy as np
        NUM_NODES = 6250
        EMBED_DIM = 64
        NUM_EDGES = 156250
        NUM_LAYERS = 3
        row, col = (edge_index[0], edge_index[1])
        n = embedding_weight.shape[0]
        deg = jax.ops.segment_sum(jnp.ones_like(row, dtype=embedding_weight.dtype), row, num_segments=n)
        deg_inv_sqrt = jnp.where(deg > 0, jax.lax.rsqrt(jnp.maximum(deg, 1.0)) * jnp.where(deg > 0, 1.0, 0.0) + jax.lax.rsqrt(jnp.maximum(deg, 1.0)) * 0.0, 0.0)
        deg_inv_sqrt = jnp.where(deg > 0, jax.lax.rsqrt(jnp.maximum(deg, 1.0)), 0.0)
        x = embedding_weight
        acc = x
        for _ in range(NUM_LAYERS):
            m = deg_inv_sqrt[row][:, None] * x[col]
            x = jax.ops.segment_sum(m, row, num_segments=n) * deg_inv_sqrt[:, None]
            acc = acc + x
        return acc / (NUM_LAYERS + 1)

    def _L2_gnn_ref(x, edge_index):
        import jax, jax.numpy as jnp
        import numpy as np
        N_NODES = 12500
        N_EDGES = 200000
        D_FEAT = 64
        row, col = (edge_index[0], edge_index[1])
        n = x.shape[0]
        deg = jax.ops.segment_sum(jnp.ones(row.shape[0], dtype=x.dtype), row, num_segments=n)
        deg_inv_sqrt = jnp.where(deg > 0, jax.lax.rsqrt(jnp.maximum(deg, 1.0)) * jnp.where(deg > 0, 1.0, 0.0), 0.0)
        deg_inv_sqrt = jnp.where(deg > 0, jax.lax.rsqrt(jnp.maximum(deg, 1.0)), 0.0)
        norm = deg_inv_sqrt[row] * deg_inv_sqrt[col]
        msgs = x[col] * norm[:, None]
        out = jax.ops.segment_sum(msgs, row, num_segments=n)
        return out

    def _L3_gnn_ref(x, edge_index, W1, Wr, br):
        import jax, jax.numpy as jnp
        import numpy as np
        N_NODES = 12500
        N_EDGES = 200000
        D_IN = 64
        D_OUT = 64

        def _scatter_mean(msgs, index, num_segments):
            s = jax.ops.segment_sum(msgs, index, num_segments=num_segments)
            cnt = jax.ops.segment_sum(jnp.ones((index.shape[0],), msgs.dtype), index, num_segments=num_segments)
            return s / jnp.clip(cnt, 1.0)[:, None]
        n = x.shape[0]
        source, target = (edge_index[0], edge_index[1])
        h = x @ W1.T
        s2t = _scatter_mean(h[source], target, n)
        t2s = _scatter_mean(h[target], source, n)
        return x @ Wr.T + br + s2t + t2s
    edge_index = jnp.stack([src, dst])
    x = _layernorm(x + _L0_gnn_ref(x, edge_attr_64, edge_attr_64_n2, edge_attr_64_n3, src, dst, L0_gnn_W_msg, L0_gnn_W_q, L0_gnn_W_k, L0_gnn_W_out, L0_gnn_gamma, L0_gnn_beta), axis=-1)
    x = _layernorm(x + _L1_gnn_ref(edge_index, x), axis=-1)
    x = _layernorm(x + _L2_gnn_ref(x, edge_index), axis=-1)
    x = _layernorm(x + _L3_gnn_ref(x, edge_index, L3_gnn_W1, L3_gnn_Wr, L3_gnn_br), axis=-1)
    return x

_drawn_inputs = setup_inputs


def setup_inputs(seed=0):
    import zlib

    import numpy as np

    out = dict(_drawn_inputs(seed))
    spreads = {'L0_gnn_gamma': (1.0, 0.2), 'L0_gnn_beta': (0.0, 0.1), 'L3_gnn_br': (0.0, 0.1)}
    factors = {}
    for name, (base, spread) in spreads.items():
        noise = np.random.default_rng([zlib.crc32(name.encode()), seed]).standard_normal(out[name].shape)
        drawn = base * np.exp(spread * noise) if base else spread * noise
        out[name] = jnp.asarray(drawn.astype(out[name].dtype))
    for name, factor in factors.items():
        out[name] = (out[name] * factor).astype(out[name].dtype)
    return out
```

```python
import concourse.bass as bass
from concourse import mybir
from contextlib import ExitStack

F32, F16, I32 = mybir.dt.float32, mybir.dt.float16, mybir.dt.int32
ALU, ACT, AX = mybir.AluOpType, mybir.ActivationFunctionType, mybir.AxisListType

LANES = 128
NODES, EDGES, DIM = 6250, 200000, 64
BLOCKS = -(-NODES // LANES)
PADDED = BLOCKS * LANES
LAST = NODES - (BLOCKS - 1) * LANES
ROWS, COLS = 125, EDGES // 125
TILES = 8
GROUPS = COLS // TILES
RING = 4
CHUNK = 1024
PER_LANE = CHUNK // LANES
CHUNKS = EDGES // CHUNK + BLOCKS
SLOT_ROWS = EDGES // LANES + BLOCKS
ROW_LOOP = 32
ROW_LOOPS = -(-SLOT_ROWS // ROW_LOOP)
SLOT_ROWS_UP = ROW_LOOPS * ROW_LOOP
FILLS = 16
FILL_COLS = SLOT_ROWS_UP * PADDED * 2 // LANES // FILLS
HIST = 32
BG = 7
BGW = BG * LANES
HALF = (BLOCKS + 1) // 2
NEG = -1.0e30
SCALE = 4096.0
HOPS = 5
MSGW = DIM + 1


def gnn_kernel(nc, x, x_t, src, dst, edge_k, edge_q, w_in, w_q, w_out, gamma, beta, w_last, b_last, out):
    table = nc.dram_tensor("node_projections", [PADDED, 2 * DIM], F32, kind="Internal").ap()
    msgs = nc.dram_tensor("messages", [EDGES + CHUNK, MSGW], F32, kind="Internal").ap()
    edge_ed = nc.dram_tensor("edge_exp_dst", [EDGES + CHUNK, 2], F32, kind="Internal").ap()
    slots = nc.dram_tensor("edge_slots", [SLOT_ROWS_UP * PADDED, 2], F16, kind="Internal").ap()
    dst_major = nc.dram_tensor("counts_dst_major", [BLOCKS, LANES, PADDED], F16, kind="Internal").ap()
    src_major = nc.dram_tensor("counts_src_major", [BLOCKS, LANES, PADDED], F16, kind="Internal").ap()

    ctx = ExitStack()
    with ctx:
        def sem(name):
            return ctx.enter_context(nc.semaphore(name))

        def allocator(stack):
            return lambda name, shape, dt: stack.enter_context(nc.sbuf_tensor(name, shape, dt))

        sb = allocator(ctx)
        X = sb("X", [LANES, BLOCKS, DIM], F32)
        mem_a = sb("mem_a", [LANES, 2 * COLS], F32)
        mem_b = sb("mem_b", [LANES, 2 * COLS], F32)
        exp_dst = mem_a[0:ROWS, :].rearrange("p (t k) -> p t k", k=2)
        src_i = mem_b[0:ROWS, 0:COLS].bitcast(I32)
        slot_idx = mem_b[0:ROWS, COLS:2 * COLS].bitcast(I32)
        xs = mem_a[:, :].bitcast(F16)[:, 0:BLOCKS * (2 * DIM + 1)].rearrange("p (b c) -> p b c", b=BLOCKS)
        total = mem_b[:, 0:BLOCKS * DIM].rearrange("p (b c) -> p b c", b=BLOCKS)
        mem_c = sb("mem_c", [LANES, 2 * COLS + 2], F32)
        pen = mem_c[0:ROWS, 0:COLS + 1]
        att = mem_c[0:ROWS, COLS + 1:2 * COLS + 1]
        payload = sb("payload", [ROWS, COLS, 2], F16)
        iota = sb("iota", [LANES, LANES], F32)
        iota16 = sb("iota16", [LANES, LANES], F16)
        lane_no = sb("lane_no", [LANES, 1], F32)
        ident = sb("ident", [LANES, LANES], F32)
        ident16 = sb("ident16", [LANES, LANES], F16)
        ones = sb("ones", [LANES, LANES], F32)
        w_node = sb("w_node", [DIM, 2 * DIM], F32)
        w_edge = sb("w_edge", [LANES, 2 * DIM], F32)
        wq = sb("wq", [2 * DIM, DIM], F32)
        wo = sb("wo", [DIM, DIM], F32)
        wl = sb("wl", [2 * DIM, DIM], F32)
        gam = sb("gam", [LANES, DIM], F32)
        bet = sb("bet", [LANES, DIM], F32)
        bl = sb("bl", [LANES, DIM], F32)
        keep_row = sb("keep_row", [LANES, SLOT_ROWS_UP], F32)
        block_of_row = sb("block_of_row", [1, SLOT_ROWS_UP], I32)
        n_rows = sb("n_rows", [1, 1], I32)
        chunk_first = sb("chunk_first", [LANES, CHUNKS], F32)
        chunk_block = sb("chunk_block", [1, CHUNKS], I32)
        chunk_base = sb("chunk_base", [1, CHUNKS], I32)
        gidx = sb("gidx", [ROWS, RING, TILES], I32)
        sidx = sb("sidx", [ROWS, RING, TILES], I32)
        spay = sb("spay", [ROWS, RING, TILES, 2], F16)
        mean = sb("mean", [LANES, BLOCKS], F32)
        var = sb("var", [LANES, BLOCKS], F32)
        deg_inv = sb("deg_inv", [LANES, BLOCKS], F32)
        deg_rsq = sb("deg_rsq", [LANES, BLOCKS], F32)
        has = sb("has", [LANES, BLOCKS], F32)

        ph = ExitStack()
        sb = allocator(ph)
        dst_i = sb("dst_i", [ROWS, COLS], I32)
        prev_i = sb("prev_i", [ROWS, COLS], I32)
        next_i = sb("next_i", [ROWS, 1], I32)
        next_f = sb("next_f", [ROWS, 1], F32)
        dblk = sb("dblk", [ROWS, COLS], F32)
        sblk = sb("sblk", [ROWS, COLS], F32)
        keep_b = sb("keep_b", [ROWS, COLS], F32)
        before = sb("before", [ROWS, COLS], F32)
        ra = sb("ra", [ROWS, COLS], F32)
        rb = sb("rb", [ROWS, COLS], F32)
        ind = sb("ind", [ROWS, COLS], F32)
        cnt = sb("cnt", [ROWS, COLS], F32)
        picked = sb("picked", [ROWS, 2, COLS], F32)
        oh_d = sb("oh_d", [ROWS, 2, HIST, BLOCKS], F16)
        oh_s = sb("oh_s", [ROWS, 2, HIST, BLOCKS], F16)
        minus1 = sb("minus1", [LANES, FILL_COLS], F16)
        row_last = sb("row_last", [ROWS, BLOCKS], F32)
        row_last_t = sb("row_last_t", [BLOCKS, ROWS], F32)
        no_break = sb("no_break", [ROWS, 1], F32)
        nb_diag = sb("nb_diag", [ROWS, ROWS], F32)
        nb_t = sb("nb_t", [BLOCKS, ROWS], F32)
        carry_t = sb("carry_t", [BLOCKS, ROWS + 1], F32)
        carry = sb("carry", [ROWS, BLOCKS], F32)
        upper = sb("upper", [LANES, LANES], F32)
        bt = sb("bt", [BLOCKS, 3], F32)
        bti = sb("bti", [BLOCKS, 3], I32)
        bend = sb("bend", [BLOCKS, 3], F32)
        bstart = sb("bstart", [BLOCKS, 3], F32)
        base_v = sb("base_v", [BLOCKS, 1], F32)
        base_m = sb("base_m", [BLOCKS, LANES], F32)
        rs_diag = sb("rs_diag", [BLOCKS, BLOCKS], F32)
        row_start = sb("row_start", [ROWS, BLOCKS], F32)
        row_no = sb("row_no", [LANES, SLOT_ROWS_UP], F32)
        row_cmp = sb("row_cmp", [BLOCKS, SLOT_ROWS_UP], F32)
        chunk_tmp = sb("chunk_tmp", [LANES, CHUNKS], F32)
        chunk_oh = sb("chunk_oh", [BLOCKS, CHUNKS], F32)
        zpad = sb("zpad", [LANES, PER_LANE * MSGW], F32)
        edpad = sb("edpad", [LANES, PER_LANE, 2], F32)
        ph.close()

        ph = ExitStack()
        sb = allocator(ph)
        xt = sb("xt", [DIM, PADDED], F32)
        proj = sb("proj", [LANES, BLOCKS, 2 * DIM], F32)
        kf = sb("kf", [LANES, RING, TILES // 2 * ROWS], F32)
        qf = sb("qf", [LANES, RING, TILES * ROWS], F32)
        gat = sb("gat", [ROWS, RING, TILES, 2 * DIM], F32)
        kk = sb("kk", [ROWS, 2, TILES, DIM], F32)
        mm = sb("mm", [ROWS, 2, TILES, DIM], F32)
        msgb = sb("msgb", [ROWS, RING, TILES, MSGW], F32)
        seg_f = sb("seg_f", [ROWS, COLS], F32)
        seg_m = sb("seg_m", [ROWS, COLS], F32)
        line = sb("line", [1, 2, ROWS], F32)
        line_c = sb("line_c", [1, ROWS + 1], F32)
        edge_v = sb("edge_v", [ROWS, 2], F32)
        edge_in = sb("edge_in", [ROWS, 1], F32)
        ph.close()

        sb = allocator(ctx)
        Y = sb("Y", [LANES, BLOCKS, DIM], F32)
        W = sb("W", [LANES, BLOCKS, DIM], F32)
        ylo = sb("ylo", [LANES, BLOCKS, DIM], F32)
        Z = sb("Z", [LANES, BLOCKS, 2 * DIM], F32)
        zt = sb("zt", [LANES, 2, 4 * LANES], F32)

        ph = ExitStack()
        sb = allocator(ph)
        mch = sb("mch", [LANES, RING, PER_LANE * MSGW], F32)
        ech = sb("ech", [LANES, RING, PER_LANE, 2], F32)
        rel = sb("rel", [LANES, RING, PER_LANE], F32)
        woh = sb("woh", [LANES, 2, PER_LANE, LANES], F32)
        agg = sb("agg", [LANES, BLOCKS + 1, MSGW], F32)
        pay = sb("pay", [LANES, 2, BLOCKS, 2], F16)
        payf = sb("payf", [LANES, 2, BLOCKS, 2], F32)
        keep_diag = sb("keep_diag", [LANES, 2, LANES], F16)
        oh = sb("oh", [LANES, 2, BG, 2, LANES], F16)
        cacc = sb("cacc", [LANES, 2, PADDED], F16)
        den = sb("den", [LANES, BLOCKS], F32)
        ph.close()

        ph = ExitStack()
        sb = allocator(ph)
        big = sb("big", [LANES, 5, HALF * LANES], F16)
        bigs = [sb(f"bigs{i}", [LANES, PADDED], F16) for i in range(2)] + [mem_c[:, :].bitcast(F16)[:, 0:PADDED]]
        one16 = sb("one16", [LANES, 1], F16)
        cnt_d = sb("cnt_d", [LANES, BLOCKS], F32)
        ph.close()

        ps = ctx.enter_context(nc.psum_tensor("ps", [LANES, 8, 512], F32))

        edges_in, consts_in, x_in, filled = sem("edges_in"), sem("consts_in"), sem("x_in"), sem("filled")
        pool_consts, vec_consts, vec = sem("pool_consts"), sem("vec_consts"), sem("vec")
        hist_ready, hist_used = sem("hist_ready"), sem("hist_used")
        tab_v, tab_pe = sem("tab_v"), sem("tab_pe")
        pick_ready, pick_used = sem("pick_ready"), sem("pick_used")
        rank_step = sem("rank_step")
        ranked = sem("ranked")
        proj_pe, proj_act, table_out = sem("proj_pe"), sem("proj_act"), sem("table_out")
        kf_in = [sem(f"kf_in{u}") for u in range(RING)]
        qf_in = [sem(f"qf_in{u}") for u in range(RING)]
        gat_in = [sem(f"gat_in{u}") for u in range(RING)]
        msg_out = [sem(f"msg_out{u}") for u in range(RING)]
        gidx_ready, edge_mm, edge_v_done, msg_ready, edge_step = (
            sem("gidx_ready"), sem("edge_mm"), sem("edge_v_done"), sem("msg_ready"), sem("edge_step"))
        line_v, line_pe = sem("line_v"), sem("line_pe")
        exp_in, exp_done, ed_out = sem("exp_in"), sem("exp_done"), sem("ed_out")
        sidx_ready = sem("sidx_ready")
        dealt = [sem(f"dealt{u}") for u in range(RING)]
        chunk_in = [sem(f"chunk_in{u}") for u in range(RING)]
        agg_rel, woh_ready, agg_mm, agg_added = sem("agg_rel"), sem("woh_ready"), sem("agg_mm"), sem("agg_added")
        nt_ready, nt_t, nt_copied, nt_mm, nt_out = (
            sem("nt_ready"), sem("nt_t"), sem("nt_copied"), sem("nt_mm"), sem("nt_out"))
        pay_in = [sem(f"pay_in{u}") for u in range(2)]
        pay_read, pay_conv, oh_ready, tile_mm, tile_copied = (
            sem("pay_read"), sem("pay_conv"), sem("oh_ready"), sem("tile_mm"), sem("tile_copied"))
        counts_out = [sem(f"counts_out{g}") for g in range(BG)]
        build_start, built = sem("build_start"), sem("built")
        big_in = [sem(f"big_in{u}") for u in range(5)]
        big_used, xs_ready, sweep_mm, lo_copied, sweep_read = (
            sem("big_used"), sem("xs_ready"), sem("sweep_mm"), sem("lo_copied"), sem("sweep_read"))
        bigs_in = [sem(f"bigs_in{u}") for u in range(3)]
        s2t_mm, s2t_lo, s2t_read = sem("s2t_mm"), sem("s2t_lo"), sem("s2t_read")
        act_v, act_done = sem("act_v"), sem("act_done")
        stored = sem("stored")

        TAB_V = 5
        JOB_CREDIT = 4
        block = ctx.enter_context(nc.Block())

        dst_rows = dst.rearrange("(p t) -> p t", t=COLS)
        src_rows = src.rearrange("(p t) -> p t", t=COLS)
        msg_rows = msgs[0:EDGES, :].rearrange("(p t) c -> p t c", t=COLS)
        fill_view = slots.rearrange("(f p c) k -> f p (c k)", f=FILLS, p=LANES)

        @block.sync
        def _(sp):
            sp.dma_start(src_i[:, :], src_rows).then_inc(edges_in, 16)
            sp.dma_start(dst_i[:, :], dst_rows).then_inc(edges_in, 16)
            sp.wait_ge(vec_consts, 3)
            sp.dma_start(prev_i[1:ROWS, :], dst[COLS - 1:EDGES - 1].rearrange("(p t) -> p t", t=COLS)).then_inc(edges_in, 16)
            sp.dma_start(prev_i[0:1, 1:COLS], dst_rows[0:1, 0:COLS - 1]).then_inc(edges_in, 16)
            sp.dma_start(next_i[0:ROWS - 1, :], dst_rows[1:ROWS, 0:1], allow_slow_non_contiguous=True).then_inc(edges_in, 16)
            for t, a in ((w_node[:, :], w_in[0:DIM, :]), (w_edge[0:DIM, :], w_in[DIM:2 * DIM, :]),
                         (w_edge[DIM:2 * DIM, :], w_in[DIM:2 * DIM, :]), (wq[:, :], w_q), (wo[:, :], w_out),
                         (wl[:, :], w_last), (gam[:, :], gamma.to_broadcast([LANES, DIM])),
                         (bet[:, :], beta.to_broadcast([LANES, DIM])), (bl[:, :], b_last.to_broadcast([LANES, DIM]))):
                sp.dma_start(t, a).then_inc(consts_in, 16)
            sp.wait_ge(vec_consts, 6)
            sp.dma_start(X[:, 0:BLOCKS - 1, :], x[0:(BLOCKS - 1) * LANES, :].rearrange("(b p) f -> p b f", p=LANES)).then_inc(x_in, 16)
            sp.dma_start(X[0:LAST, BLOCKS - 1, :], x[(BLOCKS - 1) * LANES:NODES, :]).then_inc(x_in, 16)
            for f in range(FILLS):
                sp.dma_start(fill_view[f], minus1[:, :]).then_inc(filled, 16)
            sp.dma_start(msgs[EDGES:EDGES + CHUNK, :].rearrange("(p j) c -> p (j c)", j=PER_LANE), zpad[:, :]).then_inc(filled, 16)
            sp.dma_start(edge_ed[EDGES:EDGES + CHUNK, :].rearrange("(p j) c -> p j c", j=PER_LANE), edpad[:, :, :]).then_inc(filled, 16)
            sp.wait_ge(filled, 16 * (FILLS + 2))
            sp.wait_ge(ranked, 1)
            sp.dma_start(xt[:, 0:NODES], x_t).then_inc(x_in, 16)

            def load_features(i, first):
                for u in range(RING):
                    g = RING * i + u
                    if not first:
                        sp.wait_ge(edge_mm, g - RING + 1)
                    sp.dma_start(kf[:, u, :], edge_k[bass.ds(g, 1), :, :].rearrange("a p c -> (a p) c")).then_inc(kf_in[u], 16)
                    sp.dma_start(qf[:, u, :], edge_q[bass.ds(g, 1), :, :].rearrange("a p c -> (a p) c")).then_inc(qf_in[u], 16)

            load_features(0, True)
            sp.wait_ge(proj_act, BLOCKS // 4 + 1)
            sp.dma_start(table.rearrange("(b p) f -> p b f", p=LANES), proj[:, :, :]).then_inc(table_out, 16)
            with sp.Fori(1, GROUPS // RING) as i:
                load_features(i, False)

            sp.wait_ge(exp_done, 2)
            sp.dma_start(edge_ed[0:EDGES, :].rearrange("(p t) c -> p t c", t=COLS), exp_dst[:, :, :]).then_inc(ed_out, 16)
            sp.wait_ge(ed_out, 16)
            for u in range(RING):
                sp.wait_ge(msg_out[u], 16 * (GROUPS // RING))

            def load_chunks(i, first):
                for u in range(RING):
                    r = RING * i + u
                    base = sp.value_load(chunk_base[0:1, bass.ds(r, 1)], min_val=0, max_val=EDGES)
                    if not first:
                        sp.wait_ge(agg_mm, r - RING + 1)
                    sp.dma_start(mch[:, u, :], msgs[bass.ds(base, CHUNK), :].rearrange("(p j) c -> p (j c)", j=PER_LANE)).then_inc(chunk_in[u], 16)
                    sp.dma_start(ech[:, u, :, :].rearrange("p j c -> p (j c)"),
                                 edge_ed[bass.ds(base, CHUNK), :].rearrange("(p j) c -> p (j c)", j=PER_LANE)).then_inc(chunk_in[u], 16)

            load_chunks(0, True)
            with sp.Fori(1, CHUNKS // RING) as i:
                load_chunks(i, False)

            sp.wait_ge(build_start, 1)
            rows = sp.value_load(n_rows[0:1, 0:1], min_val=1, max_val=SLOT_ROWS)
            with sp.Fori(0, ROW_LOOPS) as o:
                with sp.If(o * ROW_LOOP < rows):
                    with sp.Fori(0, ROW_LOOP // 2) as j:
                        for u in range(2):
                            r = o * ROW_LOOP + j * 2 + u
                            with sp.If(r < rows):
                                sp.wait_ge(pay_read, r + 1)
                                sp.dma_start(pay[:, u, :, :].rearrange("p s k -> p (s k)"),
                                             slots[bass.ds(r * PADDED, PADDED), :].rearrange("(p s) k -> p (s k)", s=BLOCKS)).then_inc(pay_in[u], 16)
            sp.wait_ge(built, 1)

            with sp.Fori(0, HOPS) as hop:
                for h in range(2):
                    wide = (HALF, BLOCKS - HALF)[h] * LANES
                    w = hop * 2 + h

                    def lot(b, u):
                        sp.wait_ge(big_used, w * BLOCKS + b + 1)
                        sp.dma_start(big[:, u, 0:wide], dst_major[bass.ds(b, 1), :, h * HALF * LANES:h * HALF * LANES + wide]
                                     .rearrange("a p c -> (a p) c")).then_inc(big_in[u], 16)
                    lot(0, 4)
                    with sp.Fori(0, (BLOCKS - 1) // 4) as i:
                        for u in range(4):
                            lot(i * 4 + u + 1, u)
            for b in range(3):
                sp.dma_start(bigs[b][:, :], src_major[b]).then_inc(bigs_in[b], 16)
            with sp.Fori(1, BLOCKS // 3) as i:
                for u in range(3):
                    b = i * 3 + u
                    sp.wait_ge(s2t_mm, b - 2)
                    sp.dma_start(bigs[u][:, :], src_major[bass.ds(b, 1), :, :].rearrange("a p c -> (a p) c")).then_inc(bigs_in[u], 16)
            sp.wait_ge(s2t_mm, BLOCKS - 3)
            sp.dma_start(bigs[0][:, :], src_major[BLOCKS - 1]).then_inc(bigs_in[0], 16)

            sp.wait_ge(act_done, 100)
            sp.dma_start(out[0:(BLOCKS - 1) * LANES, :].rearrange("(b p) f -> p b f", p=LANES), W[:, 0:BLOCKS - 1, :]).then_inc(stored, 16)
            sp.dma_start(out[(BLOCKS - 1) * LANES:NODES, :], W[0:LAST, BLOCKS - 1, :]).then_inc(stored, 16)
            sp.wait_ge(stored, 32)

        @block.gpsimd
        def _(gp):
            gp.iota(row_no[:, :], [[1, SLOT_ROWS_UP]], base=0, channel_multiplier=0, allow_small_or_imprecise_dtypes=True).then_inc(pool_consts, 1)
            gp.iota(lane_no[:, :], [[0, 1]], base=0, channel_multiplier=1, allow_small_or_imprecise_dtypes=True).then_inc(pool_consts, 1)

            last_node, last_slot = gp.to_reg(PADDED - 1), gp.to_reg(SLOT_ROWS_UP * PADDED - 1)

            def gather(i, first=False, last=False):
                for u in range(RING):
                    g, nu = RING * i + u, (u + 1) % RING
                    gp.wait_ge(gidx_ready, g + 1)
                    if not (last and nu == 0):
                        if not (first and nu):
                            gp.wait_ge(edge_v_done, g + 1 - RING + 1)
                        gp.tensor_copy(gidx[:, nu, :], src_i[:, bass.ds((g + 1) * TILES, TILES)]).then_inc(gidx_ready, 1)
                    for j in range(TILES):
                        gp.indirect_dma_start(gat[:, u, j, :], None, table,
                                              bass.IndirectOffsetOnAxis(ap=gidx[:, u, j:j + 1], axis=0),
                                              bounds_check=last_node, oob_is_err=False).then_inc(gat_in[u], 16)

            gp.wait_ge(edges_in, 80)
            gp.tensor_copy(gidx[:, 0, :], src_i[:, 0:TILES]).then_inc(gidx_ready, 1)
            gp.wait_ge(table_out, 16)
            gather(0, first=True)
            with gp.Fori(1, GROUPS // RING - 1) as i:
                gather(i)
            gather(GROUPS // RING - 1, last=True)

            def copy_next(g, u):
                gp.tensor_copy(sidx[:, u, :], slot_idx[:, bass.ds(g * TILES, TILES)]).then_inc(sidx_ready, 1)
                gp.tensor_copy(spay[:, u, :, :], payload[:, bass.ds(g * TILES, TILES), :]).then_inc(sidx_ready, 1)

            def deal(i, first=False, last=False):
                for u in range(RING):
                    g, nu = RING * i + u, (u + 1) % RING
                    gp.wait_ge(sidx_ready, 2 * g + 2)
                    if not (last and nu == 0):
                        if not (first and nu):
                            gp.wait_ge(dealt[nu], 16 * TILES * (i + (nu == 0)))
                        copy_next(g + 1, nu)
                    for j in range(TILES):
                        gp.indirect_dma_start(slots, bass.IndirectOffsetOnAxis(ap=sidx[:, u, j:j + 1], axis=0),
                                              spay[:, u, j, :], None,
                                              bounds_check=last_slot, oob_is_err=False).then_inc(dealt[u], 16)

            gp.wait_ge(filled, 16 * (FILLS + 2))
            copy_next(0, 0)
            deal(0, first=True)
            with gp.Fori(1, GROUPS // RING - 1) as i:
                deal(i)
            deal(GROUPS // RING - 1, last=True)
            for u in range(RING):
                gp.wait_ge(dealt[u], 16 * TILES * (GROUPS // RING))
            gp.nop().then_inc(build_start, 1)

        @block.vector
        def _(v):
            n = 0

            def step(ins):
                nonlocal n
                n += 1
                return ins.then_inc(vec, 1)

            def settled():
                v.wait_ge(vec, n)

            v.memset(prev_i[:, :], -1).then_inc(vec_consts, 1)
            v.memset(next_i[:, :], -1).then_inc(vec_consts, 1)
            v.memset(ones[:, :], 1.0).then_inc(vec_consts, 1)
            v.memset(X[:, :, :], 0.0).then_inc(vec_consts, 1)
            v.memset(minus1[:, :], -1.0).then_inc(vec_consts, 1)
            step(v.memset(edpad[:, :, 1:2], -1.0))
            step(v.memset(edpad[:, :, 0:1], 0.0))
            v.memset(zpad[:, :], 0.0).then_inc(vec_consts, 1)
            v.wait_ge(pool_consts, 2)
            step(v.tensor_copy(iota[:, :], row_no[:, 0:LANES]))
            step(v.tensor_copy(iota16[:, :], row_no[:, 0:LANES]))
            settled()
            step(v.tensor_scalar(ident[:, :], iota[:, :], lane_no[:, 0:1], None, ALU.is_equal))
            step(v.tensor_scalar(ident16[:, :], iota[:, :], lane_no[:, 0:1], None, ALU.is_equal))
            step(v.tensor_scalar(upper[:, :], iota[:, :], lane_no[:, 0:1], None, ALU.is_ge))
            v.wait_ge(edges_in, 80)
            step(v.tensor_scalar(ra[:, :].bitcast(I32), src_i[:, :], 7, None, ALU.logical_shift_right))
            settled()
            step(v.tensor_copy(sblk[:, :], ra[:, :].bitcast(I32)))
            step(v.tensor_copy(rb[:, :], src_i[:, :]))
            settled()
            step(v.scalar_tensor_tensor(payload[:, :, 0], sblk[:, :], -float(LANES), rb[:, :], ALU.mult, ALU.add))
            settled()
            step(v.tensor_scalar(ra[:, :].bitcast(I32), dst_i[:, :], 7, None, ALU.logical_shift_right))
            step(v.tensor_copy(exp_dst[:, :, 1], dst_i[:, :]))
            settled()
            step(v.tensor_copy(dblk[:, :], ra[:, :].bitcast(I32)))
            step(v.tensor_copy(rb[:, :], prev_i[:, :]))
            settled()
            step(v.scalar_tensor_tensor(payload[:, :, 1], dblk[:, :], -float(LANES), exp_dst[:, :, 1], ALU.mult, ALU.add))
            step(v.tensor_tensor(cnt[:, :], exp_dst[:, :, 1], rb[:, :], ALU.is_equal))
            step(v.tensor_scalar(ra[:, :].bitcast(I32), prev_i[:, :], 7, None, ALU.arith_shift_right))
            step(v.tensor_copy(next_f[:, :], next_i[:, :]))
            settled()
            step(v.tensor_scalar(pen[:, 0:COLS], cnt[:, :], 1.0, -NEG, ALU.subtract, ALU.mult))
            step(v.tensor_copy(rb[:, :], ra[:, :].bitcast(I32)))
            step(v.tensor_tensor(next_f[:, :], exp_dst[:, COLS - 1:COLS, 1], next_f[:, :], ALU.is_equal))
            settled()
            step(v.tensor_tensor(keep_b[:, :], dblk[:, :], rb[:, :], ALU.is_equal))
            step(v.tensor_scalar(pen[:, COLS:COLS + 1], next_f[:, :], 1.0, -NEG, ALU.subtract, ALU.mult))
            settled()
            step(v.tensor_tensor_scan(before[:, :], keep_b[:, :], keep_b[:, :], 1.0, ALU.mult, ALU.mult))
            settled()
            step(v.tensor_copy(no_break[:, :], before[:, COLS - 1:COLS]))
            settled()
            step(v.tensor_scalar(nb_diag[:, :], ident[0:ROWS, 0:ROWS], no_break[:, 0:1], None, ALU.mult))

            for k in range(COLS // HIST):
                q = k % 2
                if k >= 2:
                    v.wait_ge(hist_used, k - 1)
                for blk, one_hot in ((dblk, oh_d), (sblk, oh_s)):
                    v.tensor_tensor(one_hot[:, q, :, :],
                                    blk[:, k * HIST:(k + 1) * HIST].unsqueeze(2).to_broadcast([ROWS, HIST, BLOCKS]),
                                    iota[0:ROWS, 0:BLOCKS].unsqueeze(1).to_broadcast([ROWS, HIST, BLOCKS]),
                                    ALU.is_equal).then_inc(hist_ready, 1)
            v.wait_ge(hist_used, COLS // HIST)
            hist = ps[0:BLOCKS, 0, 0:BLOCKS]
            step(v.tensor_reduce(bt[:, 0:1], hist, AX.X, ALU.max))
            settled()
            step(v.tensor_reduce(bt[:, 2:3], hist, AX.X, ALU.add))
            settled()
            step(v.tensor_scalar(bti[:, 0:1], bt[:, 0:1], float(LANES - 1), None, ALU.add))
            step(v.tensor_scalar(bti[:, 1:2], bt[:, 2:3], float(CHUNK - 1), None, ALU.add))
            settled()
            step(v.tensor_scalar(bti[:, 0:1], bti[:, 0:1], 7, None, ALU.logical_shift_right))
            step(v.tensor_scalar(bti[:, 1:2], bti[:, 1:2], 10, None, ALU.logical_shift_right))
            settled()
            step(v.tensor_scalar(bt[:, 0:1], bti[:, 0:1], 1.0, None, ALU.max))
            step(v.tensor_copy(bt[:, 1:2], bti[:, 1:2]))
            settled()
            v.nop().then_inc(tab_v, 1)
            v.wait_ge(tab_pe, 1)
            step(v.tensor_copy(bend[:, :], ps[0:BLOCKS, 1, 0:3]))
            step(v.tensor_copy(n_rows[:, :], ps[0:1, 1, 8:9]))
            settled()
            step(v.tensor_tensor(bstart[:, :], bend[:, :], bt[:, :], ALU.subtract))
            settled()
            step(v.tensor_scalar(rs_diag[:, :], ident[0:BLOCKS, 0:BLOCKS], bstart[:, 0:1], None, ALU.mult))
            step(v.scalar_tensor_tensor(base_v[:, :], bstart[:, 1:2], -float(CHUNK), bstart[:, 2:3], ALU.mult, ALU.add))
            step(v.tensor_scalar(row_cmp[:, :], row_no[0:BLOCKS, :], bend[:, 0:1], None, ALU.is_ge))
            settled()
            step(v.tensor_scalar(base_v[:, :], base_v[:, :], -float(EDGES), None, ALU.add))
            settled()
            step(v.tensor_scalar(base_m[:, :], ones[0:BLOCKS, :], base_v[:, 0:1], None, ALU.mult))
            settled()
            v.nop().then_inc(tab_v, 1)
            v.wait_ge(tab_pe, 2)
            step(v.tensor_copy(row_start[:, :], ps[0:ROWS, 0, 0:BLOCKS]))
            step(v.tensor_copy(block_of_row[:, :].rearrange("a (k c) -> a k c", k=4), ps[0:1, 2:6, 0:SLOT_ROWS_UP // 4]))
            settled()
            step(v.tensor_scalar(row_cmp[:, :], row_no[0:BLOCKS, :], bstart[:, 0:1], None, ALU.is_equal))
            step(v.tensor_scalar(chunk_tmp[0:BLOCKS, :], row_no[0:BLOCKS, 0:CHUNKS], bend[:, 1:2], None, ALU.is_ge))
            step(v.tensor_scalar(chunk_oh[:, :], row_no[0:BLOCKS, 0:CHUNKS], bstart[:, 1:2], None, ALU.is_ge))
            settled()
            step(v.tensor_tensor(chunk_oh[:, :], chunk_oh[:, :], chunk_tmp[0:BLOCKS, :], ALU.subtract))
            settled()
            v.nop().then_inc(tab_v, 1)
            v.wait_ge(tab_pe, 3)
            step(v.tensor_scalar(keep_row[:, :].rearrange("p (k c) -> p k c", k=4), ps[:, 2:6, 0:SLOT_ROWS_UP // 4],
                                 -1.0, 1.0, ALU.mult, ALU.add))
            step(v.tensor_scalar(chunk_first[:, :], ps[:, 0, 0:CHUNKS], float(LANES), None, ALU.mult))
            step(v.tensor_copy(chunk_block[:, :], ps[0:1, 0, 0:CHUNKS]))
            settled()
            step(v.scalar_tensor_tensor(chunk_tmp[0:1, :], row_no[0:1, 0:CHUNKS], float(CHUNK), ps[0:1, 6, 0:CHUNKS], ALU.mult, ALU.mult))
            settled()
            step(v.scalar_tensor_tensor(chunk_base[:, :], ps[0:1, 1, 0:CHUNKS], float(EDGES), chunk_tmp[0:1, :], ALU.add, ALU.add))
            settled()
            v.nop().then_inc(tab_v, 1)

            def rank(s, q, first):
                v.tensor_scalar(ind[:, :], sblk[:, :], iota[0:ROWS, bass.ds(s, 1)], None, ALU.is_equal).then_inc(rank_step, 1)
                v.wait_ge(rank_step, 3 * s + 1)
                v.tensor_tensor_scan(cnt[:, :], keep_b[:, :], ind[:, :], 0.0, ALU.mult, ALU.add).then_inc(rank_step, 1)
                v.wait_ge(rank_step, 3 * s + 2)
                if not first:
                    v.wait_ge(pick_used, s - 1)
                v.tensor_tensor(picked[:, q, :], ind[:, :], cnt[:, :], ALU.mult).then_inc(pick_ready, 1)
                v.tensor_copy(row_last[:, bass.ds(s, 1)], cnt[:, COLS - 1:COLS]).then_inc(rank_step, 1)
                v.wait_ge(rank_step, 3 * s + 3)
                v.wait_ge(pick_ready, s + 1)

            rank(0, 0, True)
            rank(1, 1, True)
            with v.Fori(1, BLOCKS // 2) as i:
                for q in range(2):
                    rank(i * 2 + q, q, False)
            rank(BLOCKS - 1, 0, False)
            v.wait_ge(tab_pe, 4)
            step(v.tensor_copy(row_last_t[:, :], ps[0:BLOCKS, 4, 0:ROWS]))
            step(v.tensor_copy(nb_t[:, :], ps[0:BLOCKS, 5, 0:ROWS]))
            step(v.memset(carry_t[:, 0:1], 0.0))
            settled()
            step(v.tensor_tensor_scan(carry_t[:, 1:ROWS + 1], nb_t[:, :], row_last_t[:, :], 0.0, ALU.mult, ALU.add))
            settled()
            v.nop().then_inc(tab_v, 1)
            v.wait_ge(tab_pe, 5)
            step(v.tensor_copy(carry[:, :], ps[0:ROWS, 4, 0:BLOCKS]))
            settled()
            v.wait_ge(pick_used, BLOCKS)
            step(v.tensor_scalar(cnt[:, :].rearrange("p (k c) -> p k c", k=4), ps[0:ROWS, 0:4, 0:COLS // 4], -1.0, None, ALU.add))
            settled()
            v.nop().then_inc(tab_v, 1)

            def lookup(values, keys, base):
                def one(s, q, first):
                    if not first:
                        v.wait_ge(pick_used, base + s - 1)
                    v.tensor_scalar(picked[:, q, :], keys[:, :], iota[0:ROWS, bass.ds(s, 1)], values[:, bass.ds(s, 1)],
                                    ALU.is_equal, ALU.mult).then_inc(pick_ready, 1)
                v.wait_ge(pick_used, base)
                one(0, 0, True)
                one(1, 1, True)
                with v.Fori(1, BLOCKS // 2) as i:
                    for q in range(2):
                        one(i * 2 + q, q, False)
                one(BLOCKS - 1, 0, False)

            lookup(carry, sblk, BLOCKS)
            v.wait_ge(pick_used, 2 * BLOCKS)
            step(v.tensor_tensor(ra[:, :].rearrange("p (k c) -> p k c", k=4), ps[0:ROWS, 4:8, 0:COLS // 4],
                                 before[:, :].rearrange("p (k c) -> p k c", k=4), ALU.mult))
            lookup(row_start, dblk, 2 * BLOCKS)
            settled()
            step(v.tensor_tensor(cnt[:, :], cnt[:, :], ra[:, :], ALU.add))
            settled()
            step(v.tensor_copy(prev_i[:, :], cnt[:, :]))
            settled()
            step(v.tensor_scalar(dst_i[:, :], prev_i[:, :], 7, None, ALU.logical_shift_right))
            settled()
            step(v.tensor_copy(ra[:, :], dst_i[:, :]))
            settled()
            step(v.scalar_tensor_tensor(rb[:, :], ra[:, :], -float(LANES), cnt[:, :], ALU.mult, ALU.add))
            v.wait_ge(pick_used, 3 * BLOCKS)
            step(v.tensor_tensor(ind[:, :].rearrange("p (k c) -> p k c", k=4), ps[0:ROWS, 0:4, 0:COLS // 4],
                                 ra[:, :].rearrange("p (k c) -> p k c", k=4), ALU.add))
            settled()
            step(v.scalar_tensor_tensor(before[:, :], ind[:, :], float(PADDED), sblk[:, :], ALU.mult, ALU.add))
            settled()
            step(v.scalar_tensor_tensor(slot_idx[:, :], rb[:, :], float(BLOCKS), before[:, :], ALU.mult, ALU.add))
            settled()
            v.nop().then_inc(ranked, 1)

            v.wait_ge(filled, 16 * (FILLS + 2))
            step(v.memset(xt[:, NODES:PADDED], 0.0))
            step(v.memset(msgb[:, :, :, DIM:MSGW], 1.0))
            settled()
            v.nop().then_inc(ranked, 1)

            def edge_group(i, first):
                for u in range(RING):
                    g = RING * i + u
                    q = u % 2
                    pv = ps[0:ROWS, 4 * q:4 * q + 4, 0:6 * DIM].rearrange("p k (t c) -> p k t c", t=2)
                    gv = gat[:, u, :, :].rearrange("p (k t) c -> p k t c", t=2)
                    kv = kk[:, q, :, :].rearrange("p (k t) c -> p k t c", t=2)
                    mv = mm[:, q, :, :].rearrange("p (k t) c -> p k t c", t=2)
                    v.wait_ge(edge_mm, g + 1)
                    v.wait_ge(gat_in[u], 16 * TILES * (i + 1))
                    v.tensor_tensor(kv, pv[:, :, :, DIM:2 * DIM], gv[:, :, :, DIM:2 * DIM], ALU.add).then_inc(edge_step, 1)
                    v.tensor_tensor(mv, pv[:, :, :, 0:DIM], gv[:, :, :, 0:DIM], ALU.add).then_inc(edge_step, 1)
                    v.wait_ge(edge_step, 3 * g + 1)
                    v.tensor_tensor(kv, kv, pv[:, :, :, 2 * DIM:3 * DIM], ALU.mult).then_inc(edge_v_done, 1)
                    v.wait_ge(edge_step, 3 * g + 2)
                    if not first:
                        v.wait_ge(msg_out[u], 16 * i)
                    v.scalar_tensor_tensor(msgb[:, u, :, 0:DIM], mm[:, q, :, :], 0.01, mm[:, q, :, :], ALU.mult, ALU.max).then_inc(msg_ready, 1)
                    v.wait_ge(edge_v_done, g + 1)
                    v.tensor_reduce(att[:, bass.ds(g * TILES, TILES)], kk[:, q, :, :], AX.X, ALU.add).then_inc(edge_step, 1)

            edge_group(0, True)
            with v.Fori(1, GROUPS // RING) as i:
                edge_group(i, False)
            v.wait_ge(edge_step, 3 * GROUPS)
            v.wait_ge(msg_ready, GROUPS)
            step(v.tensor_scalar(att[:, :], att[:, :], float(DIM) ** -0.5, None, ALU.mult))
            settled()

            def passed_on(values, penalties, k, reverse):
                step(v.tensor_copy(edge_v[:, 0:1], values))
                step(v.tensor_reduce(edge_v[:, 1:2], penalties, AX.X, ALU.min))
                settled()
                v.nop().then_inc(line_v, 1)
                v.wait_ge(line_pe, 2 * k + 1)
                step(v.tensor_copy(line[:, :, :], ps[0:1, 0:2, 0:ROWS]))
                step(v.memset(line_c[:, :], NEG))
                settled()
                if reverse:
                    step(v.tensor_tensor_scan(line_c[:, 0:ROWS][:, ::-1], line[:, 1, :][:, ::-1], line[:, 0, :][:, ::-1], NEG, ALU.add, ALU.max))
                else:
                    step(v.tensor_tensor_scan(line_c[:, 1:ROWS + 1], line[:, 1, :], line[:, 0, :], NEG, ALU.add, ALU.max))
                settled()
                v.nop().then_inc(line_v, 1)
                v.wait_ge(line_pe, 2 * k + 2)
                step(v.tensor_copy(edge_in[:, :], ps[0:ROWS, 2, 0:1]))
                settled()

            step(v.tensor_tensor_scan(seg_f[:, :], pen[:, 0:COLS], att[:, :], NEG, ALU.add, ALU.max))
            settled()
            passed_on(seg_f[:, COLS - 1:COLS], pen[:, 0:COLS], 0, False)
            step(v.tensor_tensor_scan(seg_f[:, :], pen[:, 0:COLS], att[:, :], edge_in[:, 0:1], ALU.add, ALU.max))
            settled()
            step(v.tensor_tensor_scan(seg_m[:, :][:, ::-1], pen[:, 1:COLS + 1][:, ::-1], seg_f[:, :][:, ::-1], NEG, ALU.add, ALU.max))
            settled()
            passed_on(seg_m[:, 0:1], pen[:, 1:COLS + 1], 1, True)
            step(v.tensor_tensor_scan(seg_m[:, :][:, ::-1], pen[:, 1:COLS + 1][:, ::-1], seg_f[:, :][:, ::-1], edge_in[:, 0:1], ALU.add, ALU.max))
            settled()
            step(v.tensor_tensor(seg_f[:, :], att[:, :], seg_m[:, :], ALU.subtract))
            settled()
            v.nop().then_inc(exp_in, 1)
            v.wait_ge(exp_done, 1)

            step(v.memset(agg[:, :, :], 0.0))
            settled()

            def add_chunk(r):
                c = v.value_load(chunk_block[0:1, bass.ds(r, 1)], min_val=0, max_val=BLOCKS)
                v.wait_ge(agg_mm, r + 1)
                return c

            def agg_chunk(i, u, first):
                r = RING * i + u
                q = u % 2
                v.wait_ge(chunk_in[u], 32 * (i + 1))
                v.tensor_scalar(rel[:, u, :], ech[:, u, :, 1], chunk_first[:, bass.ds(r, 1)], None, ALU.subtract).then_inc(agg_rel, 1)
                v.wait_ge(agg_rel, r + 1)
                if not (first and u < 2):
                    v.wait_ge(agg_mm, r - 1)
                for j in range(PER_LANE):
                    v.tensor_scalar(woh[:, q, j, :], iota[:, :], rel[:, u, j:j + 1], ech[:, u, j, 0:1], ALU.is_equal, ALU.mult).then_inc(woh_ready, 1)
                if not (first and u == 0):
                    c = add_chunk(r - 1)
                    if not (first and u == 1):
                        v.wait_ge(agg_added, r - 1)
                    v.tensor_tensor(agg[:, bass.ds(c, 1), :].rearrange("p a c -> p (a c)"), agg[:, bass.ds(c, 1), :].rearrange("p a c -> p (a c)"),
                                    ps[:, (u + 1) % 2, 0:MSGW], ALU.add).then_inc(agg_added, 1)

            for u in range(RING):
                agg_chunk(0, u, True)
            with v.Fori(1, CHUNKS // RING) as i:
                for u in range(RING):
                    agg_chunk(i, u, False)
            c = add_chunk(CHUNKS - 1)
            v.wait_ge(agg_added, CHUNKS - 1)
            v.tensor_tensor(agg[:, bass.ds(c, 1), :].rearrange("p a c -> p (a c)"), agg[:, bass.ds(c, 1), :].rearrange("p a c -> p (a c)"),
                            ps[:, (CHUNKS - 1) % 2, 0:MSGW], ALU.add).then_inc(agg_added, 1)
            v.wait_ge(agg_added, CHUNKS)

            def over(a, w=DIM):
                return a.unsqueeze(2).to_broadcast([LANES, BLOCKS, w])

            def feat(a):
                return a.unsqueeze(1).to_broadcast([LANES, BLOCKS, DIM])

            a = 0

            def sqrt_of(t):
                nonlocal a
                settled()
                v.nop().then_inc(act_v, 1)
                a += 1
                v.wait_ge(act_done, a)

            def layer_norm(o, t, eps):
                step(v.tensor_reduce(mean[:, :], t[:, :, :], AX.X, ALU.add))
                settled()
                step(v.tensor_scalar(mean[:, :], mean[:, :], 1.0 / DIM, None, ALU.mult))
                settled()
                step(v.tensor_tensor(o[:, :, :], t[:, :, :], over(mean[:, :]), ALU.subtract))
                settled()
                step(v.tensor_tensor(ylo[:, :, :], o[:, :, :], o[:, :, :], ALU.mult))
                settled()
                step(v.tensor_reduce(var[:, :], ylo[:, :, :], AX.X, ALU.add))
                settled()
                step(v.tensor_scalar(var[:, :], var[:, :], 1.0 / DIM, eps, ALU.mult, ALU.add))
                sqrt_of(var)
                step(v.reciprocal(var[:, :], var[:, :]))
                settled()
                step(v.tensor_tensor(o[:, :, :], o[:, :, :], over(var[:, :]), ALU.mult))
                settled()

            def product_out(k, o, add):
                for q in range(13):
                    w = min(4, BLOCKS - 4 * q)
                    v.wait_ge(nt_mm, 13 * k + q + 1)
                    src_ps = ps[:, 4 + q % 2, 0:w * DIM].rearrange("p (b f) -> p b f", f=DIM)
                    v.tensor_copy(o[:, 4 * q:4 * q + w, :], src_ps).then_inc(nt_out, 1)
                v.wait_ge(nt_out, 13 * (k + 1))

            step(v.tensor_scalar(has[:, :], agg[:, 0:BLOCKS, DIM], 0.0, None, ALU.is_gt))
            step(v.tensor_scalar(den[:, :], agg[:, 0:BLOCKS, DIM], 1.0, None, ALU.max))
            settled()
            step(v.reciprocal(den[:, :], den[:, :]))
            settled()
            step(v.tensor_tensor(Z[:, :, 0:DIM], agg[:, 0:BLOCKS, 0:DIM], over(den[:, :]), ALU.mult))
            settled()
            v.nop().then_inc(nt_ready, 1)
            product_out(0, Y, None)
            step(v.scalar_tensor_tensor(Y[:, :, :], Y[:, :, :], 0.01, Y[:, :, :], ALU.mult, ALU.max))
            settled()
            step(v.tensor_tensor(Y[:, :, :], Y[:, :, :], X[:, :, :], ALU.add))
            settled()
            layer_norm(W, Y, 1e-6)
            step(v.tensor_tensor(W[:, :, :], W[:, :, :], feat(gam[:, :]), ALU.mult))
            settled()
            step(v.tensor_tensor(W[:, :, :], W[:, :, :], feat(bet[:, :]), ALU.add))
            settled()
            step(v.tensor_tensor(W[:, :, :], W[:, :, :], over(has[:, :]), ALU.mult))
            step(v.tensor_scalar(mean[:, :], has[:, :], -1.0, 1.0, ALU.mult, ALU.add))
            settled()
            step(v.tensor_tensor(Y[:, :, :], X[:, :, :], over(mean[:, :]), ALU.mult))
            settled()
            step(v.tensor_tensor(W[:, :, :], W[:, :, :], Y[:, :, :], ALU.add))
            settled()
            step(v.tensor_tensor(W[:, :, :], W[:, :, :], X[:, :, :], ALU.add))
            settled()
            layer_norm(X, W, 1e-5)

            step(v.memset(cacc[:, :, :], 0.0))
            settled()
            v.nop().then_inc(tab_v, 1)
            v.wait_ge(build_start, 1)
            rows = v.value_load(n_rows[0:1, 0:1], min_val=1, max_val=SLOT_ROWS)
            v.nop().then_inc(pay_read, 2)
            with v.Fori(0, ROW_LOOPS) as o:
                with v.If(o * ROW_LOOP < rows):
                    with v.Fori(0, ROW_LOOP // 2) as j:
                        for u in range(2):
                            r = o * ROW_LOOP + j * 2 + u
                            with v.If(r < rows):
                                v.wait_ge(pay_in[u], (o * (ROW_LOOP // 2) + j + 1) * 16)
                                v.tensor_copy(payf[:, u, :, :], pay[:, u, :, :]).then_inc(pay_read, 1)
                                v.tensor_scalar(keep_diag[:, u, :], ident16[:, :], keep_row[:, bass.ds(r, 1)], None, ALU.mult).then_inc(pay_conv, 1)
                                v.wait_ge(pay_read, r + 3)
                                for g in range(BG):
                                    q = (BG * u + g) % 2
                                    v.wait_ge(tile_mm, r * (2 * BG) + 2 * g + 2)
                                    for s in range(BG):
                                        for k in range(2):
                                            ins = v.tensor_scalar(oh[:, q, s, k, :], iota16[:, :], payf[:, u, g * BG + s, k:k + 1], None, ALU.is_equal)
                                            ins.then_inc(oh_ready, 1)
            v.wait_ge(built, 1)

            step(v.memset(one16[:, :], 1.0))
            step(v.memset(xs[:, :, 2 * DIM:2 * DIM + 1], 1.0))
            settled()

            def split(t):
                step(v.tensor_scalar(xs[:, :, 0:DIM], t[:, :, :], SCALE, None, ALU.mult))
                settled()
                step(v.scalar_tensor_tensor(xs[:, :, DIM:2 * DIM], t[:, :, :], SCALE, xs[:, :, 0:DIM], ALU.mult, ALU.subtract))
                settled()
                v.nop().then_inc(xs_ready, 1)

            def sweep(w):
                h = w % 2
                b0, b1 = ((0, HALF), (HALF, BLOCKS))[h]
                v.wait_ge(lo_copied, w + 1)
                pv = ps[:, 0:7, :].rearrange("p k (b c) -> p (k b) c", c=LANES)[:, 0:b1 - b0, :]
                v.scalar_tensor_tensor(Y[:, b0:b1, :], pv[:, :, 0:DIM], 1.0 / SCALE, ylo[:, b0:b1, :], ALU.mult, ALU.add).then_inc(sweep_read, 1)

            v.nop().then_inc(sweep_read, 1)
            split(X)
            step(v.tensor_copy(total[:, :, :], X[:, :, :]))
            for hop in range(3):
                sweep(2 * hop)
                sweep(2 * hop + 1)
                v.wait_ge(sweep_read, 2 * hop + 3)
                if hop == 0:
                    step(v.tensor_scalar(has[:, :], ps[:, 7, 0:BLOCKS], 0.0, None, ALU.is_gt))
                    settled()
                    step(v.tensor_scalar(mean[:, :], ps[:, 7, 0:BLOCKS], 1.0, None, ALU.max))
                    settled()
                    step(v.reciprocal(cnt_d[:, :], mean[:, :]))
                    settled()
                    step(v.tensor_tensor(deg_inv[:, :], cnt_d[:, :], has[:, :], ALU.mult))
                    step(v.tensor_copy(var[:, :], cnt_d[:, :]))
                    sqrt_of(var)
                    step(v.tensor_tensor(deg_rsq[:, :], var[:, :], has[:, :], ALU.mult))
                    settled()
                step(v.tensor_tensor(Y[:, :, :], Y[:, :, :], over(deg_inv[:, :]), ALU.mult))
                settled()
                if hop < 2:
                    split(Y)
                step(v.tensor_tensor(total[:, :, :], total[:, :, :], Y[:, :, :], ALU.add))
                settled()
            step(v.scalar_tensor_tensor(X[:, :, :], total[:, :, :], 0.25, X[:, :, :], ALU.mult, ALU.add))
            settled()
            layer_norm(X, X, 1e-5)
            step(v.tensor_tensor(W[:, :, :], X[:, :, :], over(deg_rsq[:, :]), ALU.mult))
            settled()
            split(W)
            sweep(6)
            sweep(7)
            v.wait_ge(sweep_read, 9)
            step(v.tensor_tensor(Y[:, :, :], Y[:, :, :], over(deg_rsq[:, :]), ALU.mult))
            settled()
            step(v.tensor_tensor(X[:, :, :], X[:, :, :], Y[:, :, :], ALU.add))
            settled()
            layer_norm(X, X, 1e-5)
            split(X)
            sweep(8)
            sweep(9)
            v.wait_ge(sweep_read, 11)
            step(v.tensor_tensor(Y[:, :, :], Y[:, :, :], over(deg_inv[:, :]), ALU.mult))
            step(v.tensor_copy(Z[:, :, 0:DIM], X[:, :, :]))
            settled()

            def s2t(b, q):
                v.wait_ge(s2t_lo, b + 1)
                v.scalar_tensor_tensor(W[:, bass.ds(b, 1), :].rearrange("p a c -> p (a c)"), ps[:, q, 0:DIM], 1.0 / SCALE,
                                       ylo[:, bass.ds(b, 1), :].rearrange("p a c -> p (a c)"), ALU.mult, ALU.add).then_inc(s2t_read, 1)
            v.nop().then_inc(s2t_read, 2)
            with v.Fori(0, BLOCKS // 2) as i:
                for q in range(2):
                    s2t(i * 2 + q, q)
            s2t(BLOCKS - 1, 0)
            v.wait_ge(s2t_read, BLOCKS + 2)
            step(v.tensor_scalar(cnt_d[:, :], cnt_d[:, :], 1.0, None, ALU.max))
            settled()
            step(v.reciprocal(cnt_d[:, :], cnt_d[:, :]))
            settled()
            step(v.tensor_tensor(W[:, :, :], W[:, :, :], over(cnt_d[:, :]), ALU.mult))
            settled()
            step(v.tensor_tensor(Z[:, :, DIM:2 * DIM], Y[:, :, :], W[:, :, :], ALU.add))
            settled()
            v.nop().then_inc(nt_ready, 1)
            product_out(1, Y, None)
            step(v.tensor_tensor(Y[:, :, :], Y[:, :, :], feat(bl[:, :]), ALU.add))
            settled()
            step(v.tensor_tensor(Y[:, :, :], Y[:, :, :], X[:, :, :], ALU.add))
            settled()
            layer_norm(W, Y, 1e-5)
            v.nop().then_inc(act_done, 100 - a)

        @block.scalar
        def _(sc):
            for q in range(BLOCKS // 4 + 1):
                w = min(4, BLOCKS - 4 * q)
                sc.wait_ge(proj_pe, q + 1)
                sc.activation(proj[:, 4 * q:4 * q + w, :], ps[:, q % 2, 0:w * 2 * DIM].rearrange("p (b f) -> p b f", f=2 * DIM), ACT.Copy).then_inc(proj_act, 1)

            def store(i):
                for u in range(RING):
                    g = RING * i + u
                    sc.wait_ge(msg_ready, g + 1)
                    sc.dma_start(msg_rows[:, bass.ds(g * TILES, TILES), :], msgb[:, u, :, :]).then_inc(msg_out[u], 16)
            with sc.Fori(0, GROUPS // RING) as i:
                store(i)
            sc.wait_ge(exp_in, 1)
            sc.activation(exp_dst[:, :, 0], seg_f[:, :], ACT.Exp).then_inc(exp_done, 2)

            def product_copies(k, part):
                for q in range(13):
                    w = min(4, BLOCKS - 4 * q)
                    sc.wait_ge(nt_t, 13 * k + q + 1)
                    if q >= 2 or k:
                        sc.wait_ge(nt_mm, 13 * k + q - 1)
                    sc.activation(zt[0:part, q % 2, 0:w * LANES], ps[0:part, 2 + q % 2, 0:w * LANES], ACT.Copy).then_inc(nt_copied, 1)

            def sqrt(t, k):
                sc.wait_ge(act_v, k)
                sc.activation(t[:, :], t[:, :], ACT.Sqrt).then_inc(act_done, 1)

            product_copies(0, DIM)
            sqrt(var, 1)
            sqrt(var, 2)

            sc.wait_ge(tab_v, TAB_V + 2)
            for g in range(BG):
                for l, mat in enumerate((dst_major, src_major)):
                    sc.dma_start(mat[0][:, g * BGW:(g + 1) * BGW], cacc[:, l, g * BGW:(g + 1) * BGW]).then_inc(counts_out[g], 16)
            sc.wait_ge(build_start, 1)
            rows = sc.value_load(n_rows[0:1, 0:1], min_val=1, max_val=SLOT_ROWS)
            with sc.Fori(0, ROW_LOOPS) as o:
                with sc.If(o * ROW_LOOP < rows):
                    with sc.Fori(0, ROW_LOOP // 2) as j:
                        for u in range(2):
                            r = o * ROW_LOOP + j * 2 + u
                            with sc.If(r < rows):
                                b = sc.value_load(block_of_row[0:1, bass.ds(r, 1)], min_val=0, max_val=BLOCKS - 1)
                                for g in range(BG):
                                    q = (BG * u + g) % 2
                                    sc.wait_ge(counts_out[g], (r + 1) * 32)
                                    for l in range(2):
                                        sc.wait_ge(tile_mm, r * (2 * BG) + 2 * g + l + 1 + JOB_CREDIT)
                                        sc.activation(cacc[:, l, g * BGW:(g + 1) * BGW],
                                                      ps[:, 4 * q + 2 * l:4 * q + 2 * l + 2, :].rearrange("p k c -> p (k c)")[:, 0:BGW], ACT.Copy).then_inc(tile_copied, 1)
                                    sc.wait_ge(tile_copied, r * (2 * BG) + 2 * g + 2 + JOB_CREDIT)
                                    for l, mat in enumerate((dst_major, src_major)):
                                        sc.dma_start(mat[bass.ds(b, 1), :, g * BGW:(g + 1) * BGW].rearrange("a p c -> (a p) c"),
                                                     cacc[:, l, g * BGW:(g + 1) * BGW]).then_inc(counts_out[g], 16)
            for g in range(BG):
                sc.wait_ge(counts_out[g], (rows + 1) * 32)
            sc.nop().then_inc(built, 1)

            def low(w):
                h = w % 2
                b0, b1 = ((0, HALF), (HALF, BLOCKS))[h]
                sc.wait_ge(sweep_mm, w + 1)
                pv = ps[:, 0:7, :].rearrange("p k (b c) -> p (k b) c", c=LANES)[:, 0:b1 - b0, :]
                sc.activation(ylo[:, b0:b1, :], pv[:, :, DIM:2 * DIM], ACT.Copy, scale=1.0 / SCALE).then_inc(lo_copied, 1)

            k = 3
            for w in range(2 * HOPS):
                low(w)
                if w in (1, 5, 7):
                    sqrt(var, k)
                    k += 1

            def s2t_low(b, q):
                sc.wait_ge(s2t_mm, b + 1)
                sc.activation(ylo[:, bass.ds(b, 1), :].rearrange("p a c -> p (a c)"), ps[:, q, DIM:2 * DIM], ACT.Copy, scale=1.0 / SCALE)
                sc.activation(cnt_d[:, bass.ds(b, 1)], ps[:, q, 2 * DIM:2 * DIM + 1], ACT.Copy).then_inc(s2t_lo, 1)
            with sc.Fori(0, BLOCKS // 2) as i:
                for q in range(2):
                    s2t_low(i * 2 + q, q)
            s2t_low(BLOCKS - 1, 0)
            product_copies(1, LANES)
            sqrt(var, k)

        @block.tensor
        def _(pe):
            for k in range(COLS // HIST):
                q = k % 2
                pe.wait_ge(hist_ready, 2 * k + 2)
                for t in range(HIST):
                    m = pe.matmul(ps[0:BLOCKS, 0, 0:BLOCKS], oh_d[:, q, t, :], oh_s[:, q, t, :], start=(k == 0 and t == 0), stop=(k == COLS // HIST - 1 and t == HIST - 1))
                m.then_inc(hist_used, 1)
            pe.wait_ge(tab_v, 1)
            pe.matmul(ps[0:BLOCKS, 1, 0:3], upper[0:BLOCKS, 0:BLOCKS], bt[:, :], start=True, stop=True)
            pe.matmul(ps[0:1, 1, 8:9], ones[0:BLOCKS, 0:1], bt[:, 0:1], start=True, stop=True).then_inc(tab_pe, 1)
            pe.wait_ge(tab_v, 2)
            pe.matmul(ps[0:ROWS, 0, 0:BLOCKS], ones[0:BLOCKS, 0:ROWS], rs_diag[:, :], start=True, stop=True)
            quarter = SLOT_ROWS_UP // 4
            for k in range(4):
                m = pe.matmul(ps[:, 2 + k, 0:quarter], ones[0:BLOCKS, :], row_cmp[:, k * quarter:(k + 1) * quarter], start=True, stop=True)
            m.then_inc(tab_pe, 1)
            pe.wait_ge(tab_v, 3)
            for k in range(4):
                pe.matmul(ps[:, 2 + k, 0:quarter], ones[0:BLOCKS, :], row_cmp[:, k * quarter:(k + 1) * quarter], start=True, stop=True)
            pe.matmul(ps[:, 0, 0:CHUNKS], ones[0:BLOCKS, :], chunk_tmp[0:BLOCKS, :], start=True, stop=True)
            pe.matmul(ps[:, 1, 0:CHUNKS], base_m[:, :], chunk_oh[:, :], start=True, stop=True)
            pe.matmul(ps[:, 6, 0:CHUNKS], ones[0:BLOCKS, :], chunk_oh[:, :], start=True, stop=True).then_inc(tab_pe, 1)
            pe.wait_ge(tab_v, 4)

            def add_picked(s, q, bank, first, last, base):
                pe.wait_ge(pick_ready, s + base + 1)
                for k in range(4):
                    m = pe.matmul(ps[0:ROWS, bank + k, 0:COLS // 4], ident[0:ROWS, 0:ROWS], picked[:, q, k * (COLS // 4):(k + 1) * (COLS // 4)],
                                  start=first, stop=last, skip_group_check=True)
                m.then_inc(pick_used, 1)

            def add_all(bank, base):
                add_picked(0, 0, bank, True, False, base)
                with pe.Fori(0, BLOCKS // 2 - 1) as i:
                    for q in range(2):
                        add_picked(i * 2 + q + 1, (q + 1) % 2, bank, False, False, base)
                add_picked(BLOCKS - 2, 1, bank, False, False, base)
                add_picked(BLOCKS - 1, 0, bank, False, True, base)

            add_all(0, 0)
            pe.wait_ge(rank_step, 3 * BLOCKS)
            pe.transpose(ps[0:BLOCKS, 4, 0:ROWS], row_last[:, :], ident[0:ROWS, 0:ROWS])
            pe.matmul(ps[0:BLOCKS, 5, 0:ROWS], ones[0:ROWS, 0:BLOCKS], nb_diag[:, :], start=True, stop=True).then_inc(tab_pe, 1)
            pe.wait_ge(tab_v, 5)
            pe.transpose(ps[0:ROWS, 4, 0:BLOCKS], carry_t[:, 0:ROWS], ident[0:BLOCKS, 0:BLOCKS]).then_inc(tab_pe, 1)
            pe.wait_ge(tab_v, 6)
            add_all(4, BLOCKS)
            add_all(0, 2 * BLOCKS)

            pe.wait_ge(ranked, 2)
            pe.wait_ge(x_in, 48)
            pe.wait_ge(consts_in, 16 * 9)
            for q in range(BLOCKS // 4 + 1):
                if q >= 2:
                    pe.wait_ge(proj_act, q - 1)
                for b in range(4 * q, min(4 * q + 4, BLOCKS)):
                    m = pe.matmul(ps[:, q % 2, (b - 4 * q) * 2 * DIM:(b - 4 * q + 1) * 2 * DIM], xt[:, b * LANES:(b + 1) * LANES], w_node[:, :], start=True, stop=True)
                m.then_inc(proj_pe, 1)
            pe.wait_ge(proj_act, BLOCKS // 4 + 1)

            def edge_group(i, first):
                for u in range(RING):
                    g = RING * i + u
                    q = u % 2
                    pe.wait_ge(kf_in[u], 16 * (i + 1))
                    pe.wait_ge(qf_in[u], 16 * (i + 1))
                    if not (first and u < 2):
                        pe.wait_ge(edge_v_done, g - 1)
                        pe.wait_ge(msg_ready, g - 1)
                    for t in range(TILES):
                        h, c = t // (TILES // 2), t % (TILES // 2)
                        o = ps[0:ROWS, 4 * q + t // 2, (t % 2) * 3 * DIM:(t % 2 + 1) * 3 * DIM]
                        pe.matmul(o[:, 0:2 * DIM], kf[h * DIM:(h + 1) * DIM, u, c * ROWS:(c + 1) * ROWS], w_edge[h * DIM:(h + 1) * DIM, :], start=True, stop=True)
                        m = pe.matmul(o[:, 2 * DIM:3 * DIM], qf[:, u, t * ROWS:(t + 1) * ROWS], wq[:, :], start=True, stop=True)
                    m.then_inc(edge_mm, 1)
            edge_group(0, True)
            with pe.Fori(1, GROUPS // RING) as i:
                edge_group(i, False)

            for k in range(2):
                pe.wait_ge(line_v, 2 * k + 1)
                pe.transpose(ps[0:1, 0, 0:ROWS], edge_v[:, 0:1], ident[0:ROWS, 0:ROWS])
                pe.transpose(ps[0:1, 1, 0:ROWS], edge_v[:, 1:2], ident[0:ROWS, 0:ROWS]).then_inc(line_pe, 1)
                pe.wait_ge(line_v, 2 * k + 2)
                pe.transpose(ps[0:ROWS, 2, 0:1], line_c[:, k:k + ROWS], ident[0:1, 0:1]).then_inc(line_pe, 1)

            def agg_chunk(i, u, first):
                r = RING * i + u
                q = u % 2
                if not (first and u < 2):
                    pe.wait_ge(agg_added, r - 1)
                pe.wait_ge(woh_ready, (r + 1) * PER_LANE)
                for j in range(PER_LANE):
                    m = pe.matmul(ps[:, q, 0:MSGW], woh[:, q, j, :], mch[:, u, j * MSGW:(j + 1) * MSGW], start=(j == 0), stop=(j == PER_LANE - 1))
                m.then_inc(agg_mm, 1)
            for u in range(RING):
                agg_chunk(0, u, True)
            with pe.Fori(1, CHUNKS // RING) as i:
                for u in range(RING):
                    agg_chunk(i, u, False)

            def node_product(k, part, w_t):
                pe.wait_ge(nt_ready, k + 1)
                for q in range(13):
                    n = min(4, BLOCKS - 4 * q)
                    if q >= 2:
                        pe.wait_ge(nt_copied, 13 * k + q - 1)
                    for b in range(n):
                        m = pe.transpose(ps[0:part, 2 + q % 2, b * LANES:(b + 1) * LANES], Z[:, 4 * q + b, 0:part], ident[:, :])
                    m.then_inc(nt_t, 1)
                    pe.wait_ge(nt_copied, 13 * k + q + 1)
                    if q >= 2:
                        pe.wait_ge(nt_out, 13 * k + q - 1)
                    for b in range(n):
                        m = pe.matmul(ps[:, 4 + q % 2, b * DIM:(b + 1) * DIM], zt[0:part, q % 2, b * LANES:(b + 1) * LANES], w_t, start=True, stop=True)
                    m.then_inc(nt_mm, 1)
            node_product(0, DIM, wo[:, :])

            pe.nop().then_inc(tile_mm, JOB_CREDIT)
            pe.nop().then_inc(tile_copied, JOB_CREDIT)
            pe.wait_ge(nt_out, 13)
            pe.wait_ge(tab_v, TAB_V + 2)
            pe.wait_ge(build_start, 1)
            rows = pe.value_load(n_rows[0:1, 0:1], min_val=1, max_val=SLOT_ROWS)
            with pe.Fori(0, ROW_LOOPS) as o:
                with pe.If(o * ROW_LOOP < rows):
                    with pe.Fori(0, ROW_LOOP // 2) as j:
                        for u in range(2):
                            r = o * ROW_LOOP + j * 2 + u
                            with pe.If(r < rows):
                                pe.wait_ge(pay_conv, r + 1)
                                for g in range(BG):
                                    q = (BG * u + g) % 2
                                    pe.wait_ge(oh_ready, r * (BLOCKS * 2) + (g + 1) * BG * 2)
                                    for l in range(2):
                                        pe.wait_ge(tile_copied, r * (2 * BG) + 2 * g + l + 1)
                                        first_bank = 4 * q + 2 * l
                                        pe.matmul(ps[:, first_bank, :], keep_diag[:, u, :], cacc[:, l, g * BGW:g * BGW + 512],
                                                  start=True, stop=False, skip_group_check=True)
                                        pe.matmul(ps[:, first_bank + 1, 0:BGW - 512], keep_diag[:, u, :], cacc[:, l, g * BGW + 512:(g + 1) * BGW],
                                                  start=True, stop=False, skip_group_check=True)
                                        for s in range(BG):
                                            m = pe.matmul(ps[:, first_bank + s // 4, (s % 4) * LANES:(s % 4 + 1) * LANES],
                                                          oh[:, q, s, 1 - l, :], oh[:, q, s, l, :],
                                                          start=False, stop=(s in (3, BG - 1)), skip_group_check=True)
                                        m.then_inc(tile_mm, 1)

            pe.nop().then_inc(big_used, 4)
            one_hop_sems = (xs_ready, sweep_read)

            def hop_sweeps(hop, degrees):
                pe.wait_ge(xs_ready, hop + 1)
                for h in range(2):
                    w = hop * 2 + h
                    n = (HALF, BLOCKS - HALF)[h]
                    pe.wait_ge(sweep_read, w + 1)

                    def block(b, u, first):
                        for s in range(n):
                            m = pe.matmul(ps[:, s // 4, (s % 4) * LANES:(s % 4 + 1) * LANES], big[:, u, s * LANES:(s + 1) * LANES],
                                          xs[:, bass.ds(b, 1), 0:2 * DIM].rearrange("p a c -> p (a c)"),
                                          start=(first and s % 4 == 0), stop=False, skip_group_check=True)
                            if degrees:
                                m = pe.matmul(ps[:, 7, h * HALF + s:h * HALF + s + 1], big[:, u, s * LANES:(s + 1) * LANES], one16[:, :],
                                              start=(first and h == 0 and s == 0), stop=False, skip_group_check=True)
                        m.then_inc(big_used, 1)
                        return m
                    pe.wait_ge(big_in[4], (w + 1) * 16)
                    block(0, 4, True)
                    with pe.Fori(0, (BLOCKS - 1) // 4) as i:
                        for u in range(4):
                            pe.wait_ge(big_in[u], (w * ((BLOCKS - 1) // 4) + i + 1) * 16)
                            block(i * 4 + u + 1, u, False)
                    pe.wait_ge(big_used, (w + 1) * BLOCKS + 4)
                    pe.nop().then_inc(sweep_mm, 1)

            pe.wait_ge(built, 1)
            hop_sweeps(0, True)
            with pe.Fori(1, HOPS) as hop:
                hop_sweeps(hop, False)

            pe.wait_ge(sweep_read, 2 * HOPS + 1)

            def s2t(b, slot, q, use):
                pe.wait_ge(bigs_in[slot], use * 16)
                pe.wait_ge(s2t_read, b + 1)
                for s in range(BLOCKS):
                    m = pe.matmul(ps[:, q, 0:2 * DIM + 1], bigs[slot][:, s * LANES:(s + 1) * LANES], xs[:, s, :],
                                  start=(s == 0), stop=(s == BLOCKS - 1))
                m.then_inc(s2t_mm, 1)
            with pe.Fori(0, BLOCKS // 6) as i:
                for u in range(6):
                    s2t(i * 6 + u, u % 3, u % 2, i * 2 + u // 3 + 1)
            s2t(BLOCKS - 1, 0, 0, BLOCKS // 3 + 1)
            node_product(1, LANES, wl[:, :])


def kernel(x, src, dst, edge_attr_64, edge_attr_64_n2, edge_attr_64_n3, L0_gnn_W_msg, L0_gnn_W_q, L0_gnn_W_k,
           L0_gnn_W_out, L0_gnn_gamma, L0_gnn_beta, L3_gnn_W1, L3_gnn_Wr, L3_gnn_br):
    import numpy as np
    import concourse.bacc as bacc
    from concourse.bass_utils import run_bass_kernel_spmd

    def plain(a):
        return np.ascontiguousarray(np.asarray(a))

    half = TILES // 2
    ek = np.asarray(edge_attr_64).reshape(ROWS, GROUPS, 2, half, DIM).transpose(1, 2, 4, 3, 0).reshape(GROUPS, 2 * DIM, half * ROWS)
    eq = np.concatenate([np.asarray(edge_attr_64_n2), np.asarray(edge_attr_64_n3)], axis=1)
    eq = eq.reshape(ROWS, GROUPS, TILES, 2 * DIM).transpose(1, 3, 2, 0).reshape(GROUPS, 2 * DIM, TILES * ROWS)
    arrays = {
        "x": plain(x), "x_t": plain(np.asarray(x).T), "src": plain(src), "dst": plain(dst),
        "edge_k": plain(ek), "edge_q": plain(eq),
        "w_in": plain(np.concatenate([np.asarray(L0_gnn_W_msg), np.asarray(L0_gnn_W_k)], axis=1)),
        "w_q": plain(L0_gnn_W_q), "w_out": plain(L0_gnn_W_out),
        "gamma": plain(L0_gnn_gamma).reshape(1, DIM), "beta": plain(L0_gnn_beta).reshape(1, DIM),
        "w_last": plain(np.concatenate([np.asarray(L3_gnn_Wr).T, np.asarray(L3_gnn_W1).T], axis=0)),
        "b_last": plain(L3_gnn_br).reshape(1, DIM),
    }
    nc = bacc.Bacc("TRN2", target_bir_lowering=False, num_devices=1)
    args = [nc.dram_tensor(f"in_{k}", a.shape, mybir.dt.from_np(a.dtype), kind="ExternalInput").ap() for k, a in arrays.items()]
    out = nc.dram_tensor("out_nodes", [NODES, DIM], F32, kind="ExternalOutput").ap()
    gnn_kernel(nc, *args, out)
    r = run_bass_kernel_spmd(nc, [{f"in_{k}": a for k, a in arrays.items()}], core_ids=[0])
    return r.results[0]["out_nodes"]
```

```python
import concourse.bass as bass
from concourse import mybir
from contextlib import ExitStack

F32, F16, I32 = mybir.dt.float32, mybir.dt.float16, mybir.dt.int32
ALU, ACT, AX = mybir.AluOpType, mybir.ActivationFunctionType, mybir.AxisListType

LANES = 128
NODES, EDGES, DIM = 6250, 200000, 64
BLOCKS = -(-NODES // LANES)
PADDED = BLOCKS * LANES
LAST = NODES - (BLOCKS - 1) * LANES
ROWS, COLS = 125, EDGES // 125
TILES = 8
GROUPS = COLS // TILES
RING = 4
CHUNK = 1024
PER_LANE = CHUNK // LANES
CHUNKS = EDGES // CHUNK + BLOCKS
SLOT_ROWS = EDGES // LANES + BLOCKS
ROW_LOOP = 32
ROW_LOOPS = -(-SLOT_ROWS // ROW_LOOP)
SLOT_ROWS_UP = ROW_LOOPS * ROW_LOOP
FILLS = 96
FILL_COLS = SLOT_ROWS_UP * PADDED * 2 // LANES // FILLS
HIST = 32
DEAL = -(-COLS // LANES)
DEAL_REST = COLS - (DEAL - 1) * LANES
DEAL_RING = 5
PICKS = 3
BG = 7
BGW = BG * LANES
HALF = (BLOCKS + 1) // 2
NEG = -1.0e30
SCALE = 4096.0
HOPS = 5
MSGW = DIM + 1


def gnn_kernel(nc, x, x_t, src, dst, edge_k, edge_q, w_in, w_q, w_out, gamma, beta, w_last, b_last, out):
    table = nc.dram_tensor("node_projections", [PADDED, 2 * DIM], F32, kind="Internal").ap()
    msgs = nc.dram_tensor("messages", [EDGES + CHUNK, MSGW], F32, kind="Internal").ap()
    edge_ed = nc.dram_tensor("edge_exp_dst", [EDGES + CHUNK, 2], F32, kind="Internal").ap()
    slots = nc.dram_tensor("edge_slots", [SLOT_ROWS_UP * PADDED, 2], F16, kind="Internal").ap()
    dst_major = nc.dram_tensor("counts_dst_major", [BLOCKS, LANES, PADDED], F16, kind="Internal").ap()
    src_major = nc.dram_tensor("counts_src_major", [BLOCKS, LANES, PADDED], F16, kind="Internal").ap()

    ctx = ExitStack()
    with ctx:
        def sem(name):
            return ctx.enter_context(nc.semaphore(name))

        def allocator(stack):
            return lambda name, shape, dt: stack.enter_context(nc.sbuf_tensor(name, shape, dt))

        sb = allocator(ctx)
        X = sb("X", [LANES, BLOCKS, DIM], F32)
        mem_a = sb("mem_a", [LANES, 2 * COLS], F32)
        mem_b = sb("mem_b", [LANES, COLS + DEAL * ROWS], F32)
        exp_dst = mem_a[0:ROWS, :].rearrange("p (t k) -> p t k", k=2)
        src_i = mem_b[0:ROWS, 0:COLS].bitcast(I32)
        slot_t = mem_b[:, COLS:COLS + DEAL * ROWS].bitcast(I32).rearrange("p (c r) -> p c r", c=DEAL)
        xs = mem_a[:, :].bitcast(F16)[:, 0:BLOCKS * (2 * DIM + 1)].rearrange("p (b c) -> p b c", b=BLOCKS)
        total = mem_b[:, 0:BLOCKS * DIM].rearrange("p (b c) -> p b c", b=BLOCKS)
        mem_c = sb("mem_c", [LANES, 2 * COLS + 2], F32)
        pen = mem_c[0:ROWS, 0:COLS + 1]
        att = mem_c[0:ROWS, COLS + 1:2 * COLS + 1]
        lanes_t = sb("lanes_t", [LANES, DEAL, ROWS, 2], F16)
        iota = sb("iota", [LANES, LANES], F32)
        iota16 = sb("iota16", [LANES, LANES], F16)
        lane_no = sb("lane_no", [LANES, 1], F32)
        ident = sb("ident", [LANES, LANES], F32)
        ident16 = sb("ident16", [LANES, LANES], F16)
        ones = sb("ones", [LANES, LANES], F32)
        w_node = sb("w_node", [DIM, 2 * DIM], F32)
        w_edge = sb("w_edge", [LANES, 2 * DIM], F32)
        wq = sb("wq", [2 * DIM, DIM], F32)
        wo = sb("wo", [DIM, DIM], F32)
        wl = sb("wl", [2 * DIM, DIM], F32)
        gam = sb("gam", [LANES, DIM], F32)
        bet = sb("bet", [LANES, DIM], F32)
        bl = sb("bl", [LANES, DIM], F32)
        keep_row = sb("keep_row", [LANES, SLOT_ROWS_UP], F32)
        row_tab = sb("row_tab", [LANES // 2, SLOT_ROWS_UP], I32)
        block_of_row, landed_need = row_tab[0:1, :], row_tab[32:33, :]
        n_rows = sb("n_rows", [1, 1], I32)
        chunk_first = sb("chunk_first", [LANES, CHUNKS], F32)
        chunk_block = sb("chunk_block", [1, CHUNKS], I32)
        chunk_base = sb("chunk_base", [1, CHUNKS], I32)
        gidx = sb("gidx", [ROWS, RING, TILES], I32)
        sidx = sb("sidx", [LANES, DEAL_RING, DEAL], I32)
        spay = sb("spay", [LANES, DEAL_RING, DEAL, 2], F16)
        mean = sb("mean", [LANES, BLOCKS], F32)
        var = sb("var", [LANES, BLOCKS], F32)
        deg_inv = sb("deg_inv", [LANES, BLOCKS], F32)
        deg_rsq = sb("deg_rsq", [LANES, BLOCKS], F32)
        has = sb("has", [LANES, BLOCKS], F32)

        ph = ExitStack()
        sb = allocator(ph)
        dblk = sb("dblk", [ROWS, COLS], F16)
        sblk = sb("sblk", [ROWS, COLS], F16)
        keep_b = sb("keep_b", [ROWS, COLS], F32)
        ind = sb("ind", [ROWS, COLS], F32)
        cnt = sb("cnt", [ROWS, COLS], F32)
        picked = sb("picked", [ROWS, PICKS, COLS], F32)
        dst_i, prev_i = ind[:, :].bitcast(I32), cnt[:, :].bitcast(I32)
        ta, tb, tc = picked[:, 0, :], picked[:, 1, :], picked[:, 2, :]
        seg_f, seg_m = ta, tb
        next_i = sb("next_i", [ROWS, 1], I32)
        next_f = sb("next_f", [ROWS, 1], F32)
        oh_mem = sb("oh_mem", [ROWS, 4 * HIST * BLOCKS], F16)
        oh_d, oh_s = (oh_mem[:, k * 2 * HIST * BLOCKS:(k + 1) * 2 * HIST * BLOCKS].rearrange("p (q t b) -> p q t b", q=2, t=HIST) for k in range(2))
        cmp_mem = oh_mem[:, :].bitcast(F32)
        row_cmp = cmp_mem[0:BLOCKS, 0:SLOT_ROWS_UP]
        chunk_tmp = cmp_mem[0:BLOCKS, SLOT_ROWS_UP:SLOT_ROWS_UP + CHUNKS]
        chunk_oh = cmp_mem[0:BLOCKS, SLOT_ROWS_UP + CHUNKS:SLOT_ROWS_UP + 2 * CHUNKS]
        minus1 = sb("minus1", [LANES, FILL_COLS], F16)
        row_last = sb("row_last", [ROWS, BLOCKS], F32)
        row_last_t = sb("row_last_t", [BLOCKS, ROWS], F32)
        no_break = sb("no_break", [ROWS, 1], F32)
        nb_diag = sb("nb_diag", [ROWS, ROWS], F32)
        nb_t = sb("nb_t", [BLOCKS, ROWS], F32)
        carry_t = sb("carry_t", [BLOCKS, ROWS + 1], F32)
        carry = sb("carry", [ROWS, BLOCKS], F32)
        upper = sb("upper", [LANES, LANES], F32)
        bt = sb("bt", [BLOCKS, 3], F32)
        bti = sb("bti", [BLOCKS, 3], I32)
        bend = sb("bend", [BLOCKS, 3], F32)
        bstart = sb("bstart", [BLOCKS, 3], F32)
        base_v = sb("base_v", [BLOCKS, 1], F32)
        base_m = sb("base_m", [BLOCKS, LANES], F32)
        need_v = sb("need_v", [BLOCKS, 1], F32)
        rs_diag = sb("rs_diag", [BLOCKS, BLOCKS], F32)
        row_start = sb("row_start", [ROWS, BLOCKS], F32)
        row_no = sb("row_no", [LANES, SLOT_ROWS_UP], F32)
        need_m = sb("need_m", [BLOCKS, LANES // 2], F32)
        zpad = lanes_t[:, :, :, :].rearrange("p c r k -> p (c r k)").bitcast(F32)[:, 0:PER_LANE * MSGW]
        edpad = sb("edpad", [LANES, PER_LANE, 2], F32)
        feats = sb("feats", [LANES, PADDED], F32)
        xt = feats[0:DIM, :]
        kf = feats[:, 0:RING * TILES // 2 * ROWS].rearrange("p (u c) -> p u c", u=RING)
        qf = feats[:, RING * TILES // 2 * ROWS:RING * TILES // 2 * ROWS * 3].rearrange("p (u c) -> p u c", u=RING)
        rows_mem = sb("rows_mem", [LANES, BLOCKS * 2 * DIM], F32)
        proj = rows_mem[:, :].rearrange("p (b c) -> p b c", b=BLOCKS)
        GAT, KK = RING * TILES * 2 * DIM, 2 * TILES * DIM
        gat = rows_mem[0:ROWS, 0:GAT].rearrange("p (u t c) -> p u t c", u=RING, t=TILES)
        kk = rows_mem[0:ROWS, GAT:GAT + KK].rearrange("p (u t c) -> p u t c", u=2, t=TILES)
        mm = rows_mem[0:ROWS, GAT + KK:GAT + 2 * KK].rearrange("p (u t c) -> p u t c", u=2, t=TILES)
        msgb = sb("msgb", [ROWS, RING, TILES, MSGW], F32)
        line = sb("line", [1, 2, ROWS], F32)
        line_c = sb("line_c", [1, ROWS + 1], F32)
        edge_v = sb("edge_v", [ROWS, 2], F32)
        edge_in = sb("edge_in", [ROWS, 1], F32)
        ph.close()

        sb = allocator(ctx)
        Y = sb("Y", [LANES, BLOCKS, DIM], F32)
        W = sb("W", [LANES, BLOCKS, DIM], F32)
        ylo = sb("ylo", [LANES, BLOCKS, DIM], F32)
        Z = sb("Z", [LANES, BLOCKS, 2 * DIM], F32)
        zt = sb("zt", [LANES, 2, 4 * LANES], F32)

        ph = ExitStack()
        sb = allocator(ph)
        mch = sb("mch", [LANES, RING, PER_LANE * MSGW], F32)
        ech = sb("ech", [LANES, RING, PER_LANE, 2], F32)
        rel = sb("rel", [LANES, RING, PER_LANE], F32)
        woh = sb("woh", [LANES, 2, PER_LANE, LANES], F32)
        agg = sb("agg", [LANES, BLOCKS + 1, MSGW], F32)
        pay = sb("pay", [LANES, 2, BLOCKS, 2], F16)
        payf = sb("payf", [LANES, 2, BLOCKS, 2], F32)
        keep_diag = sb("keep_diag", [LANES, 2, LANES], F16)
        oh = sb("oh", [LANES, 2, BG, 2, LANES], F16)
        cacc = sb("cacc", [LANES, 2, PADDED], F16)
        den = sb("den", [LANES, BLOCKS], F32)
        ph.close()

        ph = ExitStack()
        sb = allocator(ph)
        big = sb("big", [LANES, 5, HALF * LANES], F16)
        bigs = [sb(f"bigs{i}", [LANES, PADDED], F16) for i in range(2)] + [mem_c[:, :].bitcast(F16)[:, 0:PADDED]]
        one16 = sb("one16", [LANES, 1], F16)
        cnt_d = sb("cnt_d", [LANES, BLOCKS], F32)
        ph.close()

        ps = ctx.enter_context(nc.psum_tensor("ps", [LANES, 8, 512], F32))

        edges_in, consts_in, x_in, filled = sem("edges_in"), sem("consts_in"), sem("x_in"), sem("filled")
        pool_consts, vec_consts, vec = sem("pool_consts"), sem("vec_consts"), sem("vec")
        hist_ready, hist_used = sem("hist_ready"), sem("hist_used")
        tab_v, tab_pe = sem("tab_v"), sem("tab_pe")
        pick_ready, pick_used = sem("pick_ready"), sem("pick_used")
        rank_step = sem("rank_step")
        ranked = sem("ranked")
        proj_pe, proj_act, table_out = sem("proj_pe"), sem("proj_act"), sem("table_out")
        kf_in = [sem(f"kf_in{u}") for u in range(RING)]
        qf_in = [sem(f"qf_in{u}") for u in range(RING)]
        gat_in = [sem(f"gat_in{u}") for u in range(RING)]
        msg_out = [sem(f"msg_out{u}") for u in range(RING)]
        gidx_ready, edge_mm, edge_v_done, msg_ready, edge_step = (
            sem("gidx_ready"), sem("edge_mm"), sem("edge_v_done"), sem("msg_ready"), sem("edge_step"))
        line_v, line_pe = sem("line_v"), sem("line_pe")
        exp_in, exp_done, ed_out = sem("exp_in"), sem("exp_done"), sem("ed_out")
        sidx_ready = sem("sidx_ready")
        dealt = [sem(f"dealt{u}") for u in range(DEAL_RING)]
        turn_v, turn_pe, landed = sem("turn_v"), sem("turn_pe"), sem("landed")
        chunk_in = [sem(f"chunk_in{u}") for u in range(RING)]
        agg_rel, woh_ready, agg_mm, agg_added = sem("agg_rel"), sem("woh_ready"), sem("agg_mm"), sem("agg_added")
        nt_ready, nt_t, nt_copied, nt_mm, nt_out = (
            sem("nt_ready"), sem("nt_t"), sem("nt_copied"), sem("nt_mm"), sem("nt_out"))
        pay_in = [sem(f"pay_in{u}") for u in range(2)]
        pay_read, pay_conv, oh_ready, tile_mm, tile_copied = (
            sem("pay_read"), sem("pay_conv"), sem("oh_ready"), sem("tile_mm"), sem("tile_copied"))
        counts_out = [sem(f"counts_out{g}") for g in range(BG)]
        built = sem("built")
        big_in = [sem(f"big_in{u}") for u in range(5)]
        big_used, xs_ready, sweep_mm, lo_copied, sweep_read = (
            sem("big_used"), sem("xs_ready"), sem("sweep_mm"), sem("lo_copied"), sem("sweep_read"))
        bigs_in = [sem(f"bigs_in{u}") for u in range(3)]
        s2t_mm, s2t_lo, s2t_read = sem("s2t_mm"), sem("s2t_lo"), sem("s2t_read")
        act_v, act_done = sem("act_v"), sem("act_done")
        stored = sem("stored")

        TAB_V = 8
        STEPS = 3
        ITERS = GROUPS // RING
        RANK_ITERS = BLOCKS // STEPS
        HIST_STEPS = COLS // HIST
        HIST_AT = RANK_ITERS + 1
        CARRY_AT = HIST_AT + HIST_STEPS // RING + 1
        LOOK = 2 * STEPS
        START_AT = CARRY_AT + BLOCKS // LOOK + 1
        REST_AT = START_AT + BLOCKS // LOOK
        assert REST_AT <= ITERS and BLOCKS % STEPS == 1 and BLOCKS % LOOK == 1 and HIST_STEPS % RING == 2
        JOB_CREDIT = 4
        block = ctx.enter_context(nc.Block())

        dst_rows = dst.rearrange("(p t) -> p t", t=COLS)
        src_rows = src.rearrange("(p t) -> p t", t=COLS)
        msg_rows = msgs[0:EDGES, :].rearrange("(p t) c -> p t c", t=COLS)
        fill_view = slots.rearrange("(f p c) k -> f p (c k)", f=FILLS, p=LANES)

        @block.sync
        def _(sp):
            sp.dma_start(src_i[:, :], src_rows).then_inc(edges_in, 16)
            sp.dma_start(dst_i[:, :], dst_rows).then_inc(edges_in, 16)
            sp.wait_ge(vec_consts, 3)
            sp.dma_start(prev_i[1:ROWS, :], dst[COLS - 1:EDGES - 1].rearrange("(p t) -> p t", t=COLS)).then_inc(edges_in, 16)
            sp.dma_start(prev_i[0:1, 1:COLS], dst_rows[0:1, 0:COLS - 1]).then_inc(edges_in, 16)
            sp.dma_start(next_i[0:ROWS - 1, :], dst_rows[1:ROWS, 0:1], allow_slow_non_contiguous=True).then_inc(edges_in, 16)
            for t, a in ((w_node[:, :], w_in[0:DIM, :]), (w_edge[0:DIM, :], w_in[DIM:2 * DIM, :]),
                         (w_edge[DIM:2 * DIM, :], w_in[DIM:2 * DIM, :]), (wq[:, :], w_q), (wo[:, :], w_out),
                         (wl[:, :], w_last), (gam[:, :], gamma.to_broadcast([LANES, DIM])),
                         (bet[:, :], beta.to_broadcast([LANES, DIM])), (bl[:, :], b_last.to_broadcast([LANES, DIM]))):
                sp.dma_start(t, a).then_inc(consts_in, 16)
            sp.wait_ge(vec_consts, 7)
            sp.dma_start(xt[:, 0:NODES], x_t).then_inc(x_in, 16)
            sp.dma_start(X[:, 0:BLOCKS - 1, :], x[0:(BLOCKS - 1) * LANES, :].rearrange("(b p) f -> p b f", p=LANES)).then_inc(x_in, 16)
            sp.dma_start(X[0:LAST, BLOCKS - 1, :], x[(BLOCKS - 1) * LANES:NODES, :]).then_inc(x_in, 16)

            def load_features(i, first):
                for u in range(RING):
                    g = RING * i + u
                    if not first:
                        sp.wait_ge(edge_mm, (g - RING + 1) * 2)
                    sp.dma_start(kf[:, u, :], edge_k[bass.ds(g, 1), :, :].rearrange("a p c -> (a p) c")).then_inc(kf_in[u], 16)
                    sp.dma_start(qf[:, u, :], edge_q[bass.ds(g, 1), :, :].rearrange("a p c -> (a p) c")).then_inc(qf_in[u], 16)

            sp.wait_ge(proj_act, BLOCKS // 4 + 1)
            sp.dma_start(table.rearrange("(b p) f -> p b f", p=LANES), proj[:, :, :]).then_inc(table_out, 16)
            load_features(0, True)
            for f in range(FILLS):
                sp.dma_start(fill_view[f], minus1[:, :]).then_inc(filled, 16)
            sp.dma_start(msgs[EDGES:EDGES + CHUNK, :].rearrange("(p j) c -> p (j c)", j=PER_LANE), zpad).then_inc(filled, 16)
            sp.dma_start(edge_ed[EDGES:EDGES + CHUNK, :].rearrange("(p j) c -> p j c", j=PER_LANE), edpad[:, :, :]).then_inc(filled, 16)
            with sp.Fori(1, GROUPS // RING) as i:
                load_features(i, False)

            sp.wait_ge(exp_done, 2)
            sp.dma_start(edge_ed[0:EDGES, :].rearrange("(p t) c -> p t c", t=COLS), exp_dst[:, :, :]).then_inc(ed_out, 16)
            sp.wait_ge(ed_out, 16)
            for u in range(RING):
                sp.wait_ge(msg_out[u], 16 * (GROUPS // RING))

            def load_chunks(i, first):
                for u in range(RING):
                    r = RING * i + u
                    base = sp.value_load(chunk_base[0:1, bass.ds(r, 1)], min_val=0, max_val=EDGES)
                    if not first:
                        sp.wait_ge(agg_mm, r - RING + 1)
                    sp.dma_start(mch[:, u, :], msgs[bass.ds(base, CHUNK), :].rearrange("(p j) c -> p (j c)", j=PER_LANE)).then_inc(chunk_in[u], 16)
                    sp.dma_start(ech[:, u, :, :].rearrange("p j c -> p (j c)"),
                                 edge_ed[bass.ds(base, CHUNK), :].rearrange("(p j) c -> p (j c)", j=PER_LANE)).then_inc(chunk_in[u], 16)

            load_chunks(0, True)
            with sp.Fori(1, CHUNKS // RING) as i:
                load_chunks(i, False)

            rows = sp.value_load(n_rows[0:1, 0:1], min_val=1, max_val=SLOT_ROWS)
            with sp.Fori(0, ROW_LOOPS) as o:
                with sp.If(o * ROW_LOOP < rows):
                    with sp.Fori(0, ROW_LOOP // 2) as j:
                        for u in range(2):
                            r = o * ROW_LOOP + j * 2 + u
                            with sp.If(r < rows):
                                need = sp.value_load(landed_need[0:1, bass.ds(r, 1)], min_val=1, max_val=ROWS + 1)
                                sp.wait_ge(pay_read, r + 1)
                                sp.wait_ge(landed, need)
                                sp.dma_start(pay[:, u, :, :].rearrange("p s k -> p (s k)"),
                                             slots[bass.ds(r * PADDED, PADDED), :].rearrange("(p s) k -> p (s k)", s=BLOCKS)).then_inc(pay_in[u], 16)
            sp.wait_ge(built, 1)

            with sp.Fori(0, HOPS) as hop:
                for h in range(2):
                    wide = (HALF, BLOCKS - HALF)[h] * LANES
                    w = hop * 2 + h

                    def lot(b, u):
                        sp.wait_ge(big_used, w * BLOCKS + b + 1)
                        sp.dma_start(big[:, u, 0:wide], dst_major[bass.ds(b, 1), :, h * HALF * LANES:h * HALF * LANES + wide]
                                     .rearrange("a p c -> (a p) c")).then_inc(big_in[u], 16)
                    lot(0, 4)
                    with sp.Fori(0, (BLOCKS - 1) // 4) as i:
                        for u in range(4):
                            lot(i * 4 + u + 1, u)
            for b in range(3):
                sp.dma_start(bigs[b][:, :], src_major[b]).then_inc(bigs_in[b], 16)
            with sp.Fori(1, BLOCKS // 3) as i:
                for u in range(3):
                    b = i * 3 + u
                    sp.wait_ge(s2t_mm, b - 2)
                    sp.dma_start(bigs[u][:, :], src_major[bass.ds(b, 1), :, :].rearrange("a p c -> (a p) c")).then_inc(bigs_in[u], 16)
            sp.wait_ge(s2t_mm, BLOCKS - 3)
            sp.dma_start(bigs[0][:, :], src_major[BLOCKS - 1]).then_inc(bigs_in[0], 16)

            sp.wait_ge(act_done, 100)
            sp.dma_start(out[0:(BLOCKS - 1) * LANES, :].rearrange("(b p) f -> p b f", p=LANES), W[:, 0:BLOCKS - 1, :]).then_inc(stored, 16)
            sp.dma_start(out[(BLOCKS - 1) * LANES:NODES, :], W[0:LAST, BLOCKS - 1, :]).then_inc(stored, 16)
            sp.wait_ge(stored, 32)

        @block.gpsimd
        def _(gp):
            gp.iota(row_no[:, :], [[1, SLOT_ROWS_UP]], base=0, channel_multiplier=0, allow_small_or_imprecise_dtypes=True).then_inc(pool_consts, 1)
            gp.iota(lane_no[:, :], [[0, 1]], base=0, channel_multiplier=1, allow_small_or_imprecise_dtypes=True).then_inc(pool_consts, 1)

            last_node, last_slot = gp.to_reg(PADDED - 1), gp.to_reg(SLOT_ROWS_UP * PADDED - 1)

            def gather(i, first=False, last=False):
                for u in range(RING):
                    g, nu = RING * i + u, (u + 1) % RING
                    gp.wait_ge(gidx_ready, g + 1)
                    if not (last and nu == 0):
                        if not (first and nu):
                            gp.wait_ge(edge_v_done, (g + 1 - RING + 1) * 2)
                        gp.tensor_copy(gidx[:, nu, :], src_i[:, bass.ds((g + 1) * TILES, TILES)]).then_inc(gidx_ready, 1)
                    for j in range(TILES):
                        gp.indirect_dma_start(gat[:, u, j, :], None, table,
                                              bass.IndirectOffsetOnAxis(ap=gidx[:, u, j:j + 1], axis=0),
                                              bounds_check=last_node, oob_is_err=False).then_inc(gat_in[u], 16)

            gp.wait_ge(edges_in, 80)
            gp.tensor_copy(gidx[:, 0, :], src_i[:, 0:TILES]).then_inc(gidx_ready, 1)
            gp.wait_ge(table_out, 16)
            gather(0, first=True)
            with gp.Fori(1, GROUPS // RING - 1) as i:
                gather(i)
            gather(GROUPS // RING - 1, last=True)

            def copy_next(r, u):
                gp.tensor_copy(sidx[:, u, :], slot_t[:, :, bass.ds(r, 1)].rearrange("p c a -> p (c a)")).then_inc(sidx_ready, 1)
                gp.tensor_copy(spay[:, u, :, :], lanes_t[:, :, bass.ds(r, 1), :].rearrange("p c a k -> p (c a) k")).then_inc(sidx_ready, 1)

            def deal(i, first=False, last=False):
                for u in range(DEAL_RING):
                    r, nu = DEAL_RING * i + u, (u + 1) % DEAL_RING
                    gp.wait_ge(sidx_ready, 2 * r + 2)
                    if not (last and nu == 0):
                        if not (first and nu):
                            gp.wait_ge(dealt[nu], 16 * DEAL * (i + (nu == 0)))
                        copy_next(r + 1, nu)
                        if not (first and nu):
                            gp.nop().then_inc(landed, 1)
                    for c in range(DEAL):
                        m = LANES if c < DEAL - 1 else DEAL_REST
                        gp.indirect_dma_start(slots, bass.IndirectOffsetOnAxis(ap=sidx[0:m, u, c:c + 1], axis=0),
                                              spay[0:m, u, c, :], None,
                                              bounds_check=last_slot, oob_is_err=False).then_inc(dealt[u], 16)

            gp.nop().then_inc(landed, 1)
            gp.wait_ge(filled, 16 * (FILLS + 2))
            gp.wait_ge(ranked, 1)
            copy_next(0, 0)
            deal(0, first=True)
            with gp.Fori(1, ROWS // DEAL_RING - 1) as i:
                deal(i)
            deal(ROWS // DEAL_RING - 1, last=True)
            for u in range(DEAL_RING):
                gp.wait_ge(dealt[u], 16 * DEAL * (ROWS // DEAL_RING))
                gp.nop().then_inc(landed, 1)

        @block.vector
        def _(v):
            n = 0

            def step(ins):
                nonlocal n
                n += 1
                return ins.then_inc(vec, 1)

            def settled():
                v.wait_ge(vec, n)

            v.memset(prev_i[:, :], -1).then_inc(vec_consts, 1)
            v.memset(next_i[:, :], -1).then_inc(vec_consts, 1)
            v.memset(ones[:, :], 1.0).then_inc(vec_consts, 1)
            v.memset(X[:, :, :], 0.0).then_inc(vec_consts, 1)
            v.memset(xt[:, NODES:PADDED], 0.0).then_inc(vec_consts, 1)
            v.memset(minus1[:, :], -1.0).then_inc(vec_consts, 1)
            step(v.memset(edpad[:, :, 1:2], -1.0))
            step(v.memset(edpad[:, :, 0:1], 0.0))
            v.memset(lanes_t[:, :, :, :], 0.0).then_inc(vec_consts, 1)
            v.wait_ge(pool_consts, 2)
            step(v.tensor_copy(iota[:, :], row_no[:, 0:LANES]))
            step(v.tensor_copy(iota16[:, :], row_no[:, 0:LANES]))
            settled()
            step(v.tensor_scalar(ident[:, :], iota[:, :], lane_no[:, 0:1], None, ALU.is_equal))
            step(v.tensor_scalar(ident16[:, :], iota[:, :], lane_no[:, 0:1], None, ALU.is_equal))
            step(v.tensor_scalar(upper[:, :], iota[:, :], lane_no[:, 0:1], None, ALU.is_ge))
            v.wait_ge(edges_in, 80)
            step(v.tensor_scalar(ta.bitcast(I32), src_i, 7, None, ALU.logical_shift_right))
            step(v.tensor_scalar(tb.bitcast(I32), dst_i, 7, None, ALU.logical_shift_right))
            step(v.tensor_scalar(tc.bitcast(I32), prev_i, 7, None, ALU.arith_shift_right))
            step(v.tensor_copy(exp_dst[:, :, 1], dst_i))
            step(v.tensor_copy(next_f[:, :], next_i[:, :]))
            settled()
            step(v.tensor_copy(sblk[:, :], ta.bitcast(I32)))
            step(v.tensor_copy(dblk[:, :], tb.bitcast(I32)))
            step(v.tensor_copy(ind[:, :], tc.bitcast(I32)))
            settled()
            step(v.tensor_tensor(keep_b[:, :], dblk[:, :], ind[:, :], ALU.is_equal))
            step(v.tensor_copy(ta, prev_i))
            step(v.tensor_tensor(next_f[:, :], exp_dst[:, COLS - 1:COLS, 1], next_f[:, :], ALU.is_equal))
            settled()
            step(v.tensor_tensor(tb, exp_dst[:, :, 1], ta, ALU.is_equal))
            step(v.tensor_scalar(pen[:, COLS:COLS + 1], next_f[:, :], 1.0, -NEG, ALU.subtract, ALU.mult))
            settled()
            step(v.tensor_scalar(pen[:, 0:COLS], tb, 1.0, -NEG, ALU.subtract, ALU.mult))
            step(v.memset(slot_t.rearrange("p c r -> p (c r)"), 0))
            step(v.memset(msgb[:, :, :, DIM:MSGW], 1.0))
            settled()
            v.wait_ge(table_out, 16)

            def edge_group(i, u, first):
                g = RING * i + u
                q = u % 2
                for h in range(2):
                    e = g * 2 + h
                    pv = ps[0:ROWS, 4 + 2 * h:6 + 2 * h, 0:6 * DIM].rearrange("p k (t c) -> p k t c", t=2)
                    cols = slice(h * (TILES // 2), (h + 1) * (TILES // 2))
                    gv = gat[:, u, cols, :].rearrange("p (k t) c -> p k t c", t=2)
                    kv = kk[:, q, cols, :].rearrange("p (k t) c -> p k t c", t=2)
                    mv = mm[:, q, cols, :].rearrange("p (k t) c -> p k t c", t=2)
                    v.wait_ge(edge_mm, e + 1)
                    if h == 0:
                        v.wait_ge(gat_in[u], 16 * TILES * (i + 1))
                    v.tensor_tensor(kv, pv[:, :, :, DIM:2 * DIM], gv[:, :, :, DIM:2 * DIM], ALU.add).then_inc(edge_step, 1)
                    v.tensor_tensor(mv, pv[:, :, :, 0:DIM], gv[:, :, :, 0:DIM], ALU.add).then_inc(edge_step, 1)
                    v.wait_ge(edge_step, 5 * g + 2 * h + 2)
                    v.tensor_tensor(kv, kv, pv[:, :, :, 2 * DIM:3 * DIM], ALU.mult).then_inc(edge_v_done, 1)
                if not first:
                    v.wait_ge(msg_out[u], 16 * i)
                v.scalar_tensor_tensor(msgb[:, u, :, 0:DIM], mm[:, q, :, :], 0.01, mm[:, q, :, :], ALU.mult, ALU.max).then_inc(msg_ready, 1)
                v.wait_ge(edge_v_done, 2 * g + 2)
                v.tensor_reduce(att[:, bass.ds(g * TILES, TILES)], kk[:, q, :, :], AX.X, ALU.add).then_inc(edge_step, 1)

            def rank(s, q):
                v.tensor_scalar(ind[:, :], sblk[:, :], iota[0:ROWS, bass.ds(s, 1)], None, ALU.is_equal).then_inc(rank_step, 1)
                v.wait_ge(rank_step, 3 * s + 1)
                v.tensor_tensor_scan(cnt[:, :], keep_b[:, :], ind[:, :], 0.0, ALU.mult, ALU.add).then_inc(rank_step, 1)
                v.wait_ge(rank_step, 3 * s + 2)
                v.wait_ge(pick_used, s + 1)
                v.tensor_tensor(picked[:, q, :], ind[:, :], cnt[:, :], ALU.mult).then_inc(pick_ready, 1)
                v.tensor_copy(row_last[:, bass.ds(s, 1)], cnt[:, COLS - 1:COLS]).then_inc(rank_step, 1)
                v.wait_ge(rank_step, 3 * s + 3)
                v.wait_ge(pick_ready, s + 1)

            def look_up(values, keys, base, s, q):
                v.wait_ge(pick_used, base + s + 1)
                v.tensor_scalar(picked[:, q, :], keys[:, :], iota[0:ROWS, bass.ds(s, 1)], values[:, bass.ds(s, 1)],
                                ALU.is_equal, ALU.mult).then_inc(pick_ready, 1)

            def histogram(k, q):
                v.wait_ge(hist_used, k + 1)
                for blk, one_hot in ((dblk, oh_d), (sblk, oh_s)):
                    v.tensor_tensor(one_hot[:, q, :, :],
                                    blk[:, bass.ds(k * HIST, HIST)].unsqueeze(2).to_broadcast([ROWS, HIST, BLOCKS]),
                                    iota[0:ROWS, 0:BLOCKS].unsqueeze(1).to_broadcast([ROWS, HIST, BLOCKS]),
                                    ALU.is_equal).then_inc(hist_ready, 1)

            def rank_iter(i, first):
                for u in range(RING):
                    edge_group(i, u, first)
                    if u < STEPS:
                        rank(i * STEPS + u, u)

            rank_iter(0, True)
            with v.Fori(1, RANK_ITERS) as i:
                rank_iter(i, False)
            for u in range(RING):
                edge_group(RANK_ITERS, u, False)
                if u == 0:
                    rank(BLOCKS - 1, 0)
            v.wait_ge(pick_used, BLOCKS + PICKS)
            step(v.tensor_scalar(cnt[:, :].rearrange("p (k c) -> p k c", k=4), ps[0:ROWS, 0:4, 0:COLS // 4], -1.0, None, ALU.add))
            step(v.tensor_tensor_scan(picked[:, 0, :], keep_b[:, :], keep_b[:, :], 1.0, ALU.mult, ALU.mult))
            settled()
            step(v.tensor_copy(keep_b[:, :], picked[:, 0, :]))
            step(v.tensor_copy(no_break[:, :], picked[:, 0, COLS - 1:COLS]))
            settled()
            step(v.tensor_scalar(nb_diag[:, :], ident[0:ROWS, 0:ROWS], no_break[:, 0:1], None, ALU.mult))
            settled()
            v.nop().then_inc(tab_v, 1)
            v.wait_ge(tab_pe, 1)
            step(v.tensor_copy(row_last_t[:, :], ps[0:BLOCKS, 0, 0:ROWS]))
            step(v.tensor_copy(nb_t[:, :], ps[0:BLOCKS, 1, 0:ROWS]))
            step(v.memset(carry_t[:, 0:1], 0.0))
            settled()
            step(v.tensor_tensor_scan(carry_t[:, 1:ROWS + 1], nb_t[:, :], row_last_t[:, :], 0.0, ALU.mult, ALU.add))
            settled()
            v.nop().then_inc(tab_v, 1)
            v.wait_ge(tab_pe, 2)
            step(v.tensor_copy(carry[:, :], ps[0:ROWS, 2, 0:BLOCKS]))
            settled()

            with v.Fori(HIST_AT, HIST_AT + HIST_STEPS // RING) as i:
                for u in range(RING):
                    edge_group(i, u, False)
                    histogram((i - HIST_AT) * RING + u, u % 2)
            for u in range(RING):
                edge_group(CARRY_AT - 1, u, False)
                if u < 2:
                    histogram(HIST_STEPS - 2 + u, u)
            v.wait_ge(hist_used, HIST_STEPS + 2)
            hist = ps[0:BLOCKS, 0, 0:BLOCKS]
            step(v.tensor_reduce(bt[:, 0:1], hist, AX.X, ALU.max))
            settled()
            step(v.tensor_reduce(bt[:, 2:3], hist, AX.X, ALU.add))
            settled()
            step(v.tensor_scalar(bti[:, 0:1], bt[:, 0:1], float(LANES - 1), None, ALU.add))
            step(v.tensor_scalar(bti[:, 1:2], bt[:, 2:3], float(CHUNK - 1), None, ALU.add))
            settled()
            step(v.tensor_scalar(bti[:, 0:1], bti[:, 0:1], 7, None, ALU.logical_shift_right))
            step(v.tensor_scalar(bti[:, 1:2], bti[:, 1:2], 10, None, ALU.logical_shift_right))
            settled()
            step(v.tensor_scalar(bt[:, 0:1], bti[:, 0:1], 1.0, None, ALU.max))
            step(v.tensor_copy(bt[:, 1:2], bti[:, 1:2]))
            settled()
            v.nop().then_inc(tab_v, 1)
            v.wait_ge(tab_pe, 3)
            step(v.tensor_copy(bend[:, :], ps[0:BLOCKS, 1, 0:3]))
            step(v.tensor_copy(n_rows[:, :], ps[0:1, 1, 8:9]))
            settled()
            step(v.tensor_tensor(bstart[:, :], bend[:, :], bt[:, :], ALU.subtract))
            step(v.tensor_scalar(chunk_tmp[:, 0:ROWS], row_no[0:BLOCKS, 0:ROWS], float(COLS), bend[:, 2:3], ALU.mult, ALU.is_lt))
            settled()
            step(v.tensor_reduce(need_v[:, :], chunk_tmp[:, 0:ROWS], AX.X, ALU.add))
            step(v.tensor_scalar(rs_diag[:, :], ident[0:BLOCKS, 0:BLOCKS], bstart[:, 0:1], None, ALU.mult))
            step(v.scalar_tensor_tensor(base_v[:, :], bstart[:, 1:2], -float(CHUNK), bstart[:, 2:3], ALU.mult, ALU.add))
            step(v.tensor_scalar(row_cmp, row_no[0:BLOCKS, :], bend[:, 0:1], None, ALU.is_ge))
            settled()
            step(v.tensor_scalar(need_v[:, :], need_v[:, :], 1.0, None, ALU.add))
            step(v.tensor_scalar(base_v[:, :], base_v[:, :], -float(EDGES), None, ALU.add))
            settled()
            step(v.tensor_scalar(need_m[:, :], ones[0:BLOCKS, 0:LANES // 2], need_v[:, 0:1], None, ALU.mult))
            step(v.tensor_scalar(base_m[:, :], ones[0:BLOCKS, :], base_v[:, 0:1], None, ALU.mult))
            settled()
            v.nop().then_inc(tab_v, 1)
            v.wait_ge(tab_pe, 4)
            by4 = lambda t: t.rearrange("p (k c) -> p k c", k=4)
            step(v.tensor_copy(row_start[:, :], ps[0:ROWS, 0, 416:416 + BLOCKS]))
            step(v.tensor_copy(by4(block_of_row), ps[0:1, 0:4, 0:SLOT_ROWS_UP // 4]))
            step(v.tensor_scalar(row_cmp, row_no[0:BLOCKS, :], bstart[:, 0:1], None, ALU.is_equal))
            settled()
            v.nop().then_inc(tab_v, 1)
            v.wait_ge(tab_pe, 5)
            step(v.tensor_scalar(by4(keep_row[:, :]), ps[:, 0:4, 0:SLOT_ROWS_UP // 4], -1.0, 1.0, ALU.mult, ALU.add))
            step(v.tensor_scalar(row_cmp, row_no[0:BLOCKS, :], bend[:, 0:1], None, ALU.is_ge))
            settled()
            step(v.scalar_tensor_tensor(row_cmp, row_no[0:BLOCKS, :], bstart[:, 0:1], row_cmp, ALU.is_ge, ALU.subtract))
            settled()
            v.nop().then_inc(tab_v, 1)
            v.wait_ge(tab_pe, 6)
            step(v.tensor_copy(by4(landed_need), ps[32:33, 0:4, 0:SLOT_ROWS_UP // 4]))
            step(v.tensor_scalar(chunk_tmp, row_no[0:BLOCKS, 0:CHUNKS], bend[:, 1:2], None, ALU.is_ge))
            step(v.tensor_scalar(chunk_oh, row_no[0:BLOCKS, 0:CHUNKS], bstart[:, 1:2], None, ALU.is_ge))
            settled()
            step(v.tensor_tensor(chunk_oh, chunk_oh, chunk_tmp, ALU.subtract))
            settled()
            v.nop().then_inc(tab_v, 1)
            v.wait_ge(tab_pe, 7)
            step(v.tensor_scalar(chunk_first[:, :], ps[:, 0, 0:CHUNKS], float(LANES), None, ALU.mult))
            step(v.tensor_copy(chunk_block[:, :], ps[0:1, 0, 0:CHUNKS]))
            settled()
            step(v.scalar_tensor_tensor(chunk_tmp[0:1, :], row_no[0:1, 0:CHUNKS], float(CHUNK), ps[0:1, 2, 0:CHUNKS], ALU.mult, ALU.mult))
            settled()
            step(v.scalar_tensor_tensor(chunk_base[:, :], ps[0:1, 1, 0:CHUNKS], float(EDGES), chunk_tmp[0:1, :], ALU.add, ALU.add))
            settled()

            def look_iters(at, values, keys, base):
                with v.Fori(at, at + BLOCKS // LOOK) as i:
                    for u in range(RING):
                        edge_group(i, u, False)
                        if u < STEPS:
                            for k in range(2):
                                look_up(values, keys, base, (i - at) * LOOK + 2 * u + k, (2 * u + k) % PICKS)

            look_iters(CARRY_AT, carry, sblk, BLOCKS)
            for u in range(RING):
                edge_group(START_AT - 1, u, False)
                if u == 0:
                    look_up(carry, sblk, BLOCKS, BLOCKS - 1, 0)
            v.wait_ge(pick_used, 2 * BLOCKS + PICKS)
            step(v.tensor_tensor(by4(ind[:, :]), ps[0:ROWS, 0:4, 0:COLS // 4], by4(keep_b[:, :]), ALU.mult))
            settled()
            step(v.tensor_tensor(cnt[:, :], cnt[:, :], ind[:, :], ALU.add))
            settled()
            look_iters(START_AT, row_start, dblk, 2 * BLOCKS)
            look_up(row_start, dblk, 2 * BLOCKS, BLOCKS - 1, 0)
            v.wait_ge(pick_used, 3 * BLOCKS + PICKS)
            step(v.tensor_copy(ta.bitcast(I32), cnt[:, :]))
            settled()
            step(v.tensor_scalar(tb.bitcast(I32), ta.bitcast(I32), 7, None, ALU.logical_shift_right))
            settled()
            step(v.tensor_copy(tc, tb.bitcast(I32)))
            settled()
            step(v.scalar_tensor_tensor(ta, tc, -float(LANES), cnt[:, :], ALU.mult, ALU.add))
            step(v.tensor_tensor(by4(ind[:, :]), ps[0:ROWS, 0:4, 0:COLS // 4], by4(tc), ALU.add))
            settled()
            step(v.scalar_tensor_tensor(tb, ind[:, :], float(PADDED), sblk[:, :], ALU.mult, ALU.add))
            step(v.tensor_copy(cnt[:, :], src_i))
            settled()
            step(v.scalar_tensor_tensor(tc, ta, float(BLOCKS), tb, ALU.mult, ALU.add))
            step(v.scalar_tensor_tensor(ind[:, :], sblk[:, :], -float(LANES), cnt[:, :], ALU.mult, ALU.add))
            step(v.scalar_tensor_tensor(keep_b[:, :], dblk[:, :], -float(LANES), exp_dst[:, :, 1], ALU.mult, ALU.add))
            settled()
            v.nop().then_inc(turn_v, 1)
            turned = ps[:, 0:4, :].rearrange("p k (c w) -> p (k c) w", w=LANES)
            v.wait_ge(filled, 16 * (FILLS + 2))
            for k, t in enumerate((slot_t, lanes_t[:, :, :, 0], lanes_t[:, :, :, 1])):
                v.wait_ge(turn_pe, k + 1)
                step(v.tensor_copy(t[:, 0:DEAL - 1, :], turned[:, 0:DEAL - 1, 0:ROWS]))
                step(v.tensor_copy(t[0:DEAL_REST, DEAL - 1, :], turned[0:DEAL_REST, DEAL - 1, 0:ROWS]))
                settled()
                v.nop().then_inc(turn_v, 1)
            v.nop().then_inc(ranked, 1)
            with v.Fori(REST_AT, ITERS) as i:
                for u in range(RING):
                    edge_group(i, u, False)
            v.wait_ge(edge_step, 5 * GROUPS)
            v.wait_ge(msg_ready, GROUPS)
            step(v.tensor_scalar(att, att, float(DIM) ** -0.5, None, ALU.mult))
            settled()

            def passed_on(values, penalties, k, reverse):
                step(v.tensor_copy(edge_v[:, 0:1], values))
                step(v.tensor_reduce(edge_v[:, 1:2], penalties, AX.X, ALU.min))
                settled()
                v.nop().then_inc(line_v, 1)
                v.wait_ge(line_pe, 2 * k + 1)
                step(v.tensor_copy(line[:, :, :], ps[0:1, 0:2, 0:ROWS]))
                step(v.memset(line_c[:, :], NEG))
                settled()
                if reverse:
                    step(v.tensor_tensor_scan(line_c[:, 0:ROWS][:, ::-1], line[:, 1, :][:, ::-1], line[:, 0, :][:, ::-1], NEG, ALU.add, ALU.max))
                else:
                    step(v.tensor_tensor_scan(line_c[:, 1:ROWS + 1], line[:, 1, :], line[:, 0, :], NEG, ALU.add, ALU.max))
                settled()
                v.nop().then_inc(line_v, 1)
                v.wait_ge(line_pe, 2 * k + 2)
                step(v.tensor_copy(edge_in[:, :], ps[0:ROWS, 2, 0:1]))
                settled()

            step(v.tensor_tensor_scan(seg_f, pen[:, 0:COLS], att, NEG, ALU.add, ALU.max))
            settled()
            passed_on(seg_f[:, COLS - 1:COLS], pen[:, 0:COLS], 0, False)
            step(v.tensor_tensor_scan(seg_f, pen[:, 0:COLS], att, edge_in[:, 0:1], ALU.add, ALU.max))
            settled()
            step(v.tensor_tensor_scan(seg_m[:, ::-1], pen[:, 1:COLS + 1][:, ::-1], seg_f[:, ::-1], NEG, ALU.add, ALU.max))
            settled()
            passed_on(seg_m[:, 0:1], pen[:, 1:COLS + 1], 1, True)
            step(v.tensor_tensor_scan(seg_m[:, ::-1], pen[:, 1:COLS + 1][:, ::-1], seg_f[:, ::-1], edge_in[:, 0:1], ALU.add, ALU.max))
            settled()
            step(v.tensor_tensor(seg_f, att, seg_m, ALU.subtract))
            settled()
            v.nop().then_inc(exp_in, 1)
            v.wait_ge(exp_done, 1)

            step(v.memset(agg[:, :, :], 0.0))
            settled()

            def add_chunk(r):
                c = v.value_load(chunk_block[0:1, bass.ds(r, 1)], min_val=0, max_val=BLOCKS)
                v.wait_ge(agg_mm, r + 1)
                return c

            def agg_chunk(i, u, first):
                r = RING * i + u
                q = u % 2
                v.wait_ge(chunk_in[u], 32 * (i + 1))
                v.tensor_scalar(rel[:, u, :], ech[:, u, :, 1], chunk_first[:, bass.ds(r, 1)], None, ALU.subtract).then_inc(agg_rel, 1)
                v.wait_ge(agg_rel, r + 1)
                if not (first and u < 2):
                    v.wait_ge(agg_mm, r - 1)
                for j in range(PER_LANE):
                    v.tensor_scalar(woh[:, q, j, :], iota[:, :], rel[:, u, j:j + 1], ech[:, u, j, 0:1], ALU.is_equal, ALU.mult).then_inc(woh_ready, 1)
                if not (first and u == 0):
                    c = add_chunk(r - 1)
                    if not (first and u == 1):
                        v.wait_ge(agg_added, r - 1)
                    v.tensor_tensor(agg[:, bass.ds(c, 1), :].rearrange("p a c -> p (a c)"), agg[:, bass.ds(c, 1), :].rearrange("p a c -> p (a c)"),
                                    ps[:, (u + 1) % 2, 0:MSGW], ALU.add).then_inc(agg_added, 1)

            for u in range(RING):
                agg_chunk(0, u, True)
            with v.Fori(1, CHUNKS // RING) as i:
                for u in range(RING):
                    agg_chunk(i, u, False)
            c = add_chunk(CHUNKS - 1)
            v.wait_ge(agg_added, CHUNKS - 1)
            v.tensor_tensor(agg[:, bass.ds(c, 1), :].rearrange("p a c -> p (a c)"), agg[:, bass.ds(c, 1), :].rearrange("p a c -> p (a c)"),
                            ps[:, (CHUNKS - 1) % 2, 0:MSGW], ALU.add).then_inc(agg_added, 1)
            v.wait_ge(agg_added, CHUNKS)

            def over(a, w=DIM):
                return a.unsqueeze(2).to_broadcast([LANES, BLOCKS, w])

            def feat(a):
                return a.unsqueeze(1).to_broadcast([LANES, BLOCKS, DIM])

            a = 0

            def sqrt_of(t):
                nonlocal a
                settled()
                v.nop().then_inc(act_v, 1)
                a += 1
                v.wait_ge(act_done, a)

            def layer_norm(o, t, eps):
                step(v.tensor_reduce(mean[:, :], t[:, :, :], AX.X, ALU.add))
                settled()
                step(v.tensor_scalar(mean[:, :], mean[:, :], 1.0 / DIM, None, ALU.mult))
                settled()
                step(v.tensor_tensor(o[:, :, :], t[:, :, :], over(mean[:, :]), ALU.subtract))
                settled()
                step(v.tensor_tensor(ylo[:, :, :], o[:, :, :], o[:, :, :], ALU.mult))
                settled()
                step(v.tensor_reduce(var[:, :], ylo[:, :, :], AX.X, ALU.add))
                settled()
                step(v.tensor_scalar(var[:, :], var[:, :], 1.0 / DIM, eps, ALU.mult, ALU.add))
                sqrt_of(var)
                step(v.reciprocal(var[:, :], var[:, :]))
                settled()
                step(v.tensor_tensor(o[:, :, :], o[:, :, :], over(var[:, :]), ALU.mult))
                settled()

            def product_out(k, o, add):
                for q in range(13):
                    w = min(4, BLOCKS - 4 * q)
                    v.wait_ge(nt_mm, 13 * k + q + 1)
                    src_ps = ps[:, 4 + q % 2, 0:w * DIM].rearrange("p (b f) -> p b f", f=DIM)
                    v.tensor_copy(o[:, 4 * q:4 * q + w, :], src_ps).then_inc(nt_out, 1)
                v.wait_ge(nt_out, 13 * (k + 1))

            step(v.tensor_scalar(has[:, :], agg[:, 0:BLOCKS, DIM], 0.0, None, ALU.is_gt))
            step(v.tensor_scalar(den[:, :], agg[:, 0:BLOCKS, DIM], 1.0, None, ALU.max))
            settled()
            step(v.reciprocal(den[:, :], den[:, :]))
            settled()
            step(v.tensor_tensor(Z[:, :, 0:DIM], agg[:, 0:BLOCKS, 0:DIM], over(den[:, :]), ALU.mult))
            settled()
            v.nop().then_inc(nt_ready, 1)
            product_out(0, Y, None)
            step(v.scalar_tensor_tensor(Y[:, :, :], Y[:, :, :], 0.01, Y[:, :, :], ALU.mult, ALU.max))
            settled()
            step(v.tensor_tensor(Y[:, :, :], Y[:, :, :], X[:, :, :], ALU.add))
            settled()
            layer_norm(W, Y, 1e-6)
            step(v.tensor_tensor(W[:, :, :], W[:, :, :], feat(gam[:, :]), ALU.mult))
            settled()
            step(v.tensor_tensor(W[:, :, :], W[:, :, :], feat(bet[:, :]), ALU.add))
            settled()
            step(v.tensor_tensor(W[:, :, :], W[:, :, :], over(has[:, :]), ALU.mult))
            step(v.tensor_scalar(mean[:, :], has[:, :], -1.0, 1.0, ALU.mult, ALU.add))
            settled()
            step(v.tensor_tensor(Y[:, :, :], X[:, :, :], over(mean[:, :]), ALU.mult))
            settled()
            step(v.tensor_tensor(W[:, :, :], W[:, :, :], Y[:, :, :], ALU.add))
            settled()
            step(v.tensor_tensor(W[:, :, :], W[:, :, :], X[:, :, :], ALU.add))
            settled()
            layer_norm(X, W, 1e-5)

            step(v.memset(cacc[:, :, :], 0.0))
            settled()
            v.nop().then_inc(tab_v, 1)
            rows = v.value_load(n_rows[0:1, 0:1], min_val=1, max_val=SLOT_ROWS)
            v.nop().then_inc(pay_read, 2)
            with v.Fori(0, ROW_LOOPS) as o:
                with v.If(o * ROW_LOOP < rows):
                    with v.Fori(0, ROW_LOOP // 2) as j:
                        for u in range(2):
                            r = o * ROW_LOOP + j * 2 + u
                            with v.If(r < rows):
                                v.wait_ge(pay_in[u], (o * (ROW_LOOP // 2) + j + 1) * 16)
                                v.tensor_copy(payf[:, u, :, :], pay[:, u, :, :]).then_inc(pay_read, 1)
                                v.tensor_scalar(keep_diag[:, u, :], ident16[:, :], keep_row[:, bass.ds(r, 1)], None, ALU.mult).then_inc(pay_conv, 1)
                                v.wait_ge(pay_read, r + 3)
                                for g in range(BG):
                                    q = (BG * u + g) % 2
                                    v.wait_ge(tile_mm, r * (2 * BG) + 2 * g + 2)
                                    for s in range(BG):
                                        for k in range(2):
                                            ins = v.tensor_scalar(oh[:, q, s, k, :], iota16[:, :], payf[:, u, g * BG + s, k:k + 1], None, ALU.is_equal)
                                            ins.then_inc(oh_ready, 1)
            v.wait_ge(built, 1)

            step(v.memset(one16[:, :], 1.0))
            step(v.memset(xs[:, :, 2 * DIM:2 * DIM + 1], 1.0))
            settled()

            def split(t):
                step(v.tensor_scalar(xs[:, :, 0:DIM], t[:, :, :], SCALE, None, ALU.mult))
                settled()
                step(v.scalar_tensor_tensor(xs[:, :, DIM:2 * DIM], t[:, :, :], SCALE, xs[:, :, 0:DIM], ALU.mult, ALU.subtract))
                settled()
                v.nop().then_inc(xs_ready, 1)

            def sweep(w):
                h = w % 2
                b0, b1 = ((0, HALF), (HALF, BLOCKS))[h]
                v.wait_ge(lo_copied, w + 1)
                pv = ps[:, 0:7, :].rearrange("p k (b c) -> p (k b) c", c=LANES)[:, 0:b1 - b0, :]
                v.scalar_tensor_tensor(Y[:, b0:b1, :], pv[:, :, 0:DIM], 1.0 / SCALE, ylo[:, b0:b1, :], ALU.mult, ALU.add).then_inc(sweep_read, 1)

            v.nop().then_inc(sweep_read, 1)
            split(X)
            step(v.tensor_copy(total[:, :, :], X[:, :, :]))
            for hop in range(3):
                sweep(2 * hop)
                sweep(2 * hop + 1)
                v.wait_ge(sweep_read, 2 * hop + 3)
                if hop == 0:
                    step(v.tensor_scalar(has[:, :], ps[:, 7, 0:BLOCKS], 0.0, None, ALU.is_gt))
                    settled()
                    step(v.tensor_scalar(mean[:, :], ps[:, 7, 0:BLOCKS], 1.0, None, ALU.max))
                    settled()
                    step(v.reciprocal(cnt_d[:, :], mean[:, :]))
                    settled()
                    step(v.tensor_tensor(deg_inv[:, :], cnt_d[:, :], has[:, :], ALU.mult))
                    step(v.tensor_copy(var[:, :], cnt_d[:, :]))
                    sqrt_of(var)
                    step(v.tensor_tensor(deg_rsq[:, :], var[:, :], has[:, :], ALU.mult))
                    settled()
                step(v.tensor_tensor(Y[:, :, :], Y[:, :, :], over(deg_inv[:, :]), ALU.mult))
                settled()
                if hop < 2:
                    split(Y)
                step(v.tensor_tensor(total[:, :, :], total[:, :, :], Y[:, :, :], ALU.add))
                settled()
            step(v.scalar_tensor_tensor(X[:, :, :], total[:, :, :], 0.25, X[:, :, :], ALU.mult, ALU.add))
            settled()
            layer_norm(X, X, 1e-5)
            step(v.tensor_tensor(W[:, :, :], X[:, :, :], over(deg_rsq[:, :]), ALU.mult))
            settled()
            split(W)
            sweep(6)
            sweep(7)
            v.wait_ge(sweep_read, 9)
            step(v.tensor_tensor(Y[:, :, :], Y[:, :, :], over(deg_rsq[:, :]), ALU.mult))
            settled()
            step(v.tensor_tensor(X[:, :, :], X[:, :, :], Y[:, :, :], ALU.add))
            settled()
            layer_norm(X, X, 1e-5)
            split(X)
            sweep(8)
            sweep(9)
            v.wait_ge(sweep_read, 11)
            step(v.tensor_tensor(Y[:, :, :], Y[:, :, :], over(deg_inv[:, :]), ALU.mult))
            step(v.tensor_copy(Z[:, :, 0:DIM], X[:, :, :]))
            settled()

            def s2t(b, q):
                v.wait_ge(s2t_lo, b + 1)
                v.scalar_tensor_tensor(W[:, bass.ds(b, 1), :].rearrange("p a c -> p (a c)"), ps[:, q, 0:DIM], 1.0 / SCALE,
                                       ylo[:, bass.ds(b, 1), :].rearrange("p a c -> p (a c)"), ALU.mult, ALU.add).then_inc(s2t_read, 1)
            v.nop().then_inc(s2t_read, 2)
            with v.Fori(0, BLOCKS // 2) as i:
                for q in range(2):
                    s2t(i * 2 + q, q)
            s2t(BLOCKS - 1, 0)
            v.wait_ge(s2t_read, BLOCKS + 2)
            step(v.tensor_scalar(cnt_d[:, :], cnt_d[:, :], 1.0, None, ALU.max))
            settled()
            step(v.reciprocal(cnt_d[:, :], cnt_d[:, :]))
            settled()
            step(v.tensor_tensor(W[:, :, :], W[:, :, :], over(cnt_d[:, :]), ALU.mult))
            settled()
            step(v.tensor_tensor(Z[:, :, DIM:2 * DIM], Y[:, :, :], W[:, :, :], ALU.add))
            settled()
            v.nop().then_inc(nt_ready, 1)
            product_out(1, Y, None)
            step(v.tensor_tensor(Y[:, :, :], Y[:, :, :], feat(bl[:, :]), ALU.add))
            settled()
            step(v.tensor_tensor(Y[:, :, :], Y[:, :, :], X[:, :, :], ALU.add))
            settled()
            layer_norm(W, Y, 1e-5)
            v.nop().then_inc(act_done, 100 - a)

        @block.scalar
        def _(sc):
            for q in range(BLOCKS // 4 + 1):
                w = min(4, BLOCKS - 4 * q)
                sc.wait_ge(proj_pe, q + 1)
                sc.activation(proj[:, 4 * q:4 * q + w, :], ps[:, q % 2, 0:w * 2 * DIM].rearrange("p (b f) -> p b f", f=2 * DIM), ACT.Copy).then_inc(proj_act, 1)

            def store(i):
                for u in range(RING):
                    g = RING * i + u
                    sc.wait_ge(msg_ready, g + 1)
                    sc.dma_start(msg_rows[:, bass.ds(g * TILES, TILES), :], msgb[:, u, :, :]).then_inc(msg_out[u], 16)
            with sc.Fori(0, GROUPS // RING) as i:
                store(i)
            sc.wait_ge(exp_in, 1)
            sc.activation(exp_dst[:, :, 0], seg_f, ACT.Exp).then_inc(exp_done, 2)

            def product_copies(k, part):
                for q in range(13):
                    w = min(4, BLOCKS - 4 * q)
                    sc.wait_ge(nt_t, 13 * k + q + 1)
                    if q >= 2 or k:
                        sc.wait_ge(nt_mm, 13 * k + q - 1)
                    sc.activation(zt[0:part, q % 2, 0:w * LANES], ps[0:part, 2 + q % 2, 0:w * LANES], ACT.Copy).then_inc(nt_copied, 1)

            def sqrt(t, k):
                sc.wait_ge(act_v, k)
                sc.activation(t[:, :], t[:, :], ACT.Sqrt).then_inc(act_done, 1)

            product_copies(0, DIM)
            sqrt(var, 1)
            sqrt(var, 2)

            sc.wait_ge(tab_v, TAB_V)
            for g in range(BG):
                for l, mat in enumerate((dst_major, src_major)):
                    sc.dma_start(mat[0][:, g * BGW:(g + 1) * BGW], cacc[:, l, g * BGW:(g + 1) * BGW]).then_inc(counts_out[g], 16)
            rows = sc.value_load(n_rows[0:1, 0:1], min_val=1, max_val=SLOT_ROWS)
            with sc.Fori(0, ROW_LOOPS) as o:
                with sc.If(o * ROW_LOOP < rows):
                    with sc.Fori(0, ROW_LOOP // 2) as j:
                        for u in range(2):
                            r = o * ROW_LOOP + j * 2 + u
                            with sc.If(r < rows):
                                b = sc.value_load(block_of_row[0:1, bass.ds(r, 1)], min_val=0, max_val=BLOCKS - 1)
                                for g in range(BG):
                                    q = (BG * u + g) % 2
                                    sc.wait_ge(counts_out[g], (r + 1) * 32)
                                    for l in range(2):
                                        sc.wait_ge(tile_mm, r * (2 * BG) + 2 * g + l + 1 + JOB_CREDIT)
                                        sc.activation(cacc[:, l, g * BGW:(g + 1) * BGW],
                                                      ps[:, 4 * q + 2 * l:4 * q + 2 * l + 2, :].rearrange("p k c -> p (k c)")[:, 0:BGW], ACT.Copy).then_inc(tile_copied, 1)
                                    sc.wait_ge(tile_copied, r * (2 * BG) + 2 * g + 2 + JOB_CREDIT)
                                    for l, mat in enumerate((dst_major, src_major)):
                                        sc.dma_start(mat[bass.ds(b, 1), :, g * BGW:(g + 1) * BGW].rearrange("a p c -> (a p) c"),
                                                     cacc[:, l, g * BGW:(g + 1) * BGW]).then_inc(counts_out[g], 16)
            for g in range(BG):
                sc.wait_ge(counts_out[g], (rows + 1) * 32)
            sc.nop().then_inc(built, 1)

            def low(w):
                h = w % 2
                b0, b1 = ((0, HALF), (HALF, BLOCKS))[h]
                sc.wait_ge(sweep_mm, w + 1)
                pv = ps[:, 0:7, :].rearrange("p k (b c) -> p (k b) c", c=LANES)[:, 0:b1 - b0, :]
                sc.activation(ylo[:, b0:b1, :], pv[:, :, DIM:2 * DIM], ACT.Copy, scale=1.0 / SCALE).then_inc(lo_copied, 1)

            k = 3
            for w in range(2 * HOPS):
                low(w)
                if w in (1, 5, 7):
                    sqrt(var, k)
                    k += 1

            def s2t_low(b, q):
                sc.wait_ge(s2t_mm, b + 1)
                sc.activation(ylo[:, bass.ds(b, 1), :].rearrange("p a c -> p (a c)"), ps[:, q, DIM:2 * DIM], ACT.Copy, scale=1.0 / SCALE)
                sc.activation(cnt_d[:, bass.ds(b, 1)], ps[:, q, 2 * DIM:2 * DIM + 1], ACT.Copy).then_inc(s2t_lo, 1)
            with sc.Fori(0, BLOCKS // 2) as i:
                for q in range(2):
                    s2t_low(i * 2 + q, q)
            s2t_low(BLOCKS - 1, 0)
            product_copies(1, LANES)
            sqrt(var, k)

        @block.tensor
        def _(pe):
            pe.nop().then_inc(pick_used, PICKS)
            pe.nop().then_inc(hist_used, 2)
            pe.wait_ge(x_in, 48)
            pe.wait_ge(consts_in, 16 * 9)
            for q in range(BLOCKS // 4 + 1):
                if q >= 2:
                    pe.wait_ge(proj_act, q - 1)
                for b in range(4 * q, min(4 * q + 4, BLOCKS)):
                    m = pe.matmul(ps[:, q % 2, (b - 4 * q) * 2 * DIM:(b - 4 * q + 1) * 2 * DIM], xt[:, b * LANES:(b + 1) * LANES], w_node[:, :], start=True, stop=True)
                m.then_inc(proj_pe, 1)
            pe.wait_ge(proj_act, BLOCKS // 4 + 1)

            def edge_group(i, u, first):
                g = RING * i + u
                pe.wait_ge(kf_in[u], 16 * (i + 1))
                pe.wait_ge(qf_in[u], 16 * (i + 1))
                for h in range(2):
                    if not (first and u == 0):
                        pe.wait_ge(edge_v_done, g * 2 + h - 1)
                    for c in range(TILES // 2):
                        t = h * (TILES // 2) + c
                        o = ps[0:ROWS, 4 + t // 2, (t % 2) * 3 * DIM:(t % 2 + 1) * 3 * DIM]
                        pe.matmul(o[:, 0:2 * DIM], kf[h * DIM:(h + 1) * DIM, u, c * ROWS:(c + 1) * ROWS], w_edge[h * DIM:(h + 1) * DIM, :], start=True, stop=True)
                        m = pe.matmul(o[:, 2 * DIM:3 * DIM], qf[:, u, t * ROWS:(t + 1) * ROWS], wq[:, :], start=True, stop=True)
                    m.then_inc(edge_mm, 1)

            def add_picked(s, q, first, base):
                pe.wait_ge(pick_ready, s + base + 1)
                for k in range(4):
                    m = pe.matmul(ps[0:ROWS, k, 0:COLS // 4], ident[0:ROWS, 0:ROWS], picked[:, q, k * (COLS // 4):(k + 1) * (COLS // 4)],
                                  start=first, stop=False, skip_group_check=True)
                m.then_inc(pick_used, 1)

            def rank_iter(i, first):
                edge_group(i, 0, first)
                for u in range(STEPS):
                    edge_group(i, u + 1, first)
                    add_picked(i * STEPS + u, u, first and u == 0, 0)

            rank_iter(0, True)
            with pe.Fori(1, RANK_ITERS) as i:
                rank_iter(i, False)
            edge_group(RANK_ITERS, 0, False)
            edge_group(RANK_ITERS, 1, False)
            add_picked(BLOCKS - 1, 0, False, 0)
            edge_group(RANK_ITERS, 2, False)
            edge_group(RANK_ITERS, 3, False)
            pe.wait_ge(tab_v, 1)
            pe.wait_ge(rank_step, 3 * BLOCKS)
            pe.transpose(ps[0:BLOCKS, 0, 0:ROWS], row_last[:, :], ident[0:ROWS, 0:ROWS])
            pe.matmul(ps[0:BLOCKS, 1, 0:ROWS], ones[0:ROWS, 0:BLOCKS], nb_diag[:, :], start=True, stop=True).then_inc(tab_pe, 1)
            pe.wait_ge(tab_v, 2)
            pe.transpose(ps[0:ROWS, 2, 0:BLOCKS], carry_t[:, 0:ROWS], ident[0:BLOCKS, 0:BLOCKS]).then_inc(tab_pe, 1)

            def histogram(k, q, first):
                pe.wait_ge(hist_ready, 2 * k + 2)
                for t in range(HIST):
                    m = pe.matmul(ps[0:BLOCKS, 0, 0:BLOCKS], oh_d[:, q, t, :], oh_s[:, q, t, :], start=(first and t == 0), stop=False, skip_group_check=True)
                m.then_inc(hist_used, 1)

            def hist_iter(i, first):
                edge_group(i, 0, False)
                for u in range(RING - 1):
                    edge_group(i, u + 1, False)
                    histogram((i - HIST_AT) * RING + u, u % 2, first and u == 0)
                histogram((i - HIST_AT) * RING + RING - 1, (RING - 1) % 2, False)
            hist_iter(HIST_AT, True)
            with pe.Fori(HIST_AT + 1, HIST_AT + HIST_STEPS // RING) as i:
                hist_iter(i, False)
            edge_group(CARRY_AT - 1, 0, False)
            edge_group(CARRY_AT - 1, 1, False)
            histogram(HIST_STEPS - 2, 0, False)
            edge_group(CARRY_AT - 1, 2, False)
            histogram(HIST_STEPS - 1, 1, False)
            edge_group(CARRY_AT - 1, 3, False)
            pe.wait_ge(tab_v, 3)
            pe.matmul(ps[0:BLOCKS, 1, 0:3], upper[0:BLOCKS, 0:BLOCKS], bt[:, :], start=True, stop=True)
            pe.matmul(ps[0:1, 1, 8:9], ones[0:BLOCKS, 0:1], bt[:, 0:1], start=True, stop=True).then_inc(tab_pe, 1)
            quarter = SLOT_ROWS_UP // 4

            def over_rows(values, partitions):
                for k in range(4):
                    m = pe.matmul(ps[0:partitions, k, 0:quarter], values, row_cmp[:, k * quarter:(k + 1) * quarter], start=True, stop=True)
                m.then_inc(tab_pe, 1)
            pe.wait_ge(tab_v, 4)
            pe.matmul(ps[0:ROWS, 0, 416:416 + BLOCKS], ones[0:BLOCKS, 0:ROWS], rs_diag[:, :], start=True, stop=True)
            over_rows(ones[0:BLOCKS, :], LANES)
            pe.wait_ge(tab_v, 5)
            over_rows(ones[0:BLOCKS, :], LANES)
            pe.wait_ge(tab_v, 6)
            over_rows(need_m[:, :], LANES // 2)
            pe.wait_ge(tab_v, 7)
            pe.matmul(ps[:, 0, 0:CHUNKS], ones[0:BLOCKS, :], chunk_tmp, start=True, stop=True)
            pe.matmul(ps[:, 1, 0:CHUNKS], base_m[:, :], chunk_oh, start=True, stop=True)
            pe.matmul(ps[:, 2, 0:CHUNKS], ones[0:BLOCKS, :], chunk_oh, start=True, stop=True).then_inc(tab_pe, 1)

            def look_iter(i, at, base, first):
                edge_group(i, 0, False)
                for u in range(STEPS):
                    edge_group(i, u + 1, False)
                    for k in range(2):
                        add_picked((i - at) * LOOK + 2 * u + k, (2 * u + k) % PICKS, first and u == 0 and k == 0, base)

            def look_iters(at, base):
                look_iter(at, at, base, True)
                with pe.Fori(at + 1, at + BLOCKS // LOOK) as i:
                    look_iter(i, at, base, False)
            look_iters(CARRY_AT, BLOCKS)
            edge_group(START_AT - 1, 0, False)
            edge_group(START_AT - 1, 1, False)
            add_picked(BLOCKS - 1, 0, False, BLOCKS)
            edge_group(START_AT - 1, 2, False)
            edge_group(START_AT - 1, 3, False)
            look_iters(START_AT, 2 * BLOCKS)
            add_picked(BLOCKS - 1, 0, False, 2 * BLOCKS)

            turned = ps[:, 0:4, :].rearrange("p k (c w) -> p (k c) w", w=LANES)
            for k, t in enumerate((tc, ind[:, :], keep_b[:, :])):
                pe.wait_ge(turn_v, k + 1)
                for c in range(DEAL):
                    n = LANES if c < DEAL - 1 else DEAL_REST
                    m = pe.transpose(turned[0:n, c, 0:ROWS], t[:, c * LANES:c * LANES + n], ident[0:ROWS, 0:ROWS])
                m.then_inc(turn_pe, 1)
            with pe.Fori(REST_AT, ITERS) as i:
                for u in range(RING):
                    edge_group(i, u, False)

            for k in range(2):
                pe.wait_ge(line_v, 2 * k + 1)
                pe.transpose(ps[0:1, 0, 0:ROWS], edge_v[:, 0:1], ident[0:ROWS, 0:ROWS])
                pe.transpose(ps[0:1, 1, 0:ROWS], edge_v[:, 1:2], ident[0:ROWS, 0:ROWS]).then_inc(line_pe, 1)
                pe.wait_ge(line_v, 2 * k + 2)
                pe.transpose(ps[0:ROWS, 2, 0:1], line_c[:, k:k + ROWS], ident[0:1, 0:1]).then_inc(line_pe, 1)

            def agg_chunk(i, u, first):
                r = RING * i + u
                q = u % 2
                if not (first and u < 2):
                    pe.wait_ge(agg_added, r - 1)
                pe.wait_ge(woh_ready, (r + 1) * PER_LANE)
                for j in range(PER_LANE):
                    m = pe.matmul(ps[:, q, 0:MSGW], woh[:, q, j, :], mch[:, u, j * MSGW:(j + 1) * MSGW], start=(j == 0), stop=(j == PER_LANE - 1))
                m.then_inc(agg_mm, 1)
            for u in range(RING):
                agg_chunk(0, u, True)
            with pe.Fori(1, CHUNKS // RING) as i:
                for u in range(RING):
                    agg_chunk(i, u, False)

            def node_product(k, part, w_t):
                pe.wait_ge(nt_ready, k + 1)
                for q in range(13):
                    n = min(4, BLOCKS - 4 * q)
                    if q >= 2:
                        pe.wait_ge(nt_copied, 13 * k + q - 1)
                    for b in range(n):
                        m = pe.transpose(ps[0:part, 2 + q % 2, b * LANES:(b + 1) * LANES], Z[:, 4 * q + b, 0:part], ident[:, :])
                    m.then_inc(nt_t, 1)
                    pe.wait_ge(nt_copied, 13 * k + q + 1)
                    if q >= 2:
                        pe.wait_ge(nt_out, 13 * k + q - 1)
                    for b in range(n):
                        m = pe.matmul(ps[:, 4 + q % 2, b * DIM:(b + 1) * DIM], zt[0:part, q % 2, b * LANES:(b + 1) * LANES], w_t, start=True, stop=True)
                    m.then_inc(nt_mm, 1)
            node_product(0, DIM, wo[:, :])

            pe.nop().then_inc(tile_mm, JOB_CREDIT)
            pe.nop().then_inc(tile_copied, JOB_CREDIT)
            pe.wait_ge(nt_out, 13)
            pe.wait_ge(tab_v, TAB_V)
            rows = pe.value_load(n_rows[0:1, 0:1], min_val=1, max_val=SLOT_ROWS)
            with pe.Fori(0, ROW_LOOPS) as o:
                with pe.If(o * ROW_LOOP < rows):
                    with pe.Fori(0, ROW_LOOP // 2) as j:
                        for u in range(2):
                            r = o * ROW_LOOP + j * 2 + u
                            with pe.If(r < rows):
                                pe.wait_ge(pay_conv, r + 1)
                                for g in range(BG):
                                    q = (BG * u + g) % 2
                                    pe.wait_ge(oh_ready, r * (BLOCKS * 2) + (g + 1) * BG * 2)
                                    for l in range(2):
                                        pe.wait_ge(tile_copied, r * (2 * BG) + 2 * g + l + 1)
                                        first_bank = 4 * q + 2 * l
                                        pe.matmul(ps[:, first_bank, :], keep_diag[:, u, :], cacc[:, l, g * BGW:g * BGW + 512],
                                                  start=True, stop=False, skip_group_check=True)
                                        pe.matmul(ps[:, first_bank + 1, 0:BGW - 512], keep_diag[:, u, :], cacc[:, l, g * BGW + 512:(g + 1) * BGW],
                                                  start=True, stop=False, skip_group_check=True)
                                        for s in range(BG):
                                            m = pe.matmul(ps[:, first_bank + s // 4, (s % 4) * LANES:(s % 4 + 1) * LANES],
                                                          oh[:, q, s, 1 - l, :], oh[:, q, s, l, :],
                                                          start=False, stop=(s in (3, BG - 1)), skip_group_check=True)
                                        m.then_inc(tile_mm, 1)

            pe.nop().then_inc(big_used, 4)
            one_hop_sems = (xs_ready, sweep_read)

            def hop_sweeps(hop, degrees):
                pe.wait_ge(xs_ready, hop + 1)
                for h in range(2):
                    w = hop * 2 + h
                    n = (HALF, BLOCKS - HALF)[h]
                    pe.wait_ge(sweep_read, w + 1)

                    def block(b, u, first):
                        for s in range(n):
                            m = pe.matmul(ps[:, s // 4, (s % 4) * LANES:(s % 4 + 1) * LANES], big[:, u, s * LANES:(s + 1) * LANES],
                                          xs[:, bass.ds(b, 1), 0:2 * DIM].rearrange("p a c -> p (a c)"),
                                          start=(first and s % 4 == 0), stop=False, skip_group_check=True)
                            if degrees:
                                m = pe.matmul(ps[:, 7, h * HALF + s:h * HALF + s + 1], big[:, u, s * LANES:(s + 1) * LANES], one16[:, :],
                                              start=(first and h == 0 and s == 0), stop=False, skip_group_check=True)
                        m.then_inc(big_used, 1)
                        return m
                    pe.wait_ge(big_in[4], (w + 1) * 16)
                    block(0, 4, True)
                    with pe.Fori(0, (BLOCKS - 1) // 4) as i:
                        for u in range(4):
                            pe.wait_ge(big_in[u], (w * ((BLOCKS - 1) // 4) + i + 1) * 16)
                            block(i * 4 + u + 1, u, False)
                    pe.wait_ge(big_used, (w + 1) * BLOCKS + 4)
                    pe.nop().then_inc(sweep_mm, 1)

            pe.wait_ge(built, 1)
            hop_sweeps(0, True)
            with pe.Fori(1, HOPS) as hop:
                hop_sweeps(hop, False)

            pe.wait_ge(sweep_read, 2 * HOPS + 1)

            def s2t(b, slot, q, use):
                pe.wait_ge(bigs_in[slot], use * 16)
                pe.wait_ge(s2t_read, b + 1)
                for s in range(BLOCKS):
                    m = pe.matmul(ps[:, q, 0:2 * DIM + 1], bigs[slot][:, s * LANES:(s + 1) * LANES], xs[:, s, :],
                                  start=(s == 0), stop=(s == BLOCKS - 1))
                m.then_inc(s2t_mm, 1)
            with pe.Fori(0, BLOCKS // 6) as i:
                for u in range(6):
                    s2t(i * 6 + u, u % 3, u % 2, i * 2 + u // 3 + 1)
            s2t(BLOCKS - 1, 0, 0, BLOCKS // 3 + 1)
            node_product(1, LANES, wl[:, :])


def kernel(x, src, dst, edge_attr_64, edge_attr_64_n2, edge_attr_64_n3, L0_gnn_W_msg, L0_gnn_W_q, L0_gnn_W_k,
           L0_gnn_W_out, L0_gnn_gamma, L0_gnn_beta, L3_gnn_W1, L3_gnn_Wr, L3_gnn_br):
    import numpy as np
    import concourse.bacc as bacc
    from concourse.bass_utils import run_bass_kernel_spmd

    def plain(a):
        return np.ascontiguousarray(np.asarray(a))

    half = TILES // 2
    ek = np.asarray(edge_attr_64).reshape(ROWS, GROUPS, 2, half, DIM).transpose(1, 2, 4, 3, 0).reshape(GROUPS, 2 * DIM, half * ROWS)
    eq = np.concatenate([np.asarray(edge_attr_64_n2), np.asarray(edge_attr_64_n3)], axis=1)
    eq = eq.reshape(ROWS, GROUPS, TILES, 2 * DIM).transpose(1, 3, 2, 0).reshape(GROUPS, 2 * DIM, TILES * ROWS)
    arrays = {
        "x": plain(x), "x_t": plain(np.asarray(x).T), "src": plain(src), "dst": plain(dst),
        "edge_k": plain(ek), "edge_q": plain(eq),
        "w_in": plain(np.concatenate([np.asarray(L0_gnn_W_msg), np.asarray(L0_gnn_W_k)], axis=1)),
        "w_q": plain(L0_gnn_W_q), "w_out": plain(L0_gnn_W_out),
        "gamma": plain(L0_gnn_gamma).reshape(1, DIM), "beta": plain(L0_gnn_beta).reshape(1, DIM),
        "w_last": plain(np.concatenate([np.asarray(L3_gnn_Wr).T, np.asarray(L3_gnn_W1).T], axis=0)),
        "b_last": plain(L3_gnn_br).reshape(1, DIM),
    }
    nc = bacc.Bacc("TRN2", target_bir_lowering=False, num_devices=1)
    args = [nc.dram_tensor(f"in_{k}", a.shape, mybir.dt.from_np(a.dtype), kind="ExternalInput").ap() for k, a in arrays.items()]
    out = nc.dram_tensor("out_nodes", [NODES, DIM], F32, kind="ExternalOutput").ap()
    gnn_kernel(nc, *args, out)
    r = run_bass_kernel_spmd(nc, [{f"in_{k}": a for k, a in arrays.items()}], core_ids=[0])
    return r.results[0]["out_nodes"]
```

```python
import concourse.bass as bass
from concourse import mybir
from contextlib import ExitStack

F32, F16, F8, I32 = mybir.dt.float32, mybir.dt.float16, mybir.dt.float8e4, mybir.dt.int32
ALU, ACT, AX = mybir.AluOpType, mybir.ActivationFunctionType, mybir.AxisListType

LANES = 128
NODES, EDGES, DIM = 6250, 200000, 64
BLOCKS = -(-NODES // LANES)
PADDED = BLOCKS * LANES
LAST = NODES - (BLOCKS - 1) * LANES
ROWS, COLS = 125, EDGES // 125
TILES = 8
GROUPS = COLS // TILES
RING = 4
SUB = 40
SUBS = COLS // SUB
RUN = 80
RUNS = COLS // RUN
SLOT_ROWS = EDGES // LANES + BLOCKS
ROW_LOOP = 32
ROW_LOOPS = -(-SLOT_ROWS // ROW_LOOP)
SLOT_ROWS_UP = ROW_LOOPS * ROW_LOOP
FILL_ROWS = 16
FILL_COLS = FILL_ROWS * PADDED * 2 // LANES
FILLS = SLOT_ROWS_UP // FILL_ROWS
FILL_LOOP = 6
HIST = 32
DEAL = -(-COLS // LANES)
DEAL_REST = COLS - (DEAL - 1) * LANES
DEAL_RING = 5
DEAL_LOOP = 2 * DEAL_RING
DEAL_LAST = ROWS // DEAL_LOOP
EVEN_ROWS = ROWS - 1
PICKS = 3
BG = 7
BGW = BG * LANES
HALF = (BLOCKS + 1) // 2
NEG = -1.0e30
SCALE = 4096.0
HOPS = 5
MSGW = DIM + 1


def gnn_kernel(nc, x, x_t, src, dst, edge_k, edge_q, w_in, w_q, w_out, gamma, beta, w_last, b_last, out):
    table = nc.dram_tensor("node_projections", [PADDED, 2 * DIM], F32, kind="Internal").ap()
    msgs = nc.dram_tensor("messages", [EDGES, MSGW], F32, kind="Internal").ap()
    sums = nc.dram_tensor("running_sums", [EDGES, MSGW], F32, kind="Internal").ap()
    row_sums = nc.dram_tensor("sums_into_rows", [ROWS, MSGW], F32, kind="Internal").ap()
    dst_list = nc.dram_tensor("dst_as_float", [EDGES // SUB, SUB], F32, kind="Internal").ap()
    dst_firsts = nc.dram_tensor("first_dst_of_steps", [ROWS, SUBS], F32, kind="Internal").ap()
    slots = nc.dram_tensor("edge_slots", [SLOT_ROWS_UP * PADDED, 2], F16, kind="Internal").ap()
    counts = nc.dram_tensor("counts", [BLOCKS, LANES, 2, PADDED], F16, kind="Internal").ap()
    counts8 = nc.dram_tensor("capped_counts", [BLOCKS, LANES, 2, PADDED // 2], F16, kind="Internal").ap()

    ctx = ExitStack()
    with ctx:
        def sem(name):
            return ctx.enter_context(nc.semaphore(name))

        def allocator(stack):
            return lambda name, shape, dt: stack.enter_context(nc.sbuf_tensor(name, shape, dt))

        sb = allocator(ctx)
        X = sb("X", [LANES, BLOCKS, DIM], F32)
        mem_a = sb("mem_a", [LANES, 2 * COLS], F32)
        mem_b = sb("mem_b", [LANES, COLS + DEAL * ROWS], F32)
        exp_w, dst_f = mem_a[0:ROWS, 0:COLS], mem_a[0:ROWS, COLS:2 * COLS]
        src_i = mem_b[0:ROWS, 0:COLS].bitcast(I32)
        slot_t = mem_b[:, COLS:COLS + DEAL * ROWS].bitcast(I32).rearrange("p (c r) -> p c r", c=DEAL)
        xs = mem_a[:, :].bitcast(F16)[:, 0:BLOCKS * (2 * DIM + 1)].rearrange("p (b c) -> p b c", b=BLOCKS)
        total = mem_b[:, 0:BLOCKS * DIM].rearrange("p (b c) -> p b c", b=BLOCKS)
        mem_c = sb("mem_c", [LANES, 2 * COLS + 2], F32)
        pen = mem_c[0:ROWS, 0:COLS + 1]
        att = mem_c[0:ROWS, COLS + 1:2 * COLS + 1]
        lanes_t = sb("lanes_t", [LANES, DEAL, ROWS, 2], F16)
        assert 2 * DEAL_REST == LANES and ROWS % DEAL_LOOP == DEAL_RING and EVEN_ROWS % 2 == 0
        iota = sb("iota", [LANES, LANES], F32)
        iota16 = sb("iota16", [LANES, LANES], F16)
        lane_no = sb("lane_no", [LANES, 1], F32)
        ident = sb("ident", [LANES, LANES], F32)
        ident16 = sb("ident16", [LANES, LANES], F16)
        ones = sb("ones", [LANES, LANES], F32)
        w_node = sb("w_node", [DIM, 2 * DIM], F32)
        w_edge = sb("w_edge", [LANES, 2 * DIM], F32)
        wq = sb("wq", [2 * DIM, DIM], F32)
        wo = sb("wo", [DIM, DIM], F32)
        wl = sb("wl", [2 * DIM, DIM], F32)
        gam = sb("gam", [LANES, DIM], F32)
        bet = sb("bet", [LANES, DIM], F32)
        bl = sb("bl", [LANES, DIM], F32)
        keep_row = sb("keep_row", [LANES, SLOT_ROWS_UP], F32)
        row_tab = sb("row_tab", [LANES // 2 + 1, SLOT_ROWS_UP], I32)
        block_of_row, landed_need, last_of_block = row_tab[0:1, :], row_tab[32:33, :], row_tab[64:65, :]
        capped = sb("capped", [1, 1], I32)
        lane_deg = sb("lane_deg", [LANES, 1], F32)
        n_rows = sb("n_rows", [1, 1], I32)
        node_no = sb("node_no", [LANES, BLOCKS], F32)
        found = sb("found", [LANES, BLOCKS], F32)
        row_f = sb("row_f", [LANES, BLOCKS], F32)
        row_i = sb("row_i", [LANES, BLOCKS], I32)
        sub_i = sb("sub_i", [LANES, BLOCKS], I32)
        last_i = sb("last_i", [LANES, BLOCKS], I32)
        spans = sb("spans", [LANES, BLOCKS], F32)
        pay = sb("pay", [LANES, 2, BLOCKS, 2], F16)
        gidx = sb("gidx", [ROWS, RING, TILES], I32)
        sidx = sb("sidx", [LANES, DEAL_RING, DEAL], I32)
        spay = sb("spay", [LANES, DEAL_RING, DEAL, 2], F16)
        mean = sb("mean", [LANES, BLOCKS], F32)
        var = sb("var", [LANES, BLOCKS], F32)
        deg_inv = sb("deg_inv", [LANES, BLOCKS], F32)
        deg_rsq = sb("deg_rsq", [LANES, BLOCKS], F32)
        has = sb("has", [LANES, BLOCKS], F32)

        ph = ExitStack()
        sb = allocator(ph)
        dblk = sb("dblk", [ROWS, COLS], F16)
        sblk = sb("sblk", [ROWS, COLS], F16)
        keep_b = sb("keep_b", [ROWS, COLS], F32)
        ind = sb("ind", [ROWS, COLS], F32)
        cnt = sb("cnt", [ROWS, COLS], F32)
        picked_mem = sb("picked", [LANES, PICKS * COLS], F32)
        picked = picked_mem[0:ROWS, :].rearrange("p (k c) -> p k c", k=PICKS)
        dst_i, prev_i = ind[:, :].bitcast(I32), cnt[:, :].bitcast(I32)
        ta, tb, tc = picked[:, 0, :], picked[:, 1, :], picked[:, 2, :]
        seg_f, seg_m = ta, tb
        next_i = sb("next_i", [ROWS, 1], I32)
        next_f = sb("next_f", [ROWS, 1], F32)
        oh_mem = sb("oh_mem", [ROWS, 4 * HIST * BLOCKS], F16)
        oh_d, oh_s = (oh_mem[:, k * 2 * HIST * BLOCKS:(k + 1) * 2 * HIST * BLOCKS].rearrange("p (q t b) -> p q t b", q=2, t=HIST) for k in range(2))
        cmp_mem = oh_mem[:, :].bitcast(F32)
        row_cmp = cmp_mem[0:BLOCKS, 0:SLOT_ROWS_UP]
        row_tmp = cmp_mem[0:BLOCKS, SLOT_ROWS_UP:SLOT_ROWS_UP + ROWS]
        pair_no = cmp_mem[0:BLOCKS, SLOT_ROWS_UP + ROWS:SLOT_ROWS_UP + 2 * ROWS]
        firsts = sb("firsts", [LANES, ROWS], F32)
        sub_firsts = sb("sub_firsts", [ROWS, SUBS], F32)
        minus1 = sb("minus1", [LANES, FILL_COLS], F16)
        row_last = sb("row_last", [ROWS, BLOCKS], F32)
        row_last_t = sb("row_last_t", [BLOCKS, ROWS], F32)
        no_break = sb("no_break", [ROWS, 1], F32)
        nb_diag = sb("nb_diag", [ROWS, ROWS], F32)
        nb_t = sb("nb_t", [BLOCKS, ROWS], F32)
        carry_t = sb("carry_t", [BLOCKS, ROWS + 1], F32)
        carry = sb("carry", [ROWS, BLOCKS], F32)
        upper = sb("upper", [LANES, LANES], F32)
        bt = sb("bt", [BLOCKS, 2], F32)
        bti = sb("bti", [BLOCKS, 1], I32)
        bend = sb("bend", [BLOCKS, 2], F32)
        bstart = sb("bstart", [BLOCKS, 2], F32)
        need_v = sb("need_v", [BLOCKS, 1], F32)
        rs_diag = sb("rs_diag", [BLOCKS, BLOCKS], F32)
        row_start = sb("row_start", [ROWS, BLOCKS], F32)
        row_no = sb("row_no", [LANES, SLOT_ROWS_UP], F32)
        need_m = sb("need_m", [BLOCKS, LANES // 2], F32)
        feats = sb("feats", [LANES, PADDED], F32)
        xt = feats[0:DIM, :]
        kf = feats[:, 0:RING * TILES // 2 * ROWS].rearrange("p (u c) -> p u c", u=RING)
        qf = feats[:, RING * TILES // 2 * ROWS:RING * TILES // 2 * ROWS * 3].rearrange("p (u c) -> p u c", u=RING)
        rows_mem = sb("rows_mem", [LANES, BLOCKS * 2 * DIM], F32)
        proj = rows_mem[:, :].rearrange("p (b c) -> p b c", b=BLOCKS)
        GAT, KK = RING * TILES * 2 * DIM, 2 * TILES * DIM
        gat = rows_mem[0:ROWS, 0:GAT].rearrange("p (u t c) -> p u t c", u=RING, t=TILES)
        kk = rows_mem[0:ROWS, GAT:GAT + KK].rearrange("p (u t c) -> p u t c", u=2, t=TILES)
        mm = rows_mem[0:ROWS, GAT + KK:GAT + 2 * KK].rearrange("p (u t c) -> p u t c", u=2, t=TILES)
        msg_mem = sb("msg_mem", [LANES, RING * TILES * MSGW], F32)
        msgb = msg_mem[0:ROWS, :].rearrange("p (u t c) -> p u t c", u=RING, t=TILES)
        steps = msg_mem[:, 0:BLOCKS * SUB].rearrange("p (b c) -> p b c", b=BLOCKS)
        line = sb("line", [1, 2, ROWS], F32)
        line_c = sb("line_c", [1, ROWS + 1], F32)
        edge_v = sb("edge_v", [ROWS, 2], F32)
        edge_in = sb("edge_in", [ROWS, 1], F32)
        ph.close()

        ph = ExitStack()
        sb = allocator(ph)
        seg = sb("seg", [ROWS, RING, RUN, MSGW], F32)
        keep_on = sb("keep_on", [ROWS, COLS], F32)
        row_keep = sb("row_keep", [ROWS, 1], F32)
        row_diag = sb("row_diag", [ROWS, ROWS], F32)
        tail_t = sb("tail_t", [MSGW, 2, ROWS], F32)
        into_t = sb("into_t", [MSGW, ROWS + 1], F32)
        into = sb("into", [ROWS, MSGW], F32)
        ph.close()

        sb = allocator(ctx)
        node_mem = sb("node_mem", [LANES, 5 * BLOCKS * DIM], F32)
        Z = node_mem[:, 0:2 * BLOCKS * DIM].rearrange("p (b c) -> p b c", b=BLOCKS)
        Y, W, ylo = (node_mem[:, k * BLOCKS * DIM:(k + 1) * BLOCKS * DIM].rearrange("p (b c) -> p b c", b=BLOCKS) for k in (2, 3, 4))
        zt = sb("zt", [LANES, 2, 4 * LANES], F32)

        ph = ExitStack()
        sb = allocator(ph)
        agg = sb("agg", [LANES, BLOCKS, MSGW], F32)
        agg_in = sb("agg_in", [LANES, BLOCKS, MSGW], F32)
        keep_diag = sb("keep_diag", [LANES, 2, LANES], F16)
        oh = sb("oh", [LANES, 2, LANES, 2 * BG], F16)
        lanes_rep = sb("lanes_rep", [LANES, LANES, 2 * BG], F16)
        cacc = node_mem[:, 0:2 * BLOCKS * DIM].bitcast(F16).rearrange("p (l c) -> p l c", l=2)
        den = sb("den", [LANES, BLOCKS], F32)
        cacc8 = sb("cacc8", [LANES, 2, PADDED], F8)
        cacc8_pairs = cacc8[:, :, :].rearrange("p l c -> p (l c)").bitcast(F16).rearrange("p (l c) -> p l c", l=2)
        ph.close()

        ph = ExitStack()
        sb = allocator(ph)
        big = sb("big", [LANES, 5, HALF * LANES], F16)
        bigs = [sb(f"bigs{i}", [LANES, PADDED], F16) for i in range(2)] + [mem_c[:, :].bitcast(F16)[:, 0:PADDED]]
        big8 = big[:, :, :].rearrange("p u c -> p (u c)").bitcast(F8).rearrange("p (u c) -> p u c", u=5)
        bigs8 = [t[:, :].bitcast(F8) for t in bigs]
        feats_now = sb("feats_now", [LANES, 5, 2 * DIM + 1], F16)
        cnt_d = sb("cnt_d", [LANES, BLOCKS], F32)
        deg = sb("deg", [LANES, BLOCKS], F32)
        ph.close()

        ps = ctx.enter_context(nc.psum_tensor("ps", [LANES, 8, 512], F32))

        edges_in, consts_in, x_in, filled = sem("edges_in"), sem("consts_in"), sem("x_in"), sem("filled")
        pool_consts, vec_consts, vec = sem("pool_consts"), sem("vec_consts"), sem("vec")
        hist_ready, hist_used = sem("hist_ready"), sem("hist_used")
        tab_v, tab_pe = sem("tab_v"), sem("tab_pe")
        pick_ready, pick_used = sem("pick_ready"), sem("pick_used")
        rank_step = sem("rank_step")
        ranked = sem("ranked")
        proj_pe, proj_act, table_out = sem("proj_pe"), sem("proj_act"), sem("table_out")
        kf_in = [sem(f"kf_in{u}") for u in range(RING)]
        qf_in = [sem(f"qf_in{u}") for u in range(RING)]
        gat_in = [sem(f"gat_in{u}") for u in range(RING)]
        msg_out = [sem(f"msg_out{u}") for u in range(RING)]
        gidx_ready, edge_mm, edge_v_done, msg_ready, edge_step = (
            sem("gidx_ready"), sem("edge_mm"), sem("edge_v_done"), sem("msg_ready"), sem("edge_step"))
        line_v, line_pe = sem("line_v"), sem("line_pe")
        exp_in, exp_done = sem("exp_in"), sem("exp_done")
        search_v, search_pe, lists_out, steps_in = sem("search_v"), sem("search_pe"), sem("lists_out"), sem("steps_in")
        seg_in = [sem(f"seg_in{u}") for u in range(RING)]
        seg_out = [sem(f"seg_out{u}") for u in range(RING)]
        weighed, scanned, into_out, ends_in = (
            sem("weighed"), sem("scanned"), sem("into_out"), sem("ends_in"))
        sidx_ready = sem("sidx_ready")
        dealt = [sem(f"dealt{u}") for u in range(DEAL_RING)]
        turn_v, turn_pe, landed = sem("turn_v"), sem("turn_pe"), sem("landed")
        nt_ready, nt_t, nt_copied, nt_mm, nt_out = (
            sem("nt_ready"), sem("nt_t"), sem("nt_copied"), sem("nt_mm"), sem("nt_out"))
        pay_in = [sem(f"pay_in{u}") for u in range(2)]
        keep_ready, oh_ready, tile_mm, tile_copied = (
            sem("keep_ready"), sem("oh_ready"), sem("tile_mm"), sem("tile_copied"))
        counts_out = [sem(f"counts_out{g}") for g in range(BG)]
        built = sem("built")
        big_in = [sem(f"big_in{u}") for u in range(5)]
        big_used, xs_ready, sweep_mm, lo_copied, sweep_read = (
            sem("big_used"), sem("xs_ready"), sem("sweep_mm"), sem("lo_copied"), sem("sweep_read"))
        bigs_in = [sem(f"bigs_in{u}") for u in range(3)]
        lot_begun, conv_begun = sem("lot_begun"), sem("conv_begun")
        feats_ready, conv_ready, flag_v, flag_pe, flag_ready = sem("feats_ready"), sem("conv_ready"), sem("flag_v"), sem("flag_pe"), sem("flag_ready")
        s2t_mm, s2t_lo, s2t_read = sem("s2t_mm"), sem("s2t_lo"), sem("s2t_read")
        act_v, act_done = sem("act_v"), sem("act_done")
        stored = sem("stored")

        TAB_V = 8
        STEPS = 3
        ITERS = GROUPS // RING
        RANK_ITERS = BLOCKS // STEPS
        HIST_STEPS = COLS // HIST
        HIST_AT = RANK_ITERS + 1
        CARRY_AT = HIST_AT + HIST_STEPS // RING + 1
        LOOK = 2 * STEPS
        START_AT = CARRY_AT + BLOCKS // LOOK + 1
        REST_AT = START_AT + BLOCKS // LOOK
        assert REST_AT <= ITERS and BLOCKS % STEPS == 1 and BLOCKS % LOOK == 1 and HIST_STEPS % RING == 2
        JOB_CREDIT = 4
        CAP = 16.0
        WIDE = 2 * DIM + 1
        REST = 3 * WIDE
        by3 = ps[:, :, 0:3 * WIDE].rearrange("p k (j c) -> p k j c", j=3)
        OUTS = 2 * 16
        COPY_AT = DEAL - 2
        AGG_AT = 3
        ways = [(g, l) for g in range(BG) for l in range(2)]
        caps = {3: (0, 1), 5: (2, 3), 6: (4, 5, 6)}
        block = ctx.enter_context(nc.Block())

        dst_rows = dst.rearrange("(p t) -> p t", t=COLS)
        src_rows = src.rearrange("(p t) -> p t", t=COLS)
        msg_rows = msgs.rearrange("(p t) c -> p t c", t=COLS)
        sum_rows = sums.rearrange("(p t) c -> p t c", t=COLS)
        fill_view = slots.rearrange("(f p c) k -> f p (c k)", f=FILLS, p=LANES)

        def wait_copied(engine, r, g, l):
            engine.wait_ge(tile_copied, r * len(ways) + ways.index((g, l)) + 1)

        @block.sync
        def _(sp):
            sp.dma_start(src_i[:, :], src_rows).then_inc(edges_in, 16)
            sp.dma_start(dst_i[:, :], dst_rows).then_inc(edges_in, 16)
            sp.wait_ge(vec_consts, 3)
            sp.dma_start(prev_i[1:ROWS, :], dst[COLS - 1:EDGES - 1].rearrange("(p t) -> p t", t=COLS)).then_inc(edges_in, 16)
            sp.dma_start(prev_i[0:1, 1:COLS], dst_rows[0:1, 0:COLS - 1]).then_inc(edges_in, 16)
            sp.dma_start(next_i[0:ROWS - 1, :], dst_rows[1:ROWS, 0:1], allow_slow_non_contiguous=True).then_inc(edges_in, 16)
            for t, a in ((w_node[:, :], w_in[0:DIM, :]), (w_edge[0:DIM, :], w_in[DIM:2 * DIM, :]),
                         (w_edge[DIM:2 * DIM, :], w_in[DIM:2 * DIM, :]), (wq[:, :], w_q), (wo[:, :], w_out),
                         (wl[:, :], w_last), (gam[:, :], gamma.to_broadcast([LANES, DIM])),
                         (bet[:, :], beta.to_broadcast([LANES, DIM])), (bl[:, :], b_last.to_broadcast([LANES, DIM]))):
                sp.dma_start(t, a).then_inc(consts_in, 16)
            sp.wait_ge(vec_consts, 7)
            sp.dma_start(xt[:, 0:NODES], x_t).then_inc(x_in, 16)
            sp.dma_start(X[:, 0:BLOCKS - 1, :], x[0:(BLOCKS - 1) * LANES, :].rearrange("(b p) f -> p b f", p=LANES)).then_inc(x_in, 16)
            sp.dma_start(X[0:LAST, BLOCKS - 1, :], x[(BLOCKS - 1) * LANES:NODES, :]).then_inc(x_in, 16)

            def load_features(i, first):
                for u in range(RING):
                    g = RING * i + u
                    if not first:
                        sp.wait_ge(edge_mm, (g - RING + 1) * 2)
                    sp.dma_start(kf[:, u, :], edge_k[bass.ds(g, 1), :, :].rearrange("a p c -> (a p) c")).then_inc(kf_in[u], 16)
                    sp.dma_start(qf[:, u, :], edge_q[bass.ds(g, 1), :, :].rearrange("a p c -> (a p) c")).then_inc(qf_in[u], 16)

            sp.wait_ge(proj_act, BLOCKS // 4 + 1)
            sp.dma_start(table.rearrange("(b p) f -> p b f", p=LANES), proj[:, :, :]).then_inc(table_out, 16)
            load_features(0, True)
            with sp.Fori(1, START_AT) as i:
                load_features(i, False)
            sp.wait_ge(tab_v, TAB_V - 1)
            rows = sp.value_load(n_rows[0:1, 0:1], min_val=1, max_val=SLOT_ROWS)
            with sp.Fori(0, FILLS // FILL_LOOP) as i:
                with sp.If(i * (FILL_LOOP * FILL_ROWS) <= rows):
                    for f in range(FILL_LOOP):
                        sp.dma_start(fill_view[bass.ds(i * FILL_LOOP + f, 1), :, :].rearrange("a p c -> (a p) c"), minus1[:, :]).then_inc(filled, 16)
                with sp.If(i * (FILL_LOOP * FILL_ROWS) > rows):
                    sp.nop().then_inc(filled, 16 * FILL_LOOP)
            with sp.Fori(START_AT, ITERS) as i:
                load_features(i, False)

            sp.wait_ge(exp_done, 2)
            for u in range(RING):
                sp.wait_ge(msg_out[u], 16 * ITERS)

            def load_messages(i, first):
                for u in range(RING):
                    g = RING * i + u
                    if not first:
                        sp.wait_ge(seg_out[u], 16 * i)
                    sp.dma_start(seg[:, u, :, :].rearrange("p t c -> p (t c)"),
                                 msg_rows[:, bass.ds(g * RUN, RUN), :].rearrange("p t c -> p (t c)")).then_inc(seg_in[u], 16)
            load_messages(0, True)
            with sp.Fori(1, RUNS // RING) as i:
                load_messages(i, False)

            sp.wait_ge(tab_v, TAB_V)
            for g in range(BG):
                sp.nop().then_inc(counts_out[g], OUTS)

            def load_slots(r, u):
                need = sp.value_load(landed_need[0:1, bass.ds(r, 1)], min_val=1, max_val=ROWS + 1)
                sp.wait_ge(oh_ready, (r + 1) * BG)
                sp.wait_ge(landed, need)
                sp.dma_start(pay[:, u, :, :].rearrange("p s k -> p (s k)"),
                             slots[bass.ds(r * PADDED, PADDED), :].rearrange("(p s) k -> p (s k)", s=BLOCKS)).then_inc(pay_in[u], 16)

            load_slots(0, 0)
            with sp.Fori(0, ROW_LOOPS) as o:
                with sp.If(o * ROW_LOOP < rows):
                    with sp.Fori(0, ROW_LOOP // 2) as j:
                        for u in range(2):
                            r = o * ROW_LOOP + j * 2 + u
                            with sp.If(r < rows):
                                load_slots(nc.s_assert_within(r + 1, 1, SLOT_ROWS, skip_runtime_bounds_check_because="r < rows <= SLOT_ROWS"), 1 - u)
                                last = sp.value_load(last_of_block[0:1, bass.ds(r, 1)], min_val=0, max_val=1)
                                with sp.If(last > 0):
                                    b = sp.value_load(block_of_row[0:1, bass.ds(r, 1)], min_val=0, max_val=BLOCKS - 1)
                                    for g in range(BG):
                                        cols = slice(g * BGW, (g + 1) * BGW)
                                        pairs = slice(g * BGW // 2, (g + 1) * BGW // 2)
                                        wait_copied(sp, r + 1, g, 1)
                                        sp.dma_start(counts[bass.ds(b, 1), :, :, cols].rearrange("a p l c -> (a p) l c"), cacc[:, :, cols]).then_inc(counts_out[g], 16)
                                        sp.wait_ge(conv_ready, b * BG + g + 1)
                                        sp.dma_start(counts8[bass.ds(b, 1), :, :, pairs].rearrange("a p l c -> (a p) l c"), cacc8_pairs[:, :, pairs]).then_inc(counts_out[g], 16)
            for g in range(BG):
                sp.wait_ge(counts_out[g], (BLOCKS + 1) * OUTS)
            sp.nop().then_inc(built, 1)

            def load_lots(k, mat, width):
                for h in range(2):
                    wide = (HALF, BLOCKS - HALF)[h] * width
                    w = k * 2 + h

                    def lot(b, u):
                        sp.wait_ge(big_used, w * BLOCKS + b + 1)
                        sp.dma_start(big[:, u, 0:wide], mat[bass.ds(b, 1), :, 0, h * HALF * width:h * HALF * width + wide]
                                     .rearrange("a p c -> (a p) c")).then_inc(big_in[u], 16)
                    lot(0, 4)
                    with sp.Fori(0, (BLOCKS - 1) // 4) as i:
                        for u in range(4):
                            lot(i * 4 + u + 1, u)

            load_lots(0, counts8, LANES // 2)
            sp.wait_ge(flag_ready, 1)
            over = sp.value_load(capped[0:1, 0:1], min_val=0, max_val=1)
            with sp.If(over > 0):
                with sp.Fori(1, HOPS + 1) as k:
                    load_lots(k, counts, LANES)
            with sp.If(over < 1):
                for u in range(4):
                    sp.nop().then_inc(big_in[u], 2 * 16 * ((BLOCKS - 1) // 4))
                sp.nop().then_inc(big_in[4], 2 * 16)
                with sp.Fori(2, HOPS + 1) as k:
                    load_lots(k, counts8, LANES // 2)

            def load_s2t(mat, wide):
                for b in range(3):
                    sp.dma_start(bigs[b][:, 0:wide], mat[b, :, 1, :]).then_inc(bigs_in[b], 16)
                with sp.Fori(1, BLOCKS // 3) as i:
                    for u in range(3):
                        b = i * 3 + u
                        sp.wait_ge(s2t_mm, b - 2)
                        sp.dma_start(bigs[u][:, 0:wide], mat[bass.ds(b, 1), :, 1, :].rearrange("a p c -> (a p) c")).then_inc(bigs_in[u], 16)
                sp.wait_ge(s2t_mm, BLOCKS - 3)
                sp.dma_start(bigs[0][:, 0:wide], mat[BLOCKS - 1, :, 1, :]).then_inc(bigs_in[0], 16)

            with sp.If(over > 0):
                load_s2t(counts, PADDED)
            with sp.If(over < 1):
                load_s2t(counts8, PADDED // 2)

            sp.wait_ge(act_done, 100)
            sp.dma_start(out[0:(BLOCKS - 1) * LANES, :].rearrange("(b p) f -> p b f", p=LANES), W[:, 0:BLOCKS - 1, :]).then_inc(stored, 16)
            sp.dma_start(out[(BLOCKS - 1) * LANES:NODES, :], W[0:LAST, BLOCKS - 1, :]).then_inc(stored, 16)
            sp.wait_ge(stored, 32)

        @block.gpsimd
        def _(gp):
            gp.iota(row_no[:, :], [[1, SLOT_ROWS_UP]], base=0, channel_multiplier=0, allow_small_or_imprecise_dtypes=True).then_inc(pool_consts, 1)
            gp.iota(lane_no[:, :], [[0, 1]], base=0, channel_multiplier=1, allow_small_or_imprecise_dtypes=True).then_inc(pool_consts, 1)

            last_node, last_slot = gp.to_reg(PADDED - 1), gp.to_reg(SLOT_ROWS_UP * PADDED - 1)

            def gather(i, first=False, last=False):
                for u in range(RING):
                    g, nu = RING * i + u, (u + 1) % RING
                    gp.wait_ge(gidx_ready, g + 1)
                    if not (last and nu == 0):
                        if not (first and nu):
                            gp.wait_ge(edge_v_done, (g + 1 - RING + 1) * 2)
                        gp.tensor_copy(gidx[:, nu, :], src_i[:, bass.ds((g + 1) * TILES, TILES)]).then_inc(gidx_ready, 1)
                    for j in range(TILES):
                        gp.indirect_dma_start(gat[:, u, j, :], None, table,
                                              bass.IndirectOffsetOnAxis(ap=gidx[:, u, j:j + 1], axis=0),
                                              bounds_check=last_node, oob_is_err=False).then_inc(gat_in[u], 16)

            last_row, last_sub, last_edge = gp.to_reg(ROWS - 1), gp.to_reg(EDGES // SUB - 1), gp.to_reg(EDGES - 1)
            gp.wait_ge(lists_out, 32)
            for k, (values, index, last) in enumerate(((dst_firsts, row_i, last_row), (dst_list, sub_i, last_sub))):
                gp.wait_ge(search_v, k + 2)
                for b in range(BLOCKS):
                    gp.indirect_dma_start(steps[:, b, :], None, values, bass.IndirectOffsetOnAxis(ap=index[:, b:b + 1], axis=0),
                                          bounds_check=last, oob_is_err=False).then_inc(steps_in, 16)

            gp.wait_ge(edges_in, 80)
            gp.tensor_copy(gidx[:, 0, :], src_i[:, 0:TILES]).then_inc(gidx_ready, 1)
            gp.wait_ge(table_out, 16)
            gather(0, first=True)
            with gp.Fori(1, GROUPS // RING - 1) as i:
                gather(i)
            gather(GROUPS // RING - 1, last=True)

            def copy_next(r, u):
                gp.tensor_copy(sidx[:, u, :], slot_t[:, :, bass.ds(r, 1)].rearrange("p c a -> p (c a)")).then_inc(sidx_ready, 1)
                gp.tensor_copy(spay[:, u, :, :], lanes_t[:, :, bass.ds(r, 1), :].rearrange("p c a k -> p (c a) k")).then_inc(sidx_ready, 1)

            def with_rest(v, last):
                return v % 2 == 1 or (last and v == DEAL_RING - 1)

            def dealt_by(i, v, last=False):
                return i * (2 * DEAL - 1) + (DEAL - 1 + with_rest(v, last) if v < DEAL_RING else 2 * DEAL - 1)

            def deal(i, first=False, last=False):
                rows = DEAL_RING if last else DEAL_LOOP
                for v in range(rows):
                    r, u = DEAL_LOOP * i + v, v % DEAL_RING
                    for c in range(DEAL - 1 + with_rest(v, last)):
                        if c == COPY_AT:
                            if not (first and v == 0):
                                gp.wait_ge(dealt[(u - 1) % DEAL_RING], 16 * (dealt_by(i, v - 1) if v else i * (2 * DEAL - 1)))
                            if not (last and v == rows - 1):
                                gp.wait_ge(sidx_ready, 2 * r + 4)
                            if not (last and v >= rows - 2):
                                copy_next(r + 2, (u + 2) % DEAL_RING)
                            if not (first and v == 0):
                                gp.nop().then_inc(landed, 1)
                        m = DEAL_REST if c == DEAL - 1 and v % 2 == 0 else LANES
                        gp.indirect_dma_start(slots, bass.IndirectOffsetOnAxis(ap=sidx[0:m, u, c:c + 1], axis=0),
                                              spay[0:m, u, c, :], None,
                                              bounds_check=last_slot, oob_is_err=False).then_inc(dealt[u], 16)

            gp.nop().then_inc(landed, 1)
            gp.wait_ge(filled, 16 * FILLS)
            gp.wait_ge(ranked, 1)
            copy_next(0, 0)
            copy_next(1, 1)
            gp.wait_ge(sidx_ready, 2)
            deal(0, first=True)
            with gp.Fori(1, AGG_AT) as i:
                deal(i)
            for u in range(RING):
                gp.wait_ge(seg_out[u], 16 * (RUNS // RING))
            gp.wait_ge(into_out, 16)
            for b in range(BLOCKS):
                gp.indirect_dma_start(agg[:, b, :], None, sums, bass.IndirectOffsetOnAxis(ap=last_i[:, b:b + 1], axis=0),
                                      bounds_check=last_edge, oob_is_err=False).then_inc(ends_in, 16)
                gp.indirect_dma_start(agg_in[:, b, :], None, row_sums, bass.IndirectOffsetOnAxis(ap=row_i[:, b:b + 1], axis=0),
                                      bounds_check=last_row, oob_is_err=False).then_inc(ends_in, 16)
            with gp.Fori(AGG_AT, DEAL_LAST) as i:
                deal(i)
            deal(DEAL_LAST, last=True)
            for u in range(DEAL_RING):
                gp.wait_ge(dealt[u], 16 * dealt_by(DEAL_LAST, u, True))
            gp.nop().then_inc(landed, 1)

        @block.vector
        def _(v):
            n = 0

            def step(ins):
                nonlocal n
                n += 1
                return ins.then_inc(vec, 1)

            def settled():
                v.wait_ge(vec, n)

            v.memset(prev_i[:, :], -1).then_inc(vec_consts, 1)
            v.memset(next_i[:, :], -1).then_inc(vec_consts, 1)
            v.memset(ones[:, :], 1.0).then_inc(vec_consts, 1)
            v.memset(X[:, :, :], 0.0).then_inc(vec_consts, 1)
            v.memset(xt[:, NODES:PADDED], 0.0).then_inc(vec_consts, 1)
            v.memset(minus1[:, :], -1.0).then_inc(vec_consts, 1)
            v.memset(lanes_t[:, :, :, :], 0.0).then_inc(vec_consts, 1)
            v.wait_ge(pool_consts, 2)
            step(v.tensor_copy(iota[:, :], row_no[:, 0:LANES]))
            step(v.tensor_copy(iota16[:, :], row_no[:, 0:LANES]))
            settled()
            step(v.tensor_scalar(ident[:, :], iota[:, :], lane_no[:, 0:1], None, ALU.is_equal))
            step(v.tensor_scalar(ident16[:, :], iota[:, :], lane_no[:, 0:1], None, ALU.is_equal))
            step(v.tensor_scalar(node_no[:, :], iota[:, 0:BLOCKS], float(LANES), lane_no[:, 0:1], ALU.mult, ALU.add))
            step(v.tensor_scalar(upper[:, :], iota[:, :], lane_no[:, 0:1], None, ALU.is_ge))
            v.wait_ge(edges_in, 80)
            step(v.tensor_scalar(ta.bitcast(I32), src_i, 7, None, ALU.logical_shift_right))
            step(v.tensor_scalar(tb.bitcast(I32), dst_i, 7, None, ALU.logical_shift_right))
            step(v.tensor_scalar(tc.bitcast(I32), prev_i, 7, None, ALU.arith_shift_right))
            step(v.tensor_copy(dst_f, dst_i))
            step(v.tensor_copy(next_f[:, :], next_i[:, :]))
            settled()
            step(v.tensor_copy(sub_firsts[:, :], dst_f.rearrange("p (s t) -> p s t", t=SUB)[:, :, 0]))
            step(v.tensor_scalar(nb_diag[:, :], ident[0:ROWS, 0:ROWS], dst_f[:, 0:1], None, ALU.mult))
            settled()
            v.nop().then_inc(search_v, 1)
            step(v.tensor_copy(sblk[:, :], ta.bitcast(I32)))
            step(v.tensor_copy(dblk[:, :], tb.bitcast(I32)))
            step(v.tensor_copy(ind[:, :], tc.bitcast(I32)))
            settled()
            step(v.tensor_tensor(keep_b[:, :], dblk[:, :], ind[:, :], ALU.is_equal))
            step(v.tensor_copy(ta, prev_i))
            step(v.tensor_tensor(next_f[:, :], dst_f[:, COLS - 1:COLS], next_f[:, :], ALU.is_equal))
            settled()
            step(v.tensor_tensor(tb, dst_f, ta, ALU.is_equal))
            step(v.tensor_scalar(pen[:, COLS:COLS + 1], next_f[:, :], 1.0, -NEG, ALU.subtract, ALU.mult))
            settled()
            step(v.tensor_scalar(pen[:, 0:COLS], tb, 1.0, -NEG, ALU.subtract, ALU.mult))
            step(v.memset(slot_t.rearrange("p c r -> p (c r)"), 0))
            settled()

            def number(o, values, w, b0=0, b1=BLOCKS):
                cmp = picked_mem[:, 0:(b1 - b0) * w].rearrange("p (b c) -> p b c", c=w)
                step(v.tensor_tensor(cmp, values, node_no[:, b0:b1].unsqueeze(2).to_broadcast([LANES, b1 - b0, w]), ALU.is_le))
                settled()
                step(v.tensor_reduce(o[:, b0:b1], cmp, AX.X, ALU.add))
                settled()

            def index(o, scale, base):
                if base is not None:
                    step(v.scalar_tensor_tensor(found[:, :], base, float(scale), found[:, :], ALU.mult, ALU.add))
                    settled()
                step(v.tensor_scalar(found[:, :], found[:, :], -1.0, 0.0, ALU.add, ALU.max))
                settled()
                step(v.tensor_copy(o[:, :], found[:, :]))
                settled()

            v.wait_ge(search_pe, 1)
            step(v.tensor_copy(firsts[:, :], ps[:, 2, 0:ROWS]))
            settled()
            for b0, b1 in ((0, HALF), (HALF, BLOCKS)):
                number(found, firsts[:, :].unsqueeze(1).to_broadcast([LANES, b1 - b0, ROWS]), ROWS, b0, b1)
            index(row_i, 1, None)
            step(v.tensor_copy(row_f[:, :], found[:, :]))
            settled()
            v.nop().then_inc(search_v, 1)
            v.wait_ge(steps_in, 16 * BLOCKS)
            number(found, steps, SUB)
            step(v.tensor_tensor(spans[:, :], steps[:, :, 0], node_no[:, :], ALU.is_equal))
            index(sub_i, SUBS, row_f[:, :])
            step(v.tensor_copy(row_f[:, :], found[:, :]))
            settled()
            v.nop().then_inc(search_v, 1)
            v.wait_ge(steps_in, 32 * BLOCKS)
            number(found, steps, SUB)
            index(last_i, SUB, row_f[:, :])
            cmp = picked_mem[:, 0:BLOCKS * SUB].rearrange("p (b c) -> p b c", c=SUB)
            step(v.tensor_tensor(cmp, steps, node_no[:, :].unsqueeze(2).to_broadcast([LANES, BLOCKS, SUB]), ALU.is_equal))
            settled()
            step(v.tensor_reduce(has[:, :], cmp, AX.X, ALU.max))
            step(v.memset(msgb[:, :, :, DIM:MSGW], 1.0))
            settled()
            v.wait_ge(table_out, 16)

            def edge_group(i, u, first):
                g = RING * i + u
                q = u % 2
                for h in range(2):
                    e = g * 2 + h
                    pv = ps[0:ROWS, 4 + 2 * h:6 + 2 * h, 0:6 * DIM].rearrange("p k (t c) -> p k t c", t=2)
                    cols = slice(h * (TILES // 2), (h + 1) * (TILES // 2))
                    gv = gat[:, u, cols, :].rearrange("p (k t) c -> p k t c", t=2)
                    kv = kk[:, q, cols, :].rearrange("p (k t) c -> p k t c", t=2)
                    mv = mm[:, q, cols, :].rearrange("p (k t) c -> p k t c", t=2)
                    v.wait_ge(edge_mm, e + 1)
                    if h == 0:
                        v.wait_ge(gat_in[u], 16 * TILES * (i + 1))
                    v.tensor_tensor(kv, pv[:, :, :, DIM:2 * DIM], gv[:, :, :, DIM:2 * DIM], ALU.add).then_inc(edge_step, 1)
                    v.tensor_tensor(mv, pv[:, :, :, 0:DIM], gv[:, :, :, 0:DIM], ALU.add).then_inc(edge_step, 1)
                    v.wait_ge(edge_step, 5 * g + 2 * h + 2)
                    v.tensor_tensor(kv, kv, pv[:, :, :, 2 * DIM:3 * DIM], ALU.mult).then_inc(edge_v_done, 1)
                if not first:
                    v.wait_ge(msg_out[u], 16 * i)
                v.scalar_tensor_tensor(msgb[:, u, :, 0:DIM], mm[:, q, :, :], 0.01, mm[:, q, :, :], ALU.mult, ALU.max).then_inc(msg_ready, 1)
                v.wait_ge(edge_v_done, 2 * g + 2)
                v.tensor_reduce(att[:, bass.ds(g * TILES, TILES)], kk[:, q, :, :], AX.X, ALU.add).then_inc(edge_step, 1)

            def rank(s, q):
                v.tensor_scalar(ind[:, :], sblk[:, :], iota[0:ROWS, bass.ds(s, 1)], None, ALU.is_equal).then_inc(rank_step, 1)
                v.wait_ge(rank_step, 3 * s + 1)
                v.tensor_tensor_scan(cnt[:, :], keep_b[:, :], ind[:, :], 0.0, ALU.mult, ALU.add).then_inc(rank_step, 1)
                v.wait_ge(rank_step, 3 * s + 2)
                v.wait_ge(pick_used, s + 1)
                v.tensor_tensor(picked[:, q, :], ind[:, :], cnt[:, :], ALU.mult).then_inc(pick_ready, 1)
                v.tensor_copy(row_last[:, bass.ds(s, 1)], cnt[:, COLS - 1:COLS]).then_inc(rank_step, 1)
                v.wait_ge(rank_step, 3 * s + 3)
                v.wait_ge(pick_ready, s + 1)

            def look_up(values, keys, base, s, q):
                v.wait_ge(pick_used, base + s + 1)
                v.tensor_scalar(picked[:, q, :], keys[:, :], iota[0:ROWS, bass.ds(s, 1)], values[:, bass.ds(s, 1)],
                                ALU.is_equal, ALU.mult).then_inc(pick_ready, 1)

            def histogram(k, q):
                v.wait_ge(hist_used, k + 1)
                for blk, one_hot in ((dblk, oh_d), (sblk, oh_s)):
                    v.tensor_tensor(one_hot[:, q, :, :],
                                    blk[:, bass.ds(k * HIST, HIST)].unsqueeze(2).to_broadcast([ROWS, HIST, BLOCKS]),
                                    iota[0:ROWS, 0:BLOCKS].unsqueeze(1).to_broadcast([ROWS, HIST, BLOCKS]),
                                    ALU.is_equal).then_inc(hist_ready, 1)

            def rank_iter(i, first):
                for u in range(RING):
                    edge_group(i, u, first)
                    if u < STEPS:
                        rank(i * STEPS + u, u)

            rank_iter(0, True)
            with v.Fori(1, RANK_ITERS) as i:
                rank_iter(i, False)
            for u in range(RING):
                edge_group(RANK_ITERS, u, False)
                if u == 0:
                    rank(BLOCKS - 1, 0)
            v.wait_ge(pick_used, BLOCKS + PICKS)
            step(v.tensor_scalar(cnt[:, :].rearrange("p (k c) -> p k c", k=4), ps[0:ROWS, 0:4, 0:COLS // 4], -1.0, None, ALU.add))
            step(v.tensor_tensor_scan(picked[:, 0, :], keep_b[:, :], keep_b[:, :], 1.0, ALU.mult, ALU.mult))
            settled()
            step(v.tensor_copy(keep_b[:, :], picked[:, 0, :]))
            step(v.tensor_copy(no_break[:, :], picked[:, 0, COLS - 1:COLS]))
            settled()
            step(v.tensor_scalar(nb_diag[:, :], ident[0:ROWS, 0:ROWS], no_break[:, 0:1], None, ALU.mult))
            settled()
            v.nop().then_inc(tab_v, 1)
            v.wait_ge(tab_pe, 1)
            step(v.tensor_copy(row_last_t[:, :], ps[0:BLOCKS, 0, 0:ROWS]))
            step(v.tensor_copy(nb_t[:, :], ps[0:BLOCKS, 1, 0:ROWS]))
            step(v.memset(carry_t[:, 0:1], 0.0))
            settled()
            step(v.tensor_tensor_scan(carry_t[:, 1:ROWS + 1], nb_t[:, :], row_last_t[:, :], 0.0, ALU.mult, ALU.add))
            settled()
            v.nop().then_inc(tab_v, 1)
            v.wait_ge(tab_pe, 2)
            step(v.tensor_copy(carry[:, :], ps[0:ROWS, 2, 0:BLOCKS]))
            settled()

            with v.Fori(HIST_AT, HIST_AT + HIST_STEPS // RING) as i:
                for u in range(RING):
                    edge_group(i, u, False)
                    histogram((i - HIST_AT) * RING + u, u % 2)
            for u in range(RING):
                edge_group(CARRY_AT - 1, u, False)
                if u < 2:
                    histogram(HIST_STEPS - 2 + u, u)
            v.wait_ge(hist_used, HIST_STEPS + 2)
            hist = ps[0:BLOCKS, 0, 0:BLOCKS]
            step(v.tensor_reduce(bt[:, 0:1], hist, AX.X, ALU.max))
            settled()
            step(v.tensor_reduce(bt[:, 1:2], hist, AX.X, ALU.add))
            settled()
            step(v.tensor_scalar(bti[:, 0:1], bt[:, 0:1], float(LANES - 1), None, ALU.add))
            settled()
            step(v.tensor_scalar(bti[:, 0:1], bti[:, 0:1], 7, None, ALU.logical_shift_right))
            settled()
            step(v.tensor_scalar(bt[:, 0:1], bti[:, 0:1], 1.0, None, ALU.max))
            settled()
            v.nop().then_inc(tab_v, 1)
            v.wait_ge(tab_pe, 3)
            step(v.tensor_copy(bend[:, :], ps[0:BLOCKS, 1, 0:2]))
            step(v.tensor_copy(n_rows[:, :], ps[0:1, 1, 8:9]))
            settled()
            step(v.tensor_tensor(bstart[:, :], bend[:, :], bt[:, :], ALU.subtract))
            step(v.tensor_copy(row_tmp.bitcast(I32), row_no[0:BLOCKS, 0:ROWS]))
            settled()
            step(v.tensor_scalar(row_tmp.bitcast(I32), row_tmp.bitcast(I32), 1, None, ALU.logical_shift_right))
            settled()
            step(v.tensor_copy(pair_no, row_tmp.bitcast(I32)))
            settled()
            step(v.tensor_scalar(row_tmp, pair_no, 2.0 * COLS, bend[:, 1:2], ALU.mult, ALU.is_lt))
            settled()
            step(v.tensor_reduce(need_v[:, :], row_tmp, AX.X, ALU.add))
            step(v.tensor_scalar(rs_diag[:, :], ident[0:BLOCKS, 0:BLOCKS], bstart[:, 0:1], None, ALU.mult))
            step(v.tensor_scalar(row_cmp, row_no[0:BLOCKS, :], bend[:, 0:1], None, ALU.is_ge))
            settled()
            step(v.tensor_scalar(need_v[:, :], need_v[:, :], 1.0, None, ALU.add))
            settled()
            step(v.tensor_scalar(need_m[:, :], ones[0:BLOCKS, 0:LANES // 2], need_v[:, 0:1], None, ALU.mult))
            settled()
            v.nop().then_inc(tab_v, 1)
            v.wait_ge(tab_pe, 4)
            by4 = lambda t: t.rearrange("p (k c) -> p k c", k=4)
            step(v.tensor_copy(row_start[:, :], ps[0:ROWS, 0, 416:416 + BLOCKS]))
            step(v.tensor_copy(by4(block_of_row), ps[0:1, 0:4, 0:SLOT_ROWS_UP // 4]))
            step(v.tensor_scalar(row_cmp, row_no[0:BLOCKS, :], bstart[:, 0:1], None, ALU.is_equal))
            settled()
            v.nop().then_inc(tab_v, 1)
            v.wait_ge(tab_pe, 5)
            step(v.tensor_scalar(by4(keep_row[:, :]), ps[:, 0:4, 0:SLOT_ROWS_UP // 4], -1.0, 1.0, ALU.mult, ALU.add))
            step(v.tensor_scalar(row_cmp, row_no[0:BLOCKS, :], 1.0, bend[:, 0:1], ALU.add, ALU.is_equal))
            settled()
            v.nop().then_inc(tab_v, 1)
            v.wait_ge(tab_pe, 6)
            step(v.tensor_copy(by4(last_of_block), ps[64:65, 0:4, 0:SLOT_ROWS_UP // 4]))
            step(v.tensor_scalar(row_cmp, row_no[0:BLOCKS, :], bend[:, 0:1], None, ALU.is_ge))
            settled()
            step(v.scalar_tensor_tensor(row_cmp, row_no[0:BLOCKS, :], bstart[:, 0:1], row_cmp, ALU.is_ge, ALU.subtract))
            settled()
            v.nop().then_inc(tab_v, 1)
            v.wait_ge(tab_pe, 7)
            step(v.tensor_scalar(by4(landed_need), ps[32:33, 0:4, 0:SLOT_ROWS_UP // 4], 1.0, None, ALU.max))
            settled()

            def look_iters(at, values, keys, base):
                with v.Fori(at, at + BLOCKS // LOOK) as i:
                    for u in range(RING):
                        edge_group(i, u, False)
                        if u < STEPS:
                            for k in range(2):
                                look_up(values, keys, base, (i - at) * LOOK + 2 * u + k, (2 * u + k) % PICKS)

            look_iters(CARRY_AT, carry, sblk, BLOCKS)
            for u in range(RING):
                edge_group(START_AT - 1, u, False)
                if u == 0:
                    look_up(carry, sblk, BLOCKS, BLOCKS - 1, 0)
            v.wait_ge(pick_used, 2 * BLOCKS + PICKS)
            step(v.tensor_tensor(by4(ind[:, :]), ps[0:ROWS, 0:4, 0:COLS // 4], by4(keep_b[:, :]), ALU.mult))
            settled()
            step(v.tensor_tensor(cnt[:, :], cnt[:, :], ind[:, :], ALU.add))
            settled()
            look_iters(START_AT, row_start, dblk, 2 * BLOCKS)
            look_up(row_start, dblk, 2 * BLOCKS, BLOCKS - 1, 0)
            v.wait_ge(pick_used, 3 * BLOCKS + PICKS)
            step(v.tensor_copy(ta.bitcast(I32), cnt[:, :]))
            settled()
            step(v.tensor_scalar(tb.bitcast(I32), ta.bitcast(I32), 7, None, ALU.logical_shift_right))
            settled()
            step(v.tensor_copy(tc, tb.bitcast(I32)))
            settled()
            step(v.scalar_tensor_tensor(ta, tc, -float(LANES), cnt[:, :], ALU.mult, ALU.add))
            step(v.tensor_tensor(by4(ind[:, :]), ps[0:ROWS, 0:4, 0:COLS // 4], by4(tc), ALU.add))
            settled()
            step(v.scalar_tensor_tensor(tb, ind[:, :], float(PADDED), sblk[:, :], ALU.mult, ALU.add))
            step(v.tensor_copy(cnt[:, :], src_i))
            settled()
            step(v.scalar_tensor_tensor(tc, ta, float(BLOCKS), tb, ALU.mult, ALU.add))
            step(v.scalar_tensor_tensor(ind[:, :], sblk[:, :], -float(LANES), cnt[:, :], ALU.mult, ALU.add))
            step(v.scalar_tensor_tensor(keep_b[:, :], dblk[:, :], -float(LANES), dst_f, ALU.mult, ALU.add))
            settled()
            v.nop().then_inc(turn_v, 1)
            turned = ps[:, 0:4, :].rearrange("p k (c w) -> p (k c) w", w=LANES)
            for k, t in enumerate((slot_t, lanes_t[:, :, :, 0], lanes_t[:, :, :, 1])):
                v.wait_ge(turn_pe, k + 1)
                step(v.tensor_copy(t[:, 0:DEAL - 1, :], turned[:, 0:DEAL - 1, 0:ROWS]))
                rest = t[:, DEAL - 1, 0:EVEN_ROWS].rearrange("p (q k) -> p q k", k=2)
                lower = turned[:, DEAL - 1, 0:EVEN_ROWS].rearrange("p (q k) -> p q k", k=2)
                upper_half = turned[:, DEAL, 0:EVEN_ROWS].rearrange("p (q k) -> p q k", k=2)
                step(v.tensor_copy(rest[0:DEAL_REST, :, 1], lower[0:DEAL_REST, :, 0]))
                step(v.tensor_copy(rest[DEAL_REST:LANES, :, 1], upper_half[DEAL_REST:LANES, :, 1]))
                step(v.tensor_copy(t[0:DEAL_REST, DEAL - 1, ROWS - 1:ROWS], turned[0:DEAL_REST, DEAL - 1, ROWS - 1:ROWS]))
                settled()
                v.nop().then_inc(turn_v, 1)
            v.nop().then_inc(ranked, 1)
            with v.Fori(REST_AT, ITERS) as i:
                for u in range(RING):
                    edge_group(i, u, False)
            v.wait_ge(edge_step, 5 * GROUPS)
            v.wait_ge(msg_ready, GROUPS)
            step(v.tensor_scalar(att, att, float(DIM) ** -0.5, None, ALU.mult))
            settled()

            def passed_on(values, penalties, k, reverse):
                step(v.tensor_copy(edge_v[:, 0:1], values))
                step(v.tensor_reduce(edge_v[:, 1:2], penalties, AX.X, ALU.min))
                settled()
                v.nop().then_inc(line_v, 1)
                v.wait_ge(line_pe, 2 * k + 1)
                step(v.tensor_copy(line[:, :, :], ps[0:1, 0:2, 0:ROWS]))
                step(v.memset(line_c[:, :], NEG))
                settled()
                if reverse:
                    step(v.tensor_tensor_scan(line_c[:, 0:ROWS][:, ::-1], line[:, 1, :][:, ::-1], line[:, 0, :][:, ::-1], NEG, ALU.add, ALU.max))
                else:
                    step(v.tensor_tensor_scan(line_c[:, 1:ROWS + 1], line[:, 1, :], line[:, 0, :], NEG, ALU.add, ALU.max))
                settled()
                v.nop().then_inc(line_v, 1)
                v.wait_ge(line_pe, 2 * k + 2)
                step(v.tensor_copy(edge_in[:, :], ps[0:ROWS, 2, 0:1]))
                settled()

            step(v.tensor_tensor_scan(seg_f, pen[:, 0:COLS], att, NEG, ALU.add, ALU.max))
            settled()
            passed_on(seg_f[:, COLS - 1:COLS], pen[:, 0:COLS], 0, False)
            step(v.tensor_tensor_scan(seg_f, pen[:, 0:COLS], att, edge_in[:, 0:1], ALU.add, ALU.max))
            settled()
            step(v.tensor_tensor_scan(seg_m[:, ::-1], pen[:, 1:COLS + 1][:, ::-1], seg_f[:, ::-1], NEG, ALU.add, ALU.max))
            settled()
            passed_on(seg_m[:, 0:1], pen[:, 1:COLS + 1], 1, True)
            step(v.tensor_tensor_scan(seg_m[:, ::-1], pen[:, 1:COLS + 1][:, ::-1], seg_f[:, ::-1], edge_in[:, 0:1], ALU.add, ALU.max))
            settled()
            step(v.tensor_tensor(seg_f, att, seg_m, ALU.subtract))
            settled()
            v.nop().then_inc(exp_in, 1)
            v.wait_ge(exp_done, 1)

            step(v.tensor_scalar(keep_on[:, :], pen[:, 0:COLS], 0.0, None, ALU.is_ge))
            step(v.tensor_reduce(row_keep[:, :], pen[:, 0:COLS], AX.X, ALU.min))
            settled()
            step(v.tensor_scalar(row_keep[:, :], row_keep[:, :], 0.0, None, ALU.is_ge))
            settled()
            step(v.tensor_scalar(row_diag[:, :], ident[0:ROWS, 0:ROWS], row_keep[:, 0:1], None, ALU.mult))

            def weigh(i, u):
                g = RING * i + u
                v.wait_ge(seg_in[u], 16 * (i + 1))
                v.tensor_tensor(seg[:, u, :, :], seg[:, u, :, :],
                                exp_w[:, bass.ds(g * RUN, RUN)].unsqueeze(2).to_broadcast([ROWS, RUN, MSGW]), ALU.mult).then_inc(weighed, 1)

            def run_sums(i, u, first=False):
                g = RING * i + u
                v.wait_ge(weighed, g + 1)
                if not first:
                    v.wait_ge(scanned, g)
                for c in range(MSGW):
                    ins = v.tensor_tensor_scan(seg[:, u, :, c], keep_on[:, bass.ds(g * RUN, RUN)], seg[:, u, :, c],
                                               0.0 if first else seg[:, (u - 1) % RING, RUN - 1, c:c + 1], ALU.mult, ALU.add)
                ins.then_inc(scanned, 1)

            weigh(0, 0)
            for u in range(RING):
                weigh((u + 1) // RING, (u + 1) % RING)
                run_sums(0, u, first=(u == 0))
            with v.Fori(1, RUNS // RING - 1) as i:
                for u in range(RING):
                    weigh(i + (u + 1) // RING, (u + 1) % RING)
                    run_sums(i, u)
            for u in range(RING):
                if u < RING - 1:
                    weigh(RUNS // RING - 1, u + 1)
                run_sums(RUNS // RING - 1, u)
            v.wait_ge(scanned, RUNS)
            v.nop().then_inc(scanned, 1)

            v.nop().then_inc(line_v, 1)
            v.wait_ge(line_pe, 5)
            step(v.tensor_copy(tail_t[:, :, :], ps[0:MSGW, 0:2, 0:ROWS]))
            step(v.memset(into_t[:, 0:1], 0.0))
            settled()
            step(v.tensor_tensor_scan(into_t[:, 1:ROWS + 1], tail_t[:, 1, :], tail_t[:, 0, :], 0.0, ALU.mult, ALU.add))
            settled()
            v.nop().then_inc(line_v, 1)
            v.wait_ge(line_pe, 6)
            step(v.tensor_scalar(into[:, :], ps[0:ROWS, 2, 0:MSGW], keep_on[:, 0:1], None, ALU.mult))
            settled()
            v.nop().then_inc(line_v, 1)

            def over(a, w=DIM):
                return a.unsqueeze(2).to_broadcast([LANES, BLOCKS, w])

            def feat(a):
                return a.unsqueeze(1).to_broadcast([LANES, BLOCKS, DIM])

            a = 0

            def sqrt_of(t):
                nonlocal a
                settled()
                v.nop().then_inc(act_v, 1)
                a += 1
                v.wait_ge(act_done, a)

            def layer_norm(o, t, eps):
                step(v.tensor_reduce(mean[:, :], t[:, :, :], AX.X, ALU.add))
                settled()
                step(v.tensor_scalar(mean[:, :], mean[:, :], 1.0 / DIM, None, ALU.mult))
                settled()
                step(v.tensor_tensor(o[:, :, :], t[:, :, :], over(mean[:, :]), ALU.subtract))
                settled()
                step(v.tensor_tensor(ylo[:, :, :], o[:, :, :], o[:, :, :], ALU.mult))
                settled()
                step(v.tensor_reduce(var[:, :], ylo[:, :, :], AX.X, ALU.add))
                settled()
                step(v.tensor_scalar(var[:, :], var[:, :], 1.0 / DIM, eps, ALU.mult, ALU.add))
                sqrt_of(var)
                step(v.reciprocal(var[:, :], var[:, :]))
                settled()
                step(v.tensor_tensor(o[:, :, :], o[:, :, :], over(var[:, :]), ALU.mult))
                settled()

            def product_out(k, o, add):
                for q in range(13):
                    w = min(4, BLOCKS - 4 * q)
                    v.wait_ge(nt_mm, 13 * k + q + 1)
                    src_ps = ps[:, 4 + q % 2, 0:w * DIM].rearrange("p (b f) -> p b f", f=DIM)
                    v.tensor_copy(o[:, 4 * q:4 * q + w, :], src_ps).then_inc(nt_out, 1)
                v.wait_ge(nt_out, 13 * (k + 1))

            v.wait_ge(ends_in, 32 * BLOCKS)
            step(v.tensor_tensor(agg_in[:, :, :], agg_in[:, :, :], over(spans[:, :], MSGW), ALU.mult))
            settled()
            step(v.tensor_tensor(agg[:, :, :], agg[:, :, :], agg_in[:, :, :], ALU.add))
            settled()
            step(v.tensor_scalar(den[:, :], agg[:, :, DIM], 1.0, None, ALU.max))
            settled()
            step(v.reciprocal(den[:, :], den[:, :]))
            settled()
            step(v.tensor_tensor(den[:, :], den[:, :], has[:, :], ALU.mult))
            settled()
            step(v.tensor_tensor(Z[:, :, 0:DIM], agg[:, :, 0:DIM], over(den[:, :]), ALU.mult))
            settled()
            v.nop().then_inc(nt_ready, 1)
            product_out(0, Y, None)
            step(v.scalar_tensor_tensor(Y[:, :, :], Y[:, :, :], 0.01, Y[:, :, :], ALU.mult, ALU.max))
            settled()
            step(v.tensor_tensor(Y[:, :, :], Y[:, :, :], X[:, :, :], ALU.add))
            settled()
            layer_norm(W, Y, 1e-6)
            step(v.tensor_tensor(W[:, :, :], W[:, :, :], feat(gam[:, :]), ALU.mult))
            settled()
            step(v.tensor_tensor(W[:, :, :], W[:, :, :], feat(bet[:, :]), ALU.add))
            settled()
            step(v.tensor_tensor(W[:, :, :], W[:, :, :], over(has[:, :]), ALU.mult))
            step(v.tensor_scalar(mean[:, :], has[:, :], -1.0, 1.0, ALU.mult, ALU.add))
            settled()
            step(v.tensor_tensor(Y[:, :, :], X[:, :, :], over(mean[:, :]), ALU.mult))
            settled()
            step(v.tensor_tensor(W[:, :, :], W[:, :, :], Y[:, :, :], ALU.add))
            settled()
            step(v.tensor_tensor(W[:, :, :], W[:, :, :], X[:, :, :], ALU.add))
            settled()
            layer_norm(X, W, 1e-5)

            step(v.tensor_copy(lanes_rep[:, :, :], iota[:, :].unsqueeze(2).to_broadcast([LANES, LANES, 2 * BG])))
            step(v.memset(cacc[:, :, :], 0.0))
            settled()
            v.nop().then_inc(tab_v, 1)
            rows = v.value_load(n_rows[0:1, 0:1], min_val=1, max_val=SLOT_ROWS)
            v.nop().then_inc(oh_ready, 2 * BG)
            with v.Fori(0, ROW_LOOPS) as o:
                with v.If(o * ROW_LOOP < rows):
                    with v.Fori(0, ROW_LOOP // 2) as j:
                        for u in range(2):
                            r = o * ROW_LOOP + j * 2 + u
                            with v.If(r < rows):
                                v.wait_ge(pay_in[u], (o * (ROW_LOOP // 2) + j + 1) * 16)
                                b = v.value_load(block_of_row[0:1, bass.ds(r, 1)], min_val=0, max_val=BLOCKS - 1)
                                last = v.value_load(last_of_block[0:1, bass.ds(r, 1)], min_val=0, max_val=1)
                                v.tensor_scalar(keep_diag[:, u, :], ident16[:, :], keep_row[:, bass.ds(r, 1)], None, ALU.mult).then_inc(keep_ready, 1)
                                for g in range(BG):
                                    q = (BG * u + g) % 2
                                    v.wait_ge(tile_mm, r * (2 * BG) + 2 * g + 2)
                                    v.tensor_tensor(oh[:, q, :, :],
                                                    pay[:, u, g * BG:(g + 1) * BG, :].rearrange("p s k -> p (s k)").unsqueeze(1).to_broadcast([LANES, LANES, 2 * BG]),
                                                    lanes_rep[:, :, :], ALU.is_equal).then_inc(oh_ready, 1)
                                    if g in caps:
                                        with v.If(last > 0):
                                            for d in caps[g]:
                                                cols = slice(d * BGW, (d + 1) * BGW)
                                                v.wait_ge(counts_out[d], (b + 1) * OUTS)
                                                wait_copied(v, r + 1, d, 1)
                                                v.nop().then_inc(conv_begun, 1)
                                                v.tensor_scalar(cacc8[:, :, cols], cacc[:, :, cols], CAP, None, ALU.min, saturate=False).then_inc(conv_ready, 1)
            v.wait_ge(built, 1)

            step(v.memset(xs[:, :, 2 * DIM:2 * DIM + 1], 1.0))
            settled()

            def split(t):
                step(v.tensor_scalar(xs[:, :, 0:DIM], t[:, :, :], SCALE, None, ALU.mult))
                settled()
                step(v.scalar_tensor_tensor(xs[:, :, DIM:2 * DIM], t[:, :, :], SCALE, xs[:, :, 0:DIM], ALU.mult, ALU.subtract))
                settled()
                v.nop().then_inc(xs_ready, 1)

            def features(w):
                def block(b, u):
                    v.wait_ge(big_used, w * BLOCKS + b + 1)
                    v.tensor_copy(feats_now[:, u, :], xs[:, bass.ds(b, 1), :].rearrange("p a c -> p (a c)")).then_inc(feats_ready, 1)
                block(0, 4)
                with v.Fori(0, (BLOCKS - 1) // 4) as i:
                    for u in range(4):
                        block(i * 4 + u + 1, u)

            def sweep(w, degrees=False):
                features(w)
                h = w % 2
                b0, b1 = ((0, HALF), (HALF, BLOCKS))[h]
                v.wait_ge(lo_copied, w + 1)
                if degrees:
                    def three(t):
                        return t[:, b0:b0 + 24, :].rearrange("p (k j) c -> p k j c", j=3)
                    v.tensor_copy(deg[:, b0:b0 + 24].rearrange("p (k j) -> p k j", j=3), by3[:, :, :, 2 * DIM])
                    if h == 0:
                        v.tensor_copy(deg[:, 24:25], ps[:, 1, REST + DIM:REST + DIM + 1])
                        v.scalar_tensor_tensor(Y[:, 24, :], ps[:, 0, REST:REST + DIM], 1.0 / SCALE, ylo[:, 24, :], ALU.mult, ALU.add)
                    for j in range(3):
                        ins = v.scalar_tensor_tensor(three(Y)[:, :, j, :], by3[:, :, j, 0:DIM], 1.0 / SCALE, three(ylo)[:, :, j, :], ALU.mult, ALU.add)
                    ins.then_inc(sweep_read, 1)
                    return
                pv = ps[:, 0:7, :].rearrange("p k (b c) -> p (k b) c", c=LANES)[:, 0:b1 - b0, :]
                v.scalar_tensor_tensor(Y[:, b0:b1, :], pv[:, :, 0:DIM], 1.0 / SCALE, ylo[:, b0:b1, :], ALU.mult, ALU.add).then_inc(sweep_read, 1)

            v.nop().then_inc(sweep_read, 1)
            split(X)
            step(v.tensor_copy(total[:, :, :], X[:, :, :]))
            for hop in range(3):
                w = 2 * hop + (2 if hop else 0)
                sweep(w, hop == 0)
                sweep(w + 1, hop == 0)
                v.wait_ge(sweep_read, w + 3)
                if hop == 0:
                    step(v.tensor_reduce(lane_deg[:, :], deg[:, :], AX.X, ALU.add))
                    settled()
                    v.nop().then_inc(flag_v, 1)
                    v.wait_ge(flag_pe, 1)
                    step(v.tensor_scalar(capped[:, :], ps[0:1, 7, 64:65], float(EDGES), None, ALU.is_lt))
                    settled()
                    v.nop().then_inc(flag_ready, 1)
                    v.nop().then_inc(xs_ready, 1)
                    over16 = v.value_load(capped[0:1, 0:1], min_val=0, max_val=1)
                    with v.If(over16 > 0):
                        sweep(2, True)
                        sweep(3, True)
                    with v.If(over16 < 1):
                        v.nop().then_inc(sweep_read, 2)
                        v.nop().then_inc(feats_ready, 2 * BLOCKS)
                    v.wait_ge(sweep_read, 5)
                if hop == 0:
                    step(v.tensor_scalar(has[:, :], deg[:, :], 0.0, None, ALU.is_gt))
                    settled()
                    step(v.tensor_scalar(mean[:, :], deg[:, :], 1.0, None, ALU.max))
                    settled()
                    step(v.reciprocal(cnt_d[:, :], mean[:, :]))
                    settled()
                    step(v.tensor_tensor(deg_inv[:, :], cnt_d[:, :], has[:, :], ALU.mult))
                    step(v.tensor_copy(var[:, :], cnt_d[:, :]))
                    sqrt_of(var)
                    step(v.tensor_tensor(deg_rsq[:, :], var[:, :], has[:, :], ALU.mult))
                    settled()
                step(v.tensor_tensor(Y[:, :, :], Y[:, :, :], over(deg_inv[:, :]), ALU.mult))
                settled()
                if hop < 2:
                    split(Y)
                step(v.tensor_tensor(total[:, :, :], total[:, :, :], Y[:, :, :], ALU.add))
                settled()
            step(v.scalar_tensor_tensor(X[:, :, :], total[:, :, :], 0.25, X[:, :, :], ALU.mult, ALU.add))
            settled()
            layer_norm(X, X, 1e-5)
            step(v.tensor_tensor(W[:, :, :], X[:, :, :], over(deg_rsq[:, :]), ALU.mult))
            settled()
            split(W)
            sweep(8)
            sweep(9)
            v.wait_ge(sweep_read, 11)
            step(v.tensor_tensor(Y[:, :, :], Y[:, :, :], over(deg_rsq[:, :]), ALU.mult))
            settled()
            step(v.tensor_tensor(X[:, :, :], X[:, :, :], Y[:, :, :], ALU.add))
            settled()
            layer_norm(X, X, 1e-5)
            split(X)
            sweep(10)
            sweep(11)
            v.wait_ge(sweep_read, 13)
            step(v.tensor_tensor(Y[:, :, :], Y[:, :, :], over(deg_inv[:, :]), ALU.mult))
            step(v.tensor_copy(Z[:, :, 0:DIM], X[:, :, :]))
            settled()

            def s2t(b, q):
                v.wait_ge(s2t_lo, b + 1)
                v.scalar_tensor_tensor(W[:, bass.ds(b, 1), :].rearrange("p a c -> p (a c)"), ps[:, q, 0:DIM], 1.0 / SCALE,
                                       ylo[:, bass.ds(b, 1), :].rearrange("p a c -> p (a c)"), ALU.mult, ALU.add).then_inc(s2t_read, 1)
            v.nop().then_inc(s2t_read, 2)
            with v.Fori(0, BLOCKS // 2) as i:
                for q in range(2):
                    s2t(i * 2 + q, q)
            s2t(BLOCKS - 1, 0)
            v.wait_ge(s2t_read, BLOCKS + 2)
            step(v.tensor_scalar(cnt_d[:, :], cnt_d[:, :], 1.0, None, ALU.max))
            settled()
            step(v.reciprocal(cnt_d[:, :], cnt_d[:, :]))
            settled()
            step(v.tensor_tensor(W[:, :, :], W[:, :, :], over(cnt_d[:, :]), ALU.mult))
            settled()
            step(v.tensor_tensor(Z[:, :, DIM:2 * DIM], Y[:, :, :], W[:, :, :], ALU.add))
            settled()
            v.nop().then_inc(nt_ready, 1)
            product_out(1, Y, None)
            step(v.tensor_tensor(Y[:, :, :], Y[:, :, :], feat(bl[:, :]), ALU.add))
            settled()
            step(v.tensor_tensor(Y[:, :, :], Y[:, :, :], X[:, :, :], ALU.add))
            settled()
            layer_norm(W, Y, 1e-5)
            v.nop().then_inc(act_done, 100 - a)

        @block.scalar
        def _(sc):
            sc.wait_ge(search_v, 1)
            sc.dma_start(dst_firsts, sub_firsts[:, :]).then_inc(lists_out, 16)
            sc.dma_start(dst_list.rearrange("(p s) t -> p (s t)", s=SUBS), dst_f).then_inc(lists_out, 16)

            for q in range(BLOCKS // 4 + 1):
                w = min(4, BLOCKS - 4 * q)
                sc.wait_ge(proj_pe, q + 1)
                sc.activation(proj[:, 4 * q:4 * q + w, :], ps[:, q % 2, 0:w * 2 * DIM].rearrange("p (b f) -> p b f", f=2 * DIM), ACT.Copy).then_inc(proj_act, 1)

            def store(i):
                for u in range(RING):
                    g = RING * i + u
                    sc.wait_ge(msg_ready, g + 1)
                    sc.dma_start(msg_rows[:, bass.ds(g * TILES, TILES), :], msgb[:, u, :, :]).then_inc(msg_out[u], 16)
            with sc.Fori(0, GROUPS // RING) as i:
                store(i)
            sc.wait_ge(exp_in, 1)
            sc.activation(exp_w, seg_f, ACT.Exp).then_inc(exp_done, 2)

            with sc.Fori(0, RUNS // RING) as i:
                for u in range(RING):
                    g = RING * i + u
                    sc.wait_ge(scanned, g + 2)
                    sc.dma_start(sum_rows[:, bass.ds(g * RUN, RUN), :].rearrange("p t c -> p (t c)"),
                                 seg[:, u, :, :].rearrange("p t c -> p (t c)")).then_inc(seg_out[u], 16)
            sc.wait_ge(line_v, 7)
            sc.dma_start(row_sums, into[:, :]).then_inc(into_out, 16)

            def product_copies(k, part):
                for q in range(13):
                    w = min(4, BLOCKS - 4 * q)
                    sc.wait_ge(nt_t, 13 * k + q + 1)
                    if q >= 2 or k:
                        sc.wait_ge(nt_mm, 13 * k + q - 1)
                    sc.activation(zt[0:part, q % 2, 0:w * LANES], ps[0:part, 2 + q % 2, 0:w * LANES], ACT.Copy).then_inc(nt_copied, 1)

            def sqrt(t, k):
                sc.wait_ge(act_v, k)
                sc.activation(t[:, :], t[:, :], ACT.Sqrt).then_inc(act_done, 1)

            product_copies(0, DIM)
            sqrt(var, 1)
            sqrt(var, 2)

            sc.wait_ge(tab_v, TAB_V)
            rows = sc.value_load(n_rows[0:1, 0:1], min_val=1, max_val=SLOT_ROWS)
            with sc.Fori(0, ROW_LOOPS) as o:
                with sc.If(o * ROW_LOOP < rows):
                    with sc.Fori(0, ROW_LOOP // 2) as j:
                        for u in range(2):
                            r = o * ROW_LOOP + j * 2 + u
                            with sc.If(r < rows):
                                b = sc.value_load(block_of_row[0:1, bass.ds(r, 1)], min_val=0, max_val=BLOCKS - 1)
                                for g, l in ways:
                                    q = (BG * u + g) % 2
                                    if l == 0:
                                        sc.wait_ge(counts_out[g], (b + 1) * OUTS)
                                    sc.wait_ge(tile_mm, r * (2 * BG) + 2 * g + l + 1 + JOB_CREDIT)
                                    sc.activation(cacc[:, l, g * BGW:(g + 1) * BGW],
                                                  ps[:, 4 * q + 2 * l:4 * q + 2 * l + 2, :].rearrange("p k c -> p (k c)")[:, 0:BGW], ACT.Copy).then_inc(tile_copied, 1)

            def low(w, degrees=False):
                h = w % 2
                b0, b1 = ((0, HALF), (HALF, BLOCKS))[h]
                sc.wait_ge(sweep_mm, w + 1)
                if degrees:
                    if h == 0:
                        sc.activation(ylo[:, 24, :], ps[:, 1, REST:REST + DIM], ACT.Copy, scale=1.0 / SCALE)
                    for j in range(3):
                        ins = sc.activation(ylo[:, b0:b0 + 24, :].rearrange("p (k j) c -> p k j c", j=3)[:, :, j, :],
                                            by3[:, :, j, DIM:2 * DIM], ACT.Copy, scale=1.0 / SCALE)
                    ins.then_inc(lo_copied, 1)
                    return
                pv = ps[:, 0:7, :].rearrange("p k (b c) -> p (k b) c", c=LANES)[:, 0:b1 - b0, :]
                sc.activation(ylo[:, b0:b1, :], pv[:, :, DIM:2 * DIM], ACT.Copy, scale=1.0 / SCALE).then_inc(lo_copied, 1)

            k = 3
            low(0, True)
            low(1, True)
            sc.wait_ge(flag_ready, 1)
            over = sc.value_load(capped[0:1, 0:1], min_val=0, max_val=1)
            with sc.If(over > 0):
                low(2, True)
                low(3, True)
            with sc.If(over < 1):
                sc.nop().then_inc(lo_copied, 2)
            for w in range(3, 2 * HOPS + 2):
                if w > 3:
                    low(w)
                if w in (3, 7, 9):
                    sqrt(var, k)
                    k += 1

            def s2t_low(b, q):
                sc.wait_ge(s2t_mm, b + 1)
                sc.activation(ylo[:, bass.ds(b, 1), :].rearrange("p a c -> p (a c)"), ps[:, q, DIM:2 * DIM], ACT.Copy, scale=1.0 / SCALE)
                sc.activation(cnt_d[:, bass.ds(b, 1)], ps[:, q, 2 * DIM:2 * DIM + 1], ACT.Copy).then_inc(s2t_lo, 1)
            with sc.Fori(0, BLOCKS // 2) as i:
                for q in range(2):
                    s2t_low(i * 2 + q, q)
            s2t_low(BLOCKS - 1, 0)
            product_copies(1, LANES)
            sqrt(var, k)

        @block.tensor
        def _(pe):
            pe.nop().then_inc(pick_used, PICKS)
            pe.nop().then_inc(hist_used, 2)
            pe.wait_ge(search_v, 1)
            pe.matmul(ps[:, 2, 0:ROWS], ones[0:ROWS, :], nb_diag[:, :], start=True, stop=True).then_inc(search_pe, 1)
            pe.wait_ge(x_in, 48)
            pe.wait_ge(consts_in, 16 * 9)
            for q in range(BLOCKS // 4 + 1):
                if q >= 2:
                    pe.wait_ge(proj_act, q - 1)
                for b in range(4 * q, min(4 * q + 4, BLOCKS)):
                    m = pe.matmul(ps[:, q % 2, (b - 4 * q) * 2 * DIM:(b - 4 * q + 1) * 2 * DIM], xt[:, b * LANES:(b + 1) * LANES], w_node[:, :], start=True, stop=True)
                m.then_inc(proj_pe, 1)
            pe.wait_ge(proj_act, BLOCKS // 4 + 1)

            def edge_group(i, u, first):
                g = RING * i + u
                pe.wait_ge(kf_in[u], 16 * (i + 1))
                pe.wait_ge(qf_in[u], 16 * (i + 1))
                for h in range(2):
                    if not (first and u == 0):
                        pe.wait_ge(edge_v_done, g * 2 + h - 1)
                    for c in range(TILES // 2):
                        t = h * (TILES // 2) + c
                        o = ps[0:ROWS, 4 + t // 2, (t % 2) * 3 * DIM:(t % 2 + 1) * 3 * DIM]
                        pe.matmul(o[:, 0:2 * DIM], kf[h * DIM:(h + 1) * DIM, u, c * ROWS:(c + 1) * ROWS], w_edge[h * DIM:(h + 1) * DIM, :], start=True, stop=True)
                        m = pe.matmul(o[:, 2 * DIM:3 * DIM], qf[:, u, t * ROWS:(t + 1) * ROWS], wq[:, :], start=True, stop=True)
                    m.then_inc(edge_mm, 1)

            def add_picked(s, q, first, base):
                pe.wait_ge(pick_ready, s + base + 1)
                for k in range(4):
                    m = pe.matmul(ps[0:ROWS, k, 0:COLS // 4], ident[0:ROWS, 0:ROWS], picked[:, q, k * (COLS // 4):(k + 1) * (COLS // 4)],
                                  start=first, stop=False, skip_group_check=True)
                m.then_inc(pick_used, 1)

            def rank_iter(i, first):
                edge_group(i, 0, first)
                for u in range(STEPS):
                    edge_group(i, u + 1, first)
                    add_picked(i * STEPS + u, u, first and u == 0, 0)

            rank_iter(0, True)
            with pe.Fori(1, RANK_ITERS) as i:
                rank_iter(i, False)
            edge_group(RANK_ITERS, 0, False)
            edge_group(RANK_ITERS, 1, False)
            add_picked(BLOCKS - 1, 0, False, 0)
            edge_group(RANK_ITERS, 2, False)
            edge_group(RANK_ITERS, 3, False)
            pe.wait_ge(tab_v, 1)
            pe.wait_ge(rank_step, 3 * BLOCKS)
            pe.transpose(ps[0:BLOCKS, 0, 0:ROWS], row_last[:, :], ident[0:ROWS, 0:ROWS])
            pe.matmul(ps[0:BLOCKS, 1, 0:ROWS], ones[0:ROWS, 0:BLOCKS], nb_diag[:, :], start=True, stop=True).then_inc(tab_pe, 1)
            pe.wait_ge(tab_v, 2)
            pe.transpose(ps[0:ROWS, 2, 0:BLOCKS], carry_t[:, 0:ROWS], ident[0:BLOCKS, 0:BLOCKS]).then_inc(tab_pe, 1)

            def histogram(k, q, first):
                pe.wait_ge(hist_ready, 2 * k + 2)
                for t in range(HIST):
                    m = pe.matmul(ps[0:BLOCKS, 0, 0:BLOCKS], oh_d[:, q, t, :], oh_s[:, q, t, :], start=(first and t == 0), stop=False, skip_group_check=True)
                m.then_inc(hist_used, 1)

            def hist_iter(i, first):
                edge_group(i, 0, False)
                for u in range(RING - 1):
                    edge_group(i, u + 1, False)
                    histogram((i - HIST_AT) * RING + u, u % 2, first and u == 0)
                histogram((i - HIST_AT) * RING + RING - 1, (RING - 1) % 2, False)
            hist_iter(HIST_AT, True)
            with pe.Fori(HIST_AT + 1, HIST_AT + HIST_STEPS // RING) as i:
                hist_iter(i, False)
            edge_group(CARRY_AT - 1, 0, False)
            edge_group(CARRY_AT - 1, 1, False)
            histogram(HIST_STEPS - 2, 0, False)
            edge_group(CARRY_AT - 1, 2, False)
            histogram(HIST_STEPS - 1, 1, False)
            edge_group(CARRY_AT - 1, 3, False)
            pe.wait_ge(tab_v, 3)
            pe.matmul(ps[0:BLOCKS, 1, 0:2], upper[0:BLOCKS, 0:BLOCKS], bt[:, :], start=True, stop=True)
            pe.matmul(ps[0:1, 1, 8:9], ones[0:BLOCKS, 0:1], bt[:, 0:1], start=True, stop=True).then_inc(tab_pe, 1)
            quarter = SLOT_ROWS_UP // 4

            def over_rows(values, partitions):
                for k in range(4):
                    m = pe.matmul(ps[0:partitions, k, 0:quarter], values, row_cmp[:, k * quarter:(k + 1) * quarter], start=True, stop=True)
                m.then_inc(tab_pe, 1)
            pe.wait_ge(tab_v, 4)
            pe.matmul(ps[0:ROWS, 0, 416:416 + BLOCKS], ones[0:BLOCKS, 0:ROWS], rs_diag[:, :], start=True, stop=True)
            over_rows(ones[0:BLOCKS, :], LANES)
            pe.wait_ge(tab_v, 5)
            over_rows(ones[0:BLOCKS, :], LANES)
            pe.wait_ge(tab_v, 6)
            over_rows(ones[0:BLOCKS, :], LANES)
            pe.wait_ge(tab_v, 7)
            over_rows(need_m[:, :], LANES // 2)

            def look_iter(i, at, base, first):
                edge_group(i, 0, False)
                for u in range(STEPS):
                    edge_group(i, u + 1, False)
                    for k in range(2):
                        add_picked((i - at) * LOOK + 2 * u + k, (2 * u + k) % PICKS, first and u == 0 and k == 0, base)

            def look_iters(at, base):
                look_iter(at, at, base, True)
                with pe.Fori(at + 1, at + BLOCKS // LOOK) as i:
                    look_iter(i, at, base, False)
            look_iters(CARRY_AT, BLOCKS)
            edge_group(START_AT - 1, 0, False)
            edge_group(START_AT - 1, 1, False)
            add_picked(BLOCKS - 1, 0, False, BLOCKS)
            edge_group(START_AT - 1, 2, False)
            edge_group(START_AT - 1, 3, False)
            look_iters(START_AT, 2 * BLOCKS)
            add_picked(BLOCKS - 1, 0, False, 2 * BLOCKS)

            turned = ps[:, 0:4, :].rearrange("p k (c w) -> p (k c) w", w=LANES)
            for k, t in enumerate((tc, ind[:, :], keep_b[:, :])):
                pe.wait_ge(turn_v, k + 1)
                for c in range(DEAL):
                    n = LANES if c < DEAL - 1 else DEAL_REST
                    pe.transpose(turned[0:n, c, 0:ROWS], t[:, c * LANES:c * LANES + n], ident[0:ROWS, 0:ROWS])
                m = pe.transpose(turned[:, DEAL, 0:ROWS], t[:, COLS - LANES:COLS], ident[0:ROWS, 0:ROWS])
                m.then_inc(turn_pe, 1)
            with pe.Fori(REST_AT, ITERS) as i:
                for u in range(RING):
                    edge_group(i, u, False)

            for k in range(2):
                pe.wait_ge(line_v, 2 * k + 1)
                pe.transpose(ps[0:1, 0, 0:ROWS], edge_v[:, 0:1], ident[0:ROWS, 0:ROWS])
                pe.transpose(ps[0:1, 1, 0:ROWS], edge_v[:, 1:2], ident[0:ROWS, 0:ROWS]).then_inc(line_pe, 1)
                pe.wait_ge(line_v, 2 * k + 2)
                pe.transpose(ps[0:ROWS, 2, 0:1], line_c[:, k:k + ROWS], ident[0:1, 0:1]).then_inc(line_pe, 1)

            pe.wait_ge(line_v, 5)
            pe.transpose(ps[0:MSGW, 0, 0:ROWS], seg[:, RING - 1, RUN - 1, :], ident[0:ROWS, 0:ROWS])
            pe.matmul(ps[0:MSGW, 1, 0:ROWS], ones[0:ROWS, 0:MSGW], row_diag[:, :], start=True, stop=True).then_inc(line_pe, 1)
            pe.wait_ge(line_v, 6)
            pe.transpose(ps[0:ROWS, 2, 0:MSGW], into_t[:, 0:ROWS], ident[0:MSGW, 0:MSGW]).then_inc(line_pe, 1)

            def node_product(k, part, w_t):
                pe.wait_ge(nt_ready, k + 1)
                for q in range(13):
                    n = min(4, BLOCKS - 4 * q)
                    if q >= 2:
                        pe.wait_ge(nt_copied, 13 * k + q - 1)
                    for b in range(n):
                        m = pe.transpose(ps[0:part, 2 + q % 2, b * LANES:(b + 1) * LANES], Z[:, 4 * q + b, 0:part], ident[:, :])
                    m.then_inc(nt_t, 1)
                    pe.wait_ge(nt_copied, 13 * k + q + 1)
                    if q >= 2:
                        pe.wait_ge(nt_out, 13 * k + q - 1)
                    for b in range(n):
                        m = pe.matmul(ps[:, 4 + q % 2, b * DIM:(b + 1) * DIM], zt[0:part, q % 2, b * LANES:(b + 1) * LANES], w_t, start=True, stop=True)
                    m.then_inc(nt_mm, 1)
            node_product(0, DIM, wo[:, :])

            pe.nop().then_inc(tile_mm, JOB_CREDIT)
            pe.nop().then_inc(tile_copied, len(ways))
            pe.wait_ge(nt_out, 13)
            pe.wait_ge(tab_v, TAB_V)
            rows = pe.value_load(n_rows[0:1, 0:1], min_val=1, max_val=SLOT_ROWS)
            with pe.Fori(0, ROW_LOOPS) as o:
                with pe.If(o * ROW_LOOP < rows):
                    with pe.Fori(0, ROW_LOOP // 2) as j:
                        for u in range(2):
                            r = o * ROW_LOOP + j * 2 + u
                            with pe.If(r < rows):
                                pe.wait_ge(keep_ready, r + 1)
                                for g in range(BG):
                                    q = (BG * u + g) % 2
                                    pe.wait_ge(oh_ready, (r + 2) * BG + g + 1)
                                    for l in range(2):
                                        wait_copied(pe, r + 1 if g >= 2 else r, (g - 2) % BG, l)
                                        first_bank = 4 * q + 2 * l
                                        pe.matmul(ps[:, first_bank, :], keep_diag[:, u, :], cacc[:, l, g * BGW:g * BGW + 512],
                                                  start=True, stop=False, skip_group_check=True)
                                        pe.matmul(ps[:, first_bank + 1, 0:BGW - 512], keep_diag[:, u, :], cacc[:, l, g * BGW + 512:(g + 1) * BGW],
                                                  start=True, stop=False, skip_group_check=True)
                                        for s in range(BG):
                                            m = pe.matmul(ps[:, first_bank + s // 4, (s % 4) * LANES:(s % 4 + 1) * LANES],
                                                          oh[:, q, :, 2 * s + 1 - l], oh[:, q, :, 2 * s + l],
                                                          start=False, stop=(s in (3, BG - 1)), skip_group_check=True)
                                        m.then_inc(tile_mm, 1)

            pe.nop().then_inc(big_used, 4)

            def hop_sweeps(k, bufs, degrees):
                pe.wait_ge(xs_ready, k + 1)
                for h in range(2):
                    w = k * 2 + h
                    n = (HALF, BLOCKS - HALF)[h]
                    pe.wait_ge(sweep_read, w + 1)

                    def block(b, u, first):
                        pe.wait_ge(feats_ready, w * BLOCKS + b + 1)
                        pe.nop().then_inc(lot_begun, 1)
                        for s in range(n):
                            tile = bufs[:, u, s * LANES:(s + 1) * LANES]
                            if not degrees:
                                m = pe.matmul(ps[:, s // 4, (s % 4) * LANES:(s % 4 + 1) * LANES], tile, feats_now[:, u, 0:2 * DIM],
                                              start=(first and s % 4 == 0), stop=False, skip_group_check=True)
                            elif s < 24:
                                m = pe.matmul(ps[:, s // 3, (s % 3) * WIDE:(s % 3 + 1) * WIDE], tile, feats_now[:, u, :],
                                              start=(first and s % 3 == 0), stop=False, skip_group_check=True)
                            else:
                                pe.matmul(ps[:, 0, REST:REST + DIM], tile, feats_now[:, u, 0:DIM], start=False, stop=False, skip_group_check=True)
                                m = pe.matmul(ps[:, 1, REST:REST + DIM + 1], tile, feats_now[:, u, DIM:WIDE], start=False, stop=False, skip_group_check=True)
                        m.then_inc(big_used, 1)
                        return m
                    pe.wait_ge(big_in[4], (w + 1) * 16)
                    block(0, 4, True)
                    with pe.Fori(0, (BLOCKS - 1) // 4) as i:
                        for u in range(4):
                            pe.wait_ge(big_in[u], (w * ((BLOCKS - 1) // 4) + i + 1) * 16)
                            block(i * 4 + u + 1, u, False)
                    pe.wait_ge(big_used, (w + 1) * BLOCKS + 4)
                    pe.nop().then_inc(sweep_mm, 1)

            pe.wait_ge(built, 1)
            hop_sweeps(0, big8, True)
            pe.wait_ge(flag_v, 1)
            pe.matmul(ps[0:1, 7, 64:65], lane_deg[:, :], ones[:, 0:1], start=True, stop=True, skip_group_check=True).then_inc(flag_pe, 1)
            pe.wait_ge(flag_ready, 1)
            over = pe.value_load(capped[0:1, 0:1], min_val=0, max_val=1)
            with pe.If(over > 0):
                hop_sweeps(1, big, True)
                with pe.Fori(2, HOPS + 1) as k:
                    hop_sweeps(k, big, False)
            with pe.If(over < 1):
                pe.nop().then_inc(big_used, 2 * BLOCKS)
                pe.nop().then_inc(sweep_mm, 2)
                with pe.Fori(2, HOPS + 1) as k:
                    hop_sweeps(k, big8, False)

            pe.wait_ge(sweep_read, 2 * HOPS + 3)

            def s2t(bufs, b, slot, q, use):
                pe.wait_ge(bigs_in[slot], use * 16)
                pe.wait_ge(s2t_read, b + 1)
                pe.nop().then_inc(lot_begun, 1)
                for s in range(BLOCKS):
                    m = pe.matmul(ps[:, q, 0:2 * DIM + 1], bufs[slot][:, s * LANES:(s + 1) * LANES], xs[:, s, :],
                                  start=(s == 0), stop=(s == BLOCKS - 1))
                m.then_inc(s2t_mm, 1)
            def all_s2t(bufs):
                with pe.Fori(0, BLOCKS // 6) as i:
                    for u in range(6):
                        s2t(bufs, i * 6 + u, u % 3, u % 2, i * 2 + u // 3 + 1)
                s2t(bufs, BLOCKS - 1, 0, 0, BLOCKS // 3 + 1)
            with pe.If(over > 0):
                all_s2t(bigs)
            with pe.If(over < 1):
                all_s2t(bigs8)
            node_product(1, LANES, wl[:, :])


def kernel(x, src, dst, edge_attr_64, edge_attr_64_n2, edge_attr_64_n3, L0_gnn_W_msg, L0_gnn_W_q, L0_gnn_W_k,
           L0_gnn_W_out, L0_gnn_gamma, L0_gnn_beta, L3_gnn_W1, L3_gnn_Wr, L3_gnn_br):
    import numpy as np
    import concourse.bacc as bacc
    from concourse.bass_utils import run_bass_kernel_spmd

    def plain(a):
        return np.ascontiguousarray(np.asarray(a))

    half = TILES // 2
    ek = np.asarray(edge_attr_64).reshape(ROWS, GROUPS, 2, half, DIM).transpose(1, 2, 4, 3, 0).reshape(GROUPS, 2 * DIM, half * ROWS)
    eq = np.concatenate([np.asarray(edge_attr_64_n2), np.asarray(edge_attr_64_n3)], axis=1)
    eq = eq.reshape(ROWS, GROUPS, TILES, 2 * DIM).transpose(1, 3, 2, 0).reshape(GROUPS, 2 * DIM, TILES * ROWS)
    arrays = {
        "x": plain(x), "x_t": plain(np.asarray(x).T), "src": plain(src), "dst": plain(dst),
        "edge_k": plain(ek), "edge_q": plain(eq),
        "w_in": plain(np.concatenate([np.asarray(L0_gnn_W_msg), np.asarray(L0_gnn_W_k)], axis=1)),
        "w_q": plain(L0_gnn_W_q), "w_out": plain(L0_gnn_W_out),
        "gamma": plain(L0_gnn_gamma).reshape(1, DIM), "beta": plain(L0_gnn_beta).reshape(1, DIM),
        "w_last": plain(np.concatenate([np.asarray(L3_gnn_Wr).T, np.asarray(L3_gnn_W1).T], axis=0)),
        "b_last": plain(L3_gnn_br).reshape(1, DIM),
    }
    nc = bacc.Bacc("TRN2", target_bir_lowering=False, num_devices=1)
    args = [nc.dram_tensor(f"in_{k}", a.shape, mybir.dt.from_np(a.dtype), kind="ExternalInput").ap() for k, a in arrays.items()]
    out = nc.dram_tensor("out_nodes", [NODES, DIM], F32, kind="ExternalOutput").ap()
    gnn_kernel(nc, *args, out)
    r = run_bass_kernel_spmd(nc, [{f"in_{k}": a for k, a in arrays.items()}], core_ids=[0])
    return r.results[0]["out_nodes"]
```
